# Optimizing a Trainium2 kernel written in Bass

```python
import numpy as np
import jax
import jax.numpy as jnp

def _softmax(x, axis=-1):
    return jax.nn.softmax(x, axis=axis)

def _gelu(x):
    return jax.nn.gelu(x, approximate=True)

def _silu(x):
    return jax.nn.silu(x)

def _sigmoid(x):
    return jax.nn.sigmoid(x)

def _layernorm(x, axis=-1, eps=1e-05):
    m = jnp.mean(x, axis=axis, keepdims=True)
    v = jnp.var(x, axis=axis, keepdims=True)
    return (x - m) / jnp.sqrt(v + eps)

def _scatter_add(tgt, idx, src, axis=0):
    return tgt.at[idx].add(src)

def _segment_sum(src, seg, n):
    return jax.ops.segment_sum(src, seg, n)
kernel_name = 'mk_adaln_d1_jaxref_r4_e1c3d7'

def setup_inputs(seed: int=0):
    np.random.seed(seed)
    _w = jnp.asarray

    def _L0_attn_setup():
        import jax, jax.numpy as jnp
        import numpy as np
        N_HEADS = 16
        key = jax.random.key(seed)
        ks = jax.random.split(key, 9)
        B, S, D = (2, 512, 512)
        s = 0.02
        return {'X': jax.random.normal(ks[0], (B, S, D), jnp.float32), 'Wq': jax.random.normal(ks[1], (D, D), jnp.float32) * s, 'bq': jax.random.normal(ks[2], (D,), jnp.float32) * s, 'Wk': jax.random.normal(ks[3], (D, D), jnp.float32) * s, 'bk': jax.random.normal(ks[4], (D,), jnp.float32) * s, 'Wv': jax.random.normal(ks[5], (D, D), jnp.float32) * s, 'bv': jax.random.normal(ks[6], (D,), jnp.float32) * s, 'Wo': jax.random.normal(ks[7], (D, D), jnp.float32) * s, 'bo': jax.random.normal(ks[8], (D,), jnp.float32) * s}
    _L0_attn_in = _L0_attn_setup()

    def _L0_ffn_setup():
        import jax, jax.numpy as jnp
        import numpy as np
        E, K, H, F = (64, 6, 512, 192)
        G, KG = (8, 4)
        SHARED_F = 192
        SCALE = 2.5
        T = 2 * 256
        CAP = 2 * (T * K // E)

        def _grouped_topk(logits, bias):
            scores = jax.nn.sigmoid(logits.astype(jnp.float32))
            scores_b = scores + bias[None, :]
            gs = scores_b.reshape(-1, G, E // G)
            group_scores = jnp.sum(jax.lax.top_k(gs, 2)[0], axis=-1)
            gidx = jax.lax.top_k(group_scores, KG)[1]
            rows = jnp.arange(group_scores.shape[0])[:, None]
            group_mask = jnp.zeros_like(group_scores).at[rows, gidx].set(1.0)
            score_mask = jnp.repeat(group_mask, E // G, axis=-1) > 0
            tmp = jnp.where(score_mask, scores_b, -jnp.inf)
            topk_ids = jax.lax.top_k(tmp, K)[1]
            topk_w = jnp.take_along_axis(scores, topk_ids, axis=-1)
            topk_w = topk_w / jnp.sum(topk_w, axis=-1, keepdims=True)
            return (topk_w * SCALE, topk_ids)

        def _routed_moe(x, topk_w, topk_ids, w_gate, w_up, w_down):
            Tn = x.shape[0]
            flat_e = topk_ids.reshape(-1)
            order = jnp.argsort(flat_e)
            se = flat_e[order]
            pos = jnp.arange(Tn * K) - jnp.searchsorted(se, se, side='left')
            tok = order // K
            valid = pos < CAP
            slot = jnp.where(valid, pos, CAP)
            buf = jnp.zeros((E, CAP + 1, H), x.dtype).at[se, slot].set(x[tok])[:, :CAP]
            h = jax.nn.silu(jnp.einsum('ech,ehf->ecf', buf, w_gate)) * jnp.einsum('ech,ehf->ecf', buf, w_up)
            out = jnp.einsum('ecf,efh->ech', h, w_down)
            gathered = out[se, jnp.minimum(pos, CAP - 1)] * valid.astype(x.dtype)[:, None]
            w = topk_w.reshape(-1)[order].astype(x.dtype)[:, None]
            return jax.ops.segment_sum(gathered * w, tok, num_segments=Tn)
        key = jax.random.key(seed)
        ks = jax.random.split(key, 9)
        s = 0.02
        return dict(hidden_states=jax.random.normal(ks[0], (2, 256, H), jnp.float32), gate_w=jax.random.normal(ks[1], (H, E), jnp.float32) * s, bias=jax.random.normal(ks[2], (E,), jnp.float32) * s, w_gate=jax.random.normal(ks[3], (E, H, F), jnp.float32) * s, w_up=jax.random.normal(ks[4], (E, H, F), jnp.float32) * s, w_down=jax.random.normal(ks[5], (E, F, H), jnp.float32) * s, ws_gate=jax.random.normal(ks[6], (H, SHARED_F), jnp.float32) * s, ws_up=jax.random.normal(ks[7], (H, SHARED_F), jnp.float32) * s, ws_down=jax.random.normal(ks[8], (SHARED_F, H), jnp.float32) * s)
    _L0_ffn_in = _L0_ffn_setup()
    _L0_c = _w((lambda *s: np.random.randn(*s).astype(np.float32) * 0.05)(4, 512))
    _L0_wmod = _w((lambda *s: np.random.randn(*s).astype(np.float32) * 0.05)(512, 6 * 512) * 512 ** (-0.5))
    _d = {'L0_attn_X': _L0_attn_in['X'], 'L0_attn_Wq': _L0_attn_in['Wq'], 'L0_attn_bq': _L0_attn_in['bq'], 'L0_attn_Wk': _L0_attn_in['Wk'], 'L0_attn_bk': _L0_attn_in['bk'], 'L0_attn_Wv': _L0_attn_in['Wv'], 'L0_attn_bv': _L0_attn_in['bv'], 'L0_attn_Wo': _L0_attn_in['Wo'], 'L0_attn_bo': _L0_attn_in['bo'], 'L0_ffn_gate_w': _L0_ffn_in['gate_w'], 'L0_ffn_bias': _L0_ffn_in['bias'], 'L0_ffn_w_gate': _L0_ffn_in['w_gate'], 'L0_ffn_w_up': _L0_ffn_in['w_up'], 'L0_ffn_w_down': _L0_ffn_in['w_down'], 'L0_ffn_ws_gate': _L0_ffn_in['ws_gate'], 'L0_ffn_ws_up': _L0_ffn_in['ws_up'], 'L0_ffn_ws_down': _L0_ffn_in['ws_down'], 'L0_c': _L0_c, 'L0_wmod': _L0_wmod}
    _x0 = _d['L0_attn_X']
    _d['L0_attn_X'] = jax.random.normal(jax.random.fold_in(jax.random.key(seed), 1), (4, 1024, 512), dtype=_x0.dtype)
    del _x0
    return _d

def reference(L0_attn_X, L0_attn_Wq, L0_attn_bq, L0_attn_Wk, L0_attn_bk, L0_attn_Wv, L0_attn_bv, L0_attn_Wo, L0_attn_bo, L0_ffn_gate_w, L0_ffn_bias, L0_ffn_w_gate, L0_ffn_w_up, L0_ffn_w_down, L0_ffn_ws_gate, L0_ffn_ws_up, L0_ffn_ws_down, L0_c, L0_wmod):

    def _L0_attn_ref(X, Wq, bq, Wk, bk, Wv, bv, Wo, bo):
        import jax, jax.numpy as jnp
        import numpy as np
        N_HEADS = 16
        B, S, D = X.shape
        H = N_HEADS
        d_head = D // H
        scale = jnp.asarray(1.0 / np.sqrt(np.sqrt(d_head)), X.dtype)
        Q = (X @ Wq.T + bq).reshape(B, S, H, d_head) * scale
        K = (X @ Wk.T + bk).reshape(B, S, H, d_head) * scale
        V = (X @ Wv.T + bv).reshape(B, S, H, d_head)
        scores = jnp.einsum('bqhd,bkhd->bhqk', Q, K)
        causal = jnp.tril(jnp.ones((S, S), bool))
        scores = jnp.where(causal[None, None], scores, -jnp.inf)
        attn = jax.nn.softmax(scores.astype(jnp.float32), axis=-1).astype(X.dtype)
        out = jnp.einsum('bhqk,bkhd->bqhd', attn, V).reshape(B, S, D)
        return out @ Wo.T + bo

    def _L0_ffn_ref(hidden_states, gate_w, bias, w_gate, w_up, w_down, ws_gate, ws_up, ws_down):
        import jax, jax.numpy as jnp
        import numpy as np
        E, K, H, F = (64, 6, 512, 192)
        G, KG = (8, 4)
        SHARED_F = 192
        SCALE = 2.5
        T = 2 * 256
        CAP = 2 * (T * K // E)

        def _grouped_topk(logits, bias):
            scores = jax.nn.sigmoid(logits.astype(jnp.float32))
            scores_b = scores + bias[None, :]
            gs = scores_b.reshape(-1, G, E // G)
            group_scores = jnp.sum(jax.lax.top_k(gs, 2)[0], axis=-1)
            gidx = jax.lax.top_k(group_scores, KG)[1]
            rows = jnp.arange(group_scores.shape[0])[:, None]
            group_mask = jnp.zeros_like(group_scores).at[rows, gidx].set(1.0)
            score_mask = jnp.repeat(group_mask, E // G, axis=-1) > 0
            tmp = jnp.where(score_mask, scores_b, -jnp.inf)
            topk_ids = jax.lax.top_k(tmp, K)[1]
            topk_w = jnp.take_along_axis(scores, topk_ids, axis=-1)
            topk_w = topk_w / jnp.sum(topk_w, axis=-1, keepdims=True)
            return (topk_w * SCALE, topk_ids)

        def _routed_moe(x, topk_w, topk_ids, w_gate, w_up, w_down):
            Tn = x.shape[0]
            flat_e = topk_ids.reshape(-1)
            order = jnp.argsort(flat_e)
            se = flat_e[order]
            pos = jnp.arange(Tn * K) - jnp.searchsorted(se, se, side='left')
            tok = order // K
            valid = pos < CAP
            slot = jnp.where(valid, pos, CAP)
            buf = jnp.zeros((E, CAP + 1, H), x.dtype).at[se, slot].set(x[tok])[:, :CAP]
            h = jax.nn.silu(jnp.einsum('ech,ehf->ecf', buf, w_gate)) * jnp.einsum('ech,ehf->ecf', buf, w_up)
            out = jnp.einsum('ecf,efh->ech', h, w_down)
            gathered = out[se, jnp.minimum(pos, CAP - 1)] * valid.astype(x.dtype)[:, None]
            w = topk_w.reshape(-1)[order].astype(x.dtype)[:, None]
            return jax.ops.segment_sum(gathered * w, tok, num_segments=Tn)
        orig_shape = hidden_states.shape
        x = hidden_states.reshape(-1, H)
        router_logits = x @ gate_w
        topk_w, topk_ids = _grouped_topk(router_logits, bias)
        y = _routed_moe(x, topk_w, topk_ids, w_gate, w_up, w_down)
        shared = jax.nn.silu(x @ ws_gate) * (x @ ws_up) @ ws_down
        return (y + shared).reshape(orig_shape)
    x = L0_attn_X
    mod = (_silu(L0_c) @ L0_wmod).reshape(L0_c.shape[0], 6, 1, -1)
    sa, ca, ga, sb, cb, gb = (mod[:, 0], mod[:, 1], mod[:, 2], mod[:, 3], mod[:, 4], mod[:, 5])
    ga = (2 * (ga >= 0) - 1) * jnp.maximum(jnp.abs(ga), 0.25)
    gb = (2 * (gb >= 0) - 1) * jnp.maximum(jnp.abs(gb), 0.25)
    h = _layernorm(x, axis=-1) * (1 + ca) + sa
    x = x + ga * _L0_attn_ref(h, L0_attn_Wq, L0_attn_bq, L0_attn_Wk, L0_attn_bk, L0_attn_Wv, L0_attn_bv, L0_attn_Wo, L0_attn_bo)
    h = _layernorm(x, axis=-1) * (1 + cb) + sb
    x = x + gb * _L0_ffn_ref(h, L0_ffn_gate_w, L0_ffn_bias, L0_ffn_w_gate, L0_ffn_w_up, L0_ffn_w_down, L0_ffn_ws_gate, L0_ffn_ws_up, L0_ffn_ws_down)
    return x

_drawn_inputs = setup_inputs


def setup_inputs(seed=0):
    import zlib

    import numpy as np

    out = dict(_drawn_inputs(seed))
    spreads = {}
    factors = {'L0_attn_Wq': 8.0,
     'L0_attn_bq': 8.0,
     'L0_attn_Wk': 8.0,
     'L0_attn_bk': 8.0,
     'L0_attn_Wv': 8.0,
     'L0_attn_bv': 8.0,
     'L0_attn_Wo': 8.0,
     'L0_attn_bo': 8.0,
     'L0_ffn_gate_w': 8.0,
     'L0_ffn_bias': 8.0,
     'L0_ffn_w_gate': 8.0,
     'L0_ffn_w_up': 8.0,
     'L0_ffn_w_down': 8.0,
     'L0_ffn_ws_gate': 7.702,
     'L0_ffn_ws_up': 7.513,
     'L0_ffn_ws_down': 7.529,
     'L0_c': 5.185,
     'L0_wmod': 5.118}
    for name, (base, spread) in spreads.items():
        noise = np.random.default_rng([zlib.crc32(name.encode()), seed]).standard_normal(out[name].shape)
        drawn = base * np.exp(spread * noise) if base else spread * noise
        out[name] = jnp.asarray(drawn.astype(out[name].dtype))
    for name, factor in factors.items():
        out[name] = (out[name] * factor).astype(out[name].dtype)
    return out
```

```python
from contextlib import ExitStack

import concourse.bass as bass
from concourse import mybir

ALU = mybir.AluOpType
ACT = mybir.ActivationFunctionType
AX_X = mybir.AxisListType.X
F32 = mybir.dt.float32
F32R = mybir.dt.float32r
BF16 = mybir.dt.bfloat16
U32 = mybir.dt.uint32

P = 128
B, S, D = 4, 1024, 512
T = B * S
HEADS, DH = 16, 32
KT = D // P
NT = S // P
CH = 512
NC = S // CH
GH = P // DH
NG = HEADS // GH
E, TOPK, F = 64, 6, 192
FH = F // 2
GROUPS, GSIZE, KGROUPS = 8, 8, 4
CAP = 2 * (2 * 256 * TOPK // E)
ROUNDS = CAP // 8
EPS = 1e-5
QSCALE = float(DH) ** -0.25
ROUTE_SCALE = 2.5
BIG = 1e30
KiB = 1024
STK = 3 * DH + 1


def chunk_steps():
    return [(c, kt, max(0, kt * P - c * CH)) for c in range(NC) for kt in range((c + 1) * CH // P)]


def max_units():
    return [(i, kc, j, min(CH, (i + 1) * P - kc * CH))
            for i in reversed(range(NT)) for kc in range(i * P // CH + 1) for j in range(GH)]


STEPS = chunk_steps()
UNITS = max_units()
NS, NU = len(STEPS), len(UNITS)
DPG = NU + 1


def share_units():
    total = sum(u[3] for u in UNITS)
    work = sum(CH - q0 for _, _, q0 in STEPS)
    out, done, at, seen = [], 0, 0, 0
    for _, _, q0 in STEPS:
        seen += CH - q0
        n = 0
        while at < NU and done < total * min(1.0, 1.2 * seen / work):
            done += UNITS[at][3]
            at += 1
            n += 1
        out.append(n)
    out[-1] += NU - at
    return out


SHARE = share_units()

BATCH_SIGNALS = """xn xt hh hl vp vr qk hi lo dq df negm st ex pv od rch an ah at of x2 op xg var rs h2 tr wk h2h h2l lg th gu tg hs dn pre
    val vt lst vch x0 x1 mod wv wqk qkw0 qkw1 stk0 stk1 stk2 m wo wsd xi0 xi1 hw0 hw1 ww pw0 pw1 gabo""".split()


def build(nc, x, wqkvo, bq, bk, bv, bo, gate_w, bias, w_gu, w_dn, ws_gu, ws_dn, c_t, wmod, out):
    scr_w = nc.dram_tensor("scr_w", [4, 2, P, KT * D], F32, kind="Internal").ap()
    scr_gu = nc.dram_tensor("scr_gu", [2, P, KT * 2 * F], F32, kind="Internal").ap()
    scr_dn = nc.dram_tensor("scr_dn", [2, FH, 2 * D], F32, kind="Internal").ap()
    scr_qk = nc.dram_tensor("scr_qk", [2, 2, D, S], F32, kind="Internal").ap()
    scr_row = nc.dram_tensor("scr_row", [2, GH * S], F32, kind="Internal").ap()
    scr_mod = nc.dram_tensor("scr_mod", [B, 6, D], F32, kind="Internal").ap()
    HW = D + E
    htab = nc.dram_tensor("htab", [T + CAP, HW], F32, kind="Internal").ap()

    ctx = ExitStack()
    with ctx:
        arena = ctx.enter_context(nc.sbuf_tensor("arena", [P, 207 * KiB // 4], F32))
        del arena
        base = nc.sbuf_base - 207 * KiB

        def at(name, off, shape, dt=F32):
            return nc.alloc_sbuf_tensor_at(name, shape, dt, offset=base + off)

        def pair(name):
            return ctx.enter_context(nc.psum_tensor(name, [P, 2, 512], F32))

        sems = {}

        def sem(name):
            sems[name] = ctx.enter_context(nc.semaphore("s_" + name))
            return sems[name]

        pA, pB, pC, pD = (pair(n) for n in ("pA", "pB", "pC", "pD"))
        AB = [pA, pB]

        h_hi = at("h_hi", 0, [P, KT, S], F32R)
        h_lo = at("h_lo", 16 * KiB, [P, KT, S], F32R)
        v_rows = at("v_rows", 32 * KiB, [P, NT, D])
        x2_rows = at("x2_rows", 32 * KiB, [P, NT, D])
        STK0 = 48 * KiB
        q_stk = [at(f"q_stk{n}", STK0 + 32 * KiB * n, [P, GH, S], F32R) for n in range(3)]
        k_stk = [at(f"k_stk{n}", STK0 + 32 * KiB * n + 16 * KiB, [P, GH, S], F32R) for n in range(3)]
        wv = [at(f"wv{n}", STK0 + 8 * KiB * n, [P, KT, D], F32R) for n in range(2)]
        wq = [at(f"wq{n}", STK0 + 64 * KiB + 8 * KiB * n, [P, KT, D], F32R) for n in range(2)]
        wk_ = [at(f"wk{n}", STK0 + 80 * KiB + 8 * KiB * n, [P, KT, D], F32R) for n in range(2)]
        wo = [at(f"wo{n}", STK0 + 32 * KiB + 8 * KiB * n, [P, KT, D], F32R) for n in range(2)]
        wsg = [at(f"wsg{n}", STK0 + 48 * KiB + 6 * KiB * n, [P, KT, 2 * F], F32R) for n in range(2)]
        wsd = [at(f"wsd{n}", STK0 + 64 * KiB + 4 * KiB * n, [FH, 2, D], F32R) for n in range(2)]
        hs = [at(f"hs{n}", STK0 + 72 * KiB + 8 * KiB * n, [FH, 2, S], F32R) for n in range(2)]
        p_buf = at("p_buf", 144 * KiB, [P, 2, GH, CH])
        x_rows = at("x_rows", 144 * KiB, [P, NT, D])
        mask = at("mask", 160 * KiB, [P, S])
        x_in = at("x_in", 164 * KiB, [P, 2, D])
        wk = at("wk", 168 * KiB, [P, 2, 512])
        hi_s = at("hi_s", 172 * KiB, [P, 2, 512], F32R)
        lo_s = at("lo_s", 176 * KiB, [P, 2, 512], F32R)
        pre_s = at("pre_s", 172 * KiB, [P, 2, 512])
        od = at("od", 180 * KiB, [P, 2, CH])
        tmp = at("tmp", 184 * KiB, [P, 2, 512])
        h2b = at("h2b", 176 * KiB, [P, 2, 512])
        ga = at("ga", 188 * KiB, [P, D])
        gabo = at("gabo", 190 * KiB, [P, D])
        cb1 = at("cb1", 192 * KiB, [P, D])
        sbm = at("sbm", 194 * KiB, [P, D])
        gb = at("gb", 196 * KiB, [P, D])
        bv_b = at("bv_b", 198 * KiB, [P, D])
        gw = at("gw", 200 * KiB, [P, KT, E])
        ident_b = at("ident_b", 201 * KiB, [P, P], BF16)
        mask_t = at("mask_t", 201 * KiB + 256, [P, P], BF16)
        lists = at("lists", 202 * KiB, [P, B * CAP])
        ident = at("ident", 203 * KiB + 512, [P, P])
        m0 = 204 * KiB
        ones = at("ones", m0, [P, DH])
        mx = at("mx", m0 + 128, [P, GH, NT, 2])
        negm = at("negm", m0 + 384, [P, GH * NT])
        mrow = at("mrow", m0 + 512, [GH * NT, P], F32R)
        stat = at("stat", m0 + 1024, [P, NT, 6])
        mv = at("mv", m0 + 1216, [P, NT, 2])
        var = at("var", m0 + 1280, [P, NT])
        rstd = at("rstd", m0 + 1312, [P, NT])
        nhalf = at("nhalf", m0 + 1344, [P, NT])
        tokn = at("tokn", m0 + 1376, [P, NT])
        sa_c = at("sa_c", m0 + 1408, [P, KT])
        ca_c = at("ca_c", m0 + 1424 + 16, [P, KT])
        bq_c = at("bq_c", m0 + 1472, [P, KT])
        bk_c = at("bk_c", m0 + 1504, [P, KT])
        bqs = at("bqs", m0 + 1536, [P, KT])
        bks = at("bks", m0 + 1568, [P, KT])
        bias_b = at("bias_b", m0 + 1600, [P, E])
        tri = at("tri", m0 + 1856, [P, GROUPS * GROUPS])
        slots_f = at("slots_f", m0 + 2112, [P, CAP])
        v8 = at("v8", m0 + 2496, [P, NT, 8])
        wsum = at("wsum", m0 + 2752, [P, NT])
        rws = at("rws", m0 + 2784, [P, NT])
        rcol = at("rcol", m0 + 2816, [P, CH // 32])

        def rt(name, off, shape, dt=F32):
            return at(name, STK0 + off, shape, dt)
        th = rt("th", 0, [P, NT, E])
        sc = rt("sc", 2048, [P, NT, E])
        sb_ = rt("sb_", 4096, [P, NT, E])
        cmp = rt("cmp", 6144, [P, NT, GROUPS, GROUPS])
        ceq = rt("ceq", 8192, [P, NT, GROUPS, GROUPS])
        rep = rt("rep", 10240, [P, NT, E])
        sel = rt("sel", 12288, [P, NT, E])
        wdn = rt("wdn", 14336, [P, NT, E])
        valt = rt("valt", 16384, [P, 4, 2, E])
        ta = rt("ta", 18432, [P, E, 4])
        tb = rt("tb", 19456, [P, E, 4])
        tc_ = rt("tc_", 20480, [P, E, 2])
        td = rt("td", 20992, [P, E, 2])
        te = rt("te", 21504, [P, E, 2])
        tf = rt("tf", 22016, [P, E, 2])
        gsum = rt("gsum", 22528, [P, NT, GROUPS])
        gcnt = rt("gcnt", 22784, [P, NT, GROUPS])
        gsel = rt("gsel", 23040, [P, NT, GROUPS])
        gpen = rt("gpen", 23296, [P, NT, GROUPS])
        keys = rt("keys", 23552, [P, 512])
        keys2 = rt("keys2", 25600, [P, 512])
        lb = rt("lb", 27648, [P, CAP])

        wstage = [at(f"wstage{n}", STK0 + 48 * KiB + 8 * KiB * n, [P, KT * D]) for n in range(2)]
        wsh = [at(f"wsh{n}", STK0 + 64 * KiB + 8 * KiB * n, [P, KT * D], F32R) for n in range(2)]
        wsl = [at(f"wsl{n}", STK0 + 80 * KiB + 8 * KiB * n, [P, KT * D], F32R) for n in range(2)]
        wm = at("wm", STK0, [P, KT, 6 * D])
        modr = at("modr", 144 * KiB, [B, 6, D])
        modn = at("modn", 156 * KiB, [B, D])
        ct = at("ct", 32 * KiB, [P, KT, B])
        ctt = at("ctt", 32 * KiB + 64, [P, KT, B])
        cts = at("cts", 32 * KiB + 128, [P, KT, B])
        zrow = at("zrow", 33 * KiB, [CAP, HW])
        onev = at("onev", 0, [1, 2 * GH * S])

        NW = 4
        weg = [at(f"weg{n}", 6 * KiB * n, [P, KT, 2 * F]) for n in range(NW)]
        wed = [at(f"wed{n}", 24 * KiB + 4 * KiB * n, [FH + 1, 2, D]) for n in range(NW)]
        gath = [at(f"gath{n}", 48 * KiB + 2304 * n, [CAP, HW]) for n in range(NW)]
        gt = [at(f"gt{n}", 58 * KiB + 1536 * n, [P, KT, CAP]) for n in range(2)]
        the = [at(f"the{n}", 62 * KiB + 768 * n, [CAP, F]) for n in range(2)]
        hae = [at(f"hae{n}", 64 * KiB + 768 * n, [CAP, F]) for n in range(2)]
        hhe = [at(f"hhe{n}", 66 * KiB + 768 * n, [CAP, F]) for n in range(2)]
        hte = [at(f"hte{n}", 68 * KiB + 768 * n, [FH + 1, 2, CAP]) for n in range(2)]
        gbs = [at(f"gbs{n}", 70 * KiB + 2048 * n, [CAP, D]) for n in range(2)]
        ye = [at(f"ye{n}", 74 * KiB + 2048 * n, [CAP, D]) for n in range(2)]
        idg = [at(f"idg{n}", 78 * KiB + 32 * n, [CAP, 1], U32) for n in range(NW)]
        ids = [at(f"ids{n}", 78 * KiB + 32 * NW + 32 * n, [CAP, 1], U32) for n in range(NW)]
        ohc = [at(f"ohc{n}", 79 * KiB + 256 * n, [3 * B, CAP], BF16) for n in range(2)]
        idu = at("idu", 80 * KiB, [CAP, E], U32)
        oh = at("oh", 81 * KiB, [3 * B, E * CAP], BF16)
        gb12 = at("gb12", 94 * KiB, [3 * B, D], BF16)
        mall = at("mall", 96 * KiB, [E, 2 * B * CAP])
        mal2 = at("mal2", 99 * KiB, [E, 2 * B * CAP])
        fin = at("fin", 102 * KiB, [E, CAP])
        fz = at("fz", 103 * KiB, [E, CAP])
        idf = at("idf", 104 * KiB, [E, CAP])
        oge = at("oge", 105 * KiB, [E, CAP])
        ohb = [at(f"ohb{n}", 106 * KiB + 256 * n, [E, CAP], BF16) for n in range(B)]
        gbr = at("gbr", 108 * KiB, [B, D])
        gbp = [at(f"gbp{n}", 110 * KiB + 1024 * n, [B, D], BF16) for n in range(3)]
        gbq = [at(f"gbq{n}", 114 * KiB + 2048 * n, [B, D]) for n in range(2)]

        for n in BATCH_SIGNALS:
            sem(n)
        batch_sems = [sems[n] for n in BATCH_SIGNALS]
        for n in ("cst", "cst_v", "ld", "wst0", "wst1", "wsp_h", "wsp_l", "wwr0", "wwr1", "modm", "modc", "modv", "mw",
                  "csil", "zr",
                  "mrg", "mch", "idt", "idx", "ohd", "g12", "pre_idx",
                  "we0", "we1", "we2", "we3", "ga0", "ga1", "ga2", "ga3", "ic", "is", "xte", "gte", "gue", "the", "hhe",
                  "hte", "htc", "dne", "gbm", "gbs", "ye", "sc", "oc", "ech", "fgb", "ez", "pas", "end", "go_sp", "go_act", "go_dve", "go_pe"):
            sem(n)
        s = sems
        s_x, s_qkw, s_stk = [s["x0"], s["x1"]], [s["qkw0"], s["qkw1"]], [s["stk0"], s["stk1"], s["stk2"]]
        s_xi, s_hw, s_pw = [s["xi0"], s["xi1"]], [s["hw0"], s["hw1"]], [s["pw0"], s["pw1"]]
        s_we, s_ga = [s[f"we{n}"] for n in range(4)], [s[f"ga{n}"] for n in range(4)]
        s_wst, s_wwr = [s["wst0"], s["wst1"]], [s["wwr0"], s["wwr1"]]

        VCH_PER = 183

        def need(eng, name, it, n, per=None):
            eng.wait_ge(s[name], n)

        def batches(eng, body):
            with eng.Fori(0, B) as it:
                body(it)

        def end_of_batch(eng, name):
            eng.drain().then_inc(s["end"], 1)
            eng.wait_ge(s["go_" + name], 1)
            eng.sem_clear(s["go_" + name])

        splits = [(wqkvo[k], KT * D, P, scr_w[k]) for k in range(4)]
        splits += [(ws_gu, KT * 2 * F, P, scr_gu), (ws_dn, 2 * D, FH, scr_dn)]

        def store_split(sp, k):
            src, n, rows, dst = splits[k]
            sp.wait_ge(s["wsp_l"], k + 1)
            for part, t in ((0, wsh), (1, wsl)):
                sp.dma_start(dst[part], t[k % 2][0:rows, 0:n].bitcast(F32)).then_inc(s_wwr[k % 2], 16)

        def load_expert(sp, e, r, reused):
            src_g = w_gu[bass.ds(e, 1)].rearrange("o p k f -> (o p) k f")
            src_d = w_dn[bass.ds(e, 1)].rearrange("o p k f -> (o p) k f")
            if reused:
                sp.wait_ge(s["dne"], e - (NW - 1))
            sp.dma_start(weg[r][:, :, :], src_g).then_inc(s_we[r], 16)
            sp.dma_start(wed[r][0:FH, :, :], src_d).then_inc(s_we[r], 16)

        def evac_chunk(act, it, g, c):
            need(act, "pv", it, g * NS + (4 if c == 0 else NS))
            n = g * NC + c
            if n >= 1:
                need(act, "at", it, n)
            act.activation(od[:, :, :], pC[:, :, :], ACT.Copy).then_inc(s["od"], 1)

        block = ctx.enter_context(nc.Block())

        @block.sync
        def _(sp):
            sp.dma_start(ct[:, :, :], c_t).then_inc(s["ld"], 16)
            sp.dma_start(wm[:, :, :], wmod).then_inc(s["ld"], 16)
            for k, (src, n, rows, dst) in enumerate(splits):
                if k >= 2:
                    sp.wait_ge(s["wsp_l"], k - 1)
                sp.dma_start(wstage[k % 2][0:rows, 0:n], src).then_inc(s_wst[k % 2], 16)
                if k >= 1:
                    store_split(sp, k - 1)
            store_split(sp, len(splits) - 1)
            sp.dma_start(bq_c[:, :], bq).then_inc(s["cst"], 16)
            sp.dma_start(bk_c[:, :], bk).then_inc(s["cst"], 16)
            sp.dma_start(bv_b[:, :], bv.partition_broadcast(P)).then_inc(s["cst"], 16)
            sp.dma_start(bias_b[:, :], bias.partition_broadcast(P)).then_inc(s["cst"], 16)
            sp.dma_start(gw[:, :, :], gate_w).then_inc(s["cst"], 16)
            sp.wait_ge(s["zr"], 3)
            sp.dma_start(htab[T:T + CAP, :], zrow[:, :]).then_inc(s["pre_idx"], 16)
            sp.dma_start(out[T:T + CAP, :], zrow[:, 0:D]).then_inc(s["pre_idx"], 16)
            for r in range(2):
                sp.dma_start(scr_row[r:r + 1, :], onev[:, r * GH * S:(r + 1) * GH * S]).then_inc(s["pre_idx"], 16)
            sp.wait_ge(s["modv"], 1)
            sp.dma_start(scr_mod, modr[:, :, :]).then_inc(s["mw"], 16)
            sp.wait_ge(s["mw"], 16)
            sp.wait_ge(s["pre_idx"], 64)
            for n in range(2):
                sp.wait_ge(s_wwr[n], 32 * 3)

            def body(it):
                xb = x.rearrange("(b t p) d -> b p t d", b=B, p=P)[bass.ds(it, 1)].rearrange("o p t d -> (o p) t d")
                xt = x.rearrange("(b t p) d -> b t p d", b=B, p=P)[bass.ds(it, 1)].rearrange("o t p d -> (o t) p d")
                ht = htab[0:T, :].rearrange("(b t p) d -> b t p d", b=B, p=P)[bass.ds(it, 1)].rearrange(
                    "o t p d -> (o t) p d")
                ot = out[0:T, :].rearrange("(b t p) d -> b t p d", b=B, p=P)[bass.ds(it, 1)].rearrange(
                    "o t p d -> (o t) p d")
                mod = scr_mod[bass.ds(it, 1)].rearrange("o m d -> (o m) d")
                for h in range(2):
                    sp.dma_start(x_rows[:, 4 * h:4 * h + 4, :], xb[:, 4 * h:4 * h + 4, :]).then_inc(s_x[h], 16)
                for n, dst in ((0, sa_c), (1, ca_c)):
                    sp.dma_start(dst[:, :], mod[n].rearrange("(k p) -> p k", p=P), allow_slow_non_contiguous=True).then_inc(s["mod"], 16)
                for n, dst in ((2, ga), (4, cb1), (3, sbm), (5, gb)):
                    sp.dma_start(dst[:, :], mod[n].partition_broadcast(P)).then_inc(s["mod"], 16)
                sp.dma_start(gabo[:, :], bo.partition_broadcast(P)).then_inc(s["mod"], 16)
                for n in range(2):
                    sp.dma_start(wv[n][:, :, :].bitcast(F32), scr_w[2, n].rearrange("p (k d) -> p k d", k=KT)).then_inc(s["wv"], 16)
                for k, dst in ((0, wq), (1, wk_)):
                    for n in range(2):
                        sp.dma_start(dst[n][:, :, :].bitcast(F32), scr_w[k, n].rearrange("p (k d) -> p k d", k=KT)).then_inc(s["wqk"], 16)

                def load_stack(g):
                    for u in range(2):
                        sp.wait_ge(s_qkw[u], 32 * (2 * g + 2))
                    for dst, t, parts in ((q_stk[g % 3], 0, (0, 1, 0)), (k_stk[g % 3], 1, (0, 0, 1))):
                        for r, part in enumerate(parts):
                            src = scr_qk[t, part, g * P:(g + 1) * P, :].rearrange("(j d) s -> d j s", d=DH)
                            sp.dma_start(dst[r * DH:(r + 1) * DH, :, :].bitcast(F32), src).then_inc(s_stk[g % 3], 16)
                    for r, dst in enumerate((q_stk[g % 3], k_stk[g % 3])):
                        sp.dma_start(dst[3 * DH:STK, :, :].rearrange("p j s -> p (j s)").bitcast(F32), scr_row[r:r + 1, :]).then_inc(
                            s_stk[g % 3], 16)

                for u in range(16):
                    m, t, c = u // 4, u // 2 % 2, u % 2
                    need(sp, "lo", it, u + 1)
                    for part, src in ((0, hi_s), (1, lo_s)):
                        sp.dma_start(scr_qk[t, part, m * P:(m + 1) * P, c * CH:(c + 1) * CH],
                                     src[:, u % 2, :].bitcast(F32)).then_inc(s_qkw[u % 2], 16)
                    if u == 5:
                        need(sp, "vp", it, NT)
                        load_stack(0)
                    if u == 9:
                        load_stack(1)

                def shift_row(g):
                    need(sp, "df", it, DPG * (g + 1))
                    sp.dma_start(q_stk[g % 3][3 * DH:STK, :, :].rearrange("p j s -> p (j s)").bitcast(F32),
                                 mrow[:, :].bitcast(F32)).then_inc(s["m"], 16)

                shift_row(0)
                need(sp, "qk", it, 16)
                load_stack(2)
                shift_row(1)
                need(sp, "st", it, 2 * NS)
                load_stack(3)
                shift_row(2)
                need(sp, "st", it, 2 * NS * 2)
                for n in range(2):
                    sp.dma_start(wo[n][:, :, :].bitcast(F32), scr_w[3, n].rearrange("p (k d) -> p k d", k=KT)).then_inc(s["wo"], 16)
                    sp.dma_start(wsg[n][:, :, :].bitcast(F32), scr_gu[n].rearrange("p (k d) -> p k d", k=KT)).then_inc(s["wo"], 16)
                shift_row(3)
                need(sp, "st", it, 2 * NS * 3)
                for n in range(2):
                    sp.dma_start(wsd[n][:, :, :].bitcast(F32), scr_dn[n].rearrange("p (k d) -> p k d", k=2)).then_inc(s["wsd"], 16)

                def load_x(i):
                    if i >= 2:
                        need(sp, "xg", it, i - 1)
                    sp.dma_start(x_in[:, i % 2, :], xt[i]).then_inc(s_xi[i % 2], 16)

                load_x(0)
                load_x(1)
                for i in range(NT):
                    if i + 2 < NT:
                        load_x(i + 2)
                    need(sp, "h2", it, i + 1)
                    sp.dma_start(ht[i][:, 0:D], h2b[:, i % 2, :]).then_inc(s_hw[i % 2], 16)
                for i in range(NT):
                    need(sp, "pre", it, i + 1)
                    sp.dma_start(ot[i], pre_s[:, i % 2, :]).then_inc(s_pw[i % 2], 16)
                need(sp, "val", it, 1)
                sp.dma_start(ht.rearrange("t p d -> p t d")[:, :, D:HW], wdn[:, :, :]).then_inc(s["ww"], 16)
                for n in range(2):
                    sp.wait_ge(s_hw[n], 64)
                    sp.wait_ge(s_pw[n], 64)
                sp.wait_ge(s["ww"], 16)
                end_of_batch(sp, "sp")

            batches(sp, body)

            sp.dma_start(mall[:, 0:B * CAP], lists[0:E, :]).then_inc(s["mrg"], 16)
            sp.dma_start(mall[:, B * CAP:2 * B * CAP], lists[E:2 * E, :]).then_inc(s["mrg"], 16)
            sp.dma_start(gbr[:, :], scr_mod[:, 5, :]).then_inc(s["fgb"], 16)
            load_expert_peeled = 3
            for e in range(load_expert_peeled):
                load_expert(sp, e, e, False)
            sp.wait_ge(s["idx"], 1)
            for n in range(3):
                sp.dma_start(gb12[B * n:B * n + B, :], gbp[n][:, :]).then_inc(s["g12"], 16)
                for b in range(B):
                    sp.dma_start(oh[B * n + b:B * n + b + 1, :], ohb[b][:, :]).then_inc(s["g12"], 16)
            load_expert(sp, 3, 3, False)
            with sp.Fori(0, (E - NW) // NW) as k:
                for r in range(NW):
                    load_expert(sp, k * NW + (NW + r), r, True)

        @block.gpsimd
        def _(pool):
            pool.memset(ident[:, :], 0.0).then_inc(s["cst_v"], 1)
            pool.memset(mask[:, :], 0.0).then_inc(s["cst_v"], 1)
            pool.memset(tri[:, :], 1.0).then_inc(s["cst_v"], 1)
            pool.memset(ones[:, :], 1.0).then_inc(s["cst_v"], 1)
            pool.memset(nhalf[:, :], -0.5).then_inc(s["cst_v"], 1)
            pool.memset(ident_b[:, :], 0.0).then_inc(s["cst_v"], 1)
            pool.memset(mask_t[:, :], 0.0).then_inc(s["cst_v"], 1)
            pool.memset(zrow[:, :], 0.0).then_inc(s["zr"], 1)
            pool.memset(onev[:, 0:GH * S], 0.0).then_inc(s["zr"], 1)
            pool.memset(onev[:, GH * S:2 * GH * S], 1.0).then_inc(s["zr"], 1)
            pool.wait_ge(s["cst_v"], 7)
            pool.affine_select(out=ident[:, :], in_=ident[:, :], compare_op=ALU.not_equal, fill=1.0, base=0,
                               pattern=[[-1, P]], channel_multiplier=1).then_inc(s["cst_v"], 1)
            pool.affine_select(out=ident_b[:, :], in_=ident_b[:, :], compare_op=ALU.not_equal, fill=1.0, base=0,
                               pattern=[[-1, P]], channel_multiplier=1).then_inc(s["cst_v"], 1)
            pool.affine_select(out=mask_t[:, :], in_=mask_t[:, :], compare_op=ALU.is_ge, fill=-BIG, base=0,
                               pattern=[[1, P]], channel_multiplier=-1).then_inc(s["cst_v"], 1)
            pool.affine_select(out=mask[:, :], in_=mask[:, :], compare_op=ALU.is_ge, fill=-BIG, base=S - P,
                               pattern=[[-1, S]], channel_multiplier=1).then_inc(s["cst_v"], 1)
            pool.affine_select(out=tri[:, :].rearrange("p (g h) -> p g h", g=GROUPS),
                               in_=tri[:, :].rearrange("p (g h) -> p g h", g=GROUPS), compare_op=ALU.is_ge, fill=0.0,
                               base=-1, pattern=[[1, GROUPS], [-1, GROUPS]], channel_multiplier=0).then_inc(s["cst_v"], 1)
            pool.iota(tokn[:, :], pattern=[[-P, NT]], base=T, channel_multiplier=-1,
                      allow_small_or_imprecise_dtypes=True).then_inc(s["cst_v"], 1)
            pool.iota(slots_f[:, :], pattern=[[1, CAP]], base=0, channel_multiplier=0,
                      allow_small_or_imprecise_dtypes=True).then_inc(s["cst_v"], 1)

            def body(it):
                need(pool, "var", it, NT)
                pool.tensor_tensor(rstd[:, :], var[:, :], nhalf[:, :], ALU.pow).then_inc(s["rs"], 1)
                for n in range(NG * NC):
                    g, c = n // NC, n % NC
                    pool.wait_ge(s["rch"], 4 * n + 4)
                    pool.tensor_tensor(od[:, 0, :], od[:, 0, :], tmp[:, 1, :], ALU.mult).then_inc(s["an"], 1)
                    need(pool, "ah", it, n + 1)
                    pool.tensor_tensor(h_lo[:, g, c * CH:(c + 1) * CH], od[:, 0, :],
                                       h_hi[:, g, c * CH:(c + 1) * CH].bitcast(F32), ALU.subtract).then_inc(s["at"], 1)
                need(pool, "mod", it, 16 * 7)
                pool.tensor_tensor(gabo[:, :], gabo[:, :], ga[:, :], ALU.mult).then_inc(s["gabo"], 1)
                pool.wait_ge(s["gabo"], 1)
                need(pool, "at", it, NG * NC)
                def tile_low(i):
                    need(pool, "h2h", it, i + 1)
                    pool.tensor_tensor(h_lo[:, :, i * P:i * P + P], wk[:, i % 2, :].rearrange("p (k q) -> p k q", k=KT),
                                       h_hi[:, :, i * P:i * P + P].bitcast(F32), ALU.subtract).then_inc(s["h2l"], 1)

                for i in range(NT):
                    pool.wait_ge(s_xi[i % 2], 16 * (i // 2) + 16)
                    if i >= 2:
                        need(pool, "x2", it, i - 1)
                    pool.tensor_tensor(od[:, i % 2, :], x_in[:, i % 2, :], gabo[:, :], ALU.add).then_inc(s["xg"], 1)
                    need(pool, "var", it, NT + i + 1)
                    pool.tensor_tensor(rstd[:, i:i + 1], var[:, i:i + 1], nhalf[:, i:i + 1], ALU.pow).then_inc(s["rs"], 1)
                    if i >= 2:
                        tile_low(i - 2)
                tile_low(NT - 2)
                tile_low(NT - 1)
                pool.drain()
                pool.wait_ge(s["end"], 4)
                for x in batch_sems:
                    pool.sem_clear(x)
                pool.sem_clear(s["end"])
                for n in ("sp", "act", "dve", "pe"):
                    pool.sem_inc(s["go_" + n], 1)

            batches(pool, body)

            def gather(e, r, reused):
                if reused:
                    pool.wait_ge(s["ye"], e - (NW - 1))
                pool.tensor_copy(idg[r][:, :], idu[:, bass.ds(e, 1)]).then_inc(s["ic"], 1)
                pool.wait_ge(s["ic"], e + 1)
                pool.sem_inc(s["pas"], 1)
                pool.indirect_dma_start(gath[r][:, :], None, htab, bass.IndirectOffsetOnAxis(ap=idg[r][:, :], axis=0)).then_inc(
                    s_ga[r], 16)

            def scatter(e, r, first):
                pool.tensor_copy(ids[r][:, :], idu[:, bass.ds(e, 1)]).then_inc(s["is"], 1)
                pool.wait_ge(s["is"], e + 1)
                pool.wait_ge(s["ye"], e + 1)
                if not first:
                    pool.wait_ge(s["sc"], e * 16)
                pool.sem_inc(s["pas"], 1)
                pool.indirect_dma_start(out, bass.IndirectOffsetOnAxis(ap=ids[r][:, :], axis=0), ye[r % 2][:, :], None,
                                        compute_op=ALU.add).then_inc(s["sc"], 16)

            for z in wed + hte:
                pool.memset(z[FH:FH + 1, :, :], 0.0).then_inc(s["ez"], 1)
            pool.wait_ge(s["idt"], 2)
            for e in range(NW):
                gather(e, e, False)
            scatter(0, 0, True)
            with pool.Fori(0, (E - NW) // NW) as k:
                for r in range(NW):
                    gather(k * NW + (r + 4), r, True)
                    scatter(k * NW + (r + 1), (r + 1) % NW, False)
            for e in range(E - NW + 1, E):
                scatter(e, e % NW, False)
            pool.wait_ge(s["sc"], 16 * E)

        @block.scalar
        def _(act):
            act.wait_ge(s["ld"], 32)
            act.activation(ctt[:, :, :], ct[:, :, :], ACT.Tanh, scale=0.5).then_inc(s["csil"], 1)
            for k, (src, n, rows, dst) in enumerate(splits):
                act.wait_ge(s_wst[k % 2], 16 * (k // 2) + 16)
                if k >= 2:
                    act.wait_ge(s_wwr[k % 2], 32 * (k // 2))
                act.activation(wsh[k % 2][0:rows, 0:n], wstage[k % 2][0:rows, 0:n], ACT.Copy).then_inc(s["wsp_h"], 1)
            for n in range(6):
                act.wait_ge(s["modm"], n + 1)
                act.activation(modr[:, n, :], AB[n // 2 % 2][0:B, n % 2, :], ACT.Copy).then_inc(s["modc"], 1)
            act.wait_ge(s["cst"], 80)
            act.mul(bqs[:, :], bq_c[:, :], QSCALE).then_inc(s["csil"], 1)
            act.mul(bks[:, :], bk_c[:, :], QSCALE).then_inc(s["csil"], 1)
            act.wait_ge(s["csil"], 4)

            def body(it):
                need(act, "mod", it, 16 * 7)
                for n in range(2 * KT):
                    h, k = n // KT, n % KT
                    need(act, "xt", it, n + 1)
                    if n >= 2:
                        need(act, "hl", it, n - 1)
                    src = AB[k // 2][:, k % 2, :]
                    act.activation(wk[:, n % 2, :], src, ACT.Identity, bias=sa_c[:, k:k + 1], scale=ca_c[:, k:k + 1])
                    act.activation(h_hi[:, k, h * 512:h * 512 + 512], src, ACT.Identity, bias=sa_c[:, k:k + 1],
                                   scale=ca_c[:, k:k + 1]).then_inc(s["hh"], 1)
                for u in range(16):
                    m, t = u // 4, u // 2 % 2
                    need(act, "qk", it, u + 1)
                    if u >= 2:
                        need(act, "lo", it, u - 1)
                        act.wait_ge(s_qkw[u % 2], 32 * (u // 2))
                    else:
                        need(act, "hl", it, 2 * KT)
                    b_ = (bqs, bks)[t][:, m:m + 1]
                    act.activation(wk[:, u % 2, :], pC[:, u % 2, :], ACT.Identity, bias=b_, scale=QSCALE)
                    act.activation(hi_s[:, u % 2, :], pC[:, u % 2, :], ACT.Identity, bias=b_, scale=QSCALE).then_inc(s["hi"], 1)
                for g in range(NG):
                    for st, (c, kt, q0) in enumerate(STEPS):
                        for hp in range(2):
                            v = 2 * (g * NS + st) + hp
                            need(act, "st", it, v + 1)
                            if g * NS + st >= 2:
                                need(act, "pv", it, g * NS + st - 1)
                            act.activation(p_buf[:, st % 2, 2 * hp:2 * hp + 2, q0:CH], AB[v % 2][:, :, q0:CH],
                                           ACT.Exp).then_inc(s["ex"], 1)
                        if st == NC * 2:
                            evac_chunk(act, it, g, 0)
                    evac_chunk(act, it, g, 1)
                for i in range(NT):
                    need(act, "tr", it, i + 1)
                    if i >= 2:
                        need(act, "lg", it, i - 1)
                        need(act, "h2l", it, i - 1)
                    else:
                        need(act, "lo", it, 16)
                    src = pB[:, i % 2, :].rearrange("p (k q) -> p k q", k=KT)
                    act.activation(wk[:, i % 2, :].rearrange("p (k q) -> p k q", k=KT), src, ACT.Copy).then_inc(s["wk"], 1)
                    act.activation(h_hi[:, :, i * P:i * P + P], src, ACT.Copy).then_inc(s["h2h"], 1)
                    need(act, "lg", it, i + 1)
                    act.activation(th[:, i, :], pC[:, i % 2, 0:E], ACT.Tanh, scale=0.5).then_inc(s["th"], 1)
                for w in range(4):
                    need(act, "gu", it, w + 1)
                    if w >= 2:
                        need(act, "hs", it, w - 1)
                    else:
                        need(act, "h2l", it, NT)
                    act.activation(wk[0:FH, w % 2, :], pA[0:FH, w % 2, :], ACT.Tanh, scale=0.5).then_inc(s["tg"], 1)
                end_of_batch(act, "act")

            batches(act, body)

            def xcopy(e, r):
                act.wait_ge(s["xte"], e + 1)
                act.activation(gt[r % 2][:, :, :], pB[:, r % 2, 0:KT * CAP].rearrange("p (k q) -> p k q", k=KT),
                               ACT.Copy).then_inc(s["gte"], 1)

            def gbcopy(e, r, early):
                act.wait_ge(s["gbm"], e + 1)
                if not early:
                    act.wait_ge(s["ye"], e - 1)
                act.activation(gbs[r % 2][:, :], pD[0:CAP, 0, :], ACT.Copy).then_inc(s["gbs"], 1)

            def htcopy(e, r, early):
                act.wait_ge(s["hte"], e + 1)
                if not early:
                    act.wait_ge(s["dne"], e - 1)
                act.activation(hte[r % 2][0:FH, :, :], pD[0:FH, 1, 0:2 * CAP].rearrange("p (k q) -> p k q", k=2),
                               ACT.Copy).then_inc(s["htc"], 1)

            def slot(e, r, more, early=False):
                act.wait_ge(s["gue"], e + 1)
                if not early:
                    act.wait_ge(s["hhe"], e - 1)
                act.activation(the[r % 2][:, :], pA[0:CAP, r % 2, 0:F], ACT.Tanh, scale=0.5).then_inc(s["the"], 1)
                if more:
                    xcopy(e + 1, r + 1)

            xcopy(0, 0)
            slot(0, 0, True, True)
            htcopy(0, 0, True)
            slot(1, 1, True, True)
            gbcopy(0, 0, True)
            htcopy(1, 1, True)
            slot(2, 2, True)
            gbcopy(1, 1, True)
            htcopy(2, 2, False)
            with act.Fori(0, (E - NW) // NW) as k:
                for r in range(NW):
                    e = k * NW + (r + 3)
                    slot(e, r + 3, True)
                    gbcopy(k * NW + (r + 2), r + 2, False)
                    htcopy(e, r + 3, False)
            slot(E - 1, E - 1, False)
            gbcopy(E - 2, E - 2, False)
            htcopy(E - 1, E - 1, False)
            gbcopy(E - 1, E - 1, False)

        @block.vector
        def _(dve):
            dve.wait_ge(s["csil"], 1)
            dve.scalar_tensor_tensor(out=cts[:, :, :], in0=ctt[:, :, :], scalar=1.0, in1=ct[:, :, :], op0=ALU.add,
                                     op1=ALU.mult).then_inc(s["mch"], 1)
            dve.wait_ge(s["mch"], 1)
            dve.tensor_scalar(cts[:, :, :], cts[:, :, :], 0.5, None, ALU.mult).then_inc(s["csil"], 1)
            for k, (src, n, rows, dst) in enumerate(splits):
                dve.wait_ge(s["wsp_h"], k + 1)
                dve.tensor_tensor(wsl[k % 2][0:rows, 0:n], wstage[k % 2][0:rows, 0:n],
                                  wsh[k % 2][0:rows, 0:n].bitcast(F32), ALU.subtract).then_inc(s["wsp_l"], 1)
            dve.wait_ge(s["modc"], 6)
            chain = [1]

            def link(ins):
                chain[0] += 1
                ins.then_inc(s["mch"], 1)
                dve.wait_ge(s["mch"], chain[0])

            for n in (1, 4):
                link(dve.tensor_scalar(modr[:, n, :], modr[:, n, :], 1.0, None, ALU.add))
            for n in (2, 5):
                link(dve.tensor_scalar(modn[:, :], modr[:, n, :], -1.0, None, ALU.mult))
                link(dve.tensor_tensor(modn[:, :], modn[:, :], modr[:, n, :], ALU.max))
                link(dve.tensor_scalar(modn[:, :], modn[:, :], 0.25, None, ALU.max))
                link(dve.tensor_scalar(modr[:, n, :], modr[:, n, :], 0.0, None, ALU.is_ge))
                link(dve.tensor_scalar(modr[:, n, :], modr[:, n, :], 2.0, -1.0, ALU.mult, ALU.add))
                link(dve.tensor_tensor(modr[:, n, :], modr[:, n, :], modn[:, :], ALU.mult))
            dve.drain().then_inc(s["modv"], 1)
            dve.wait_ge(s["cst_v"], 14)
            dve.wait_ge(s["cst"], 80)

            def body(it):
                n_ch = [0]

                def link(ins):
                    n_ch[0] += 1
                    ins.then_inc(s["vch"], 1)
                    dve.wait_ge(s["vch"], n_ch[0])

                for i in range(NT):
                    if i % 4 == 0:
                        dve.wait_ge(s_x[i // 4], 16)
                    link(dve.bn_stats(stat[:, i, :], x_rows[:, i, :]))
                    link(dve.bn_aggr(mv[:, i, :], stat[:, i, :]))
                    dve.tensor_scalar(var[:, i:i + 1], mv[:, i, 1:2], EPS, None, ALU.add).then_inc(s["var"], 1)
                need(dve, "rs", it, 1)
                for i in range(NT):
                    dve.tensor_scalar(x_rows[:, i, :], x_rows[:, i, :], mv[:, i, 0:1], rstd[:, i:i + 1], ALU.subtract,
                                      ALU.mult).then_inc(s["xn"], 1)
                for n in range(2 * KT):
                    h, k = n // KT, n % KT
                    need(dve, "hh", it, n + 1)
                    dve.tensor_tensor(h_lo[:, k, h * 512:h * 512 + 512], wk[:, n % 2, :],
                                      h_hi[:, k, h * 512:h * 512 + 512].bitcast(F32), ALU.subtract).then_inc(s["hl"], 1)
                for i in range(NT):
                    need(dve, "vp", it, i + 1)
                    dve.tensor_tensor(v_rows[:, i, :], pC[:, i % 2, :], bv_b[:, :], ALU.add).then_inc(s["vr"], 1)

                def qk_low(u):
                    need(dve, "hi", it, u + 1)
                    dve.tensor_tensor(lo_s[:, u % 2, :], wk[:, u % 2, :], hi_s[:, u % 2, :].bitcast(F32),
                                      ALU.subtract).then_inc(s["lo"], 1)

                def unit_max(g, u):
                    i, kc, j, w = UNITS[u]
                    n = g * DPG + u
                    need(dve, "dq", it, n + 1)
                    x0 = kc * CH - i * P + S - P
                    dve.tensor_tensor_reduce(pD[:, n % 2, 0:w], pD[:, n % 2, 0:w], mask[:, x0:x0 + w], 1.0, -3e38, ALU.add,
                                             ALU.max, mx[:, j, i, kc:kc + 1]).then_inc(s["df"], 1)

                def group_max(g):
                    need(dve, "df", it, g * DPG + NU)
                    link(dve.tensor_tensor(mx[:, :, 4:8, 0], mx[:, :, 4:8, 0], mx[:, :, 4:8, 1], ALU.max))
                    dve.tensor_scalar(negm[:, :].rearrange("p (j i) -> p j i", j=GH), mx[:, :, :, 0], -1.0, None,
                                      ALU.mult).then_inc(s["negm"], 1)
                    n = g * DPG + NU
                    need(dve, "dq", it, n + 1)
                    if g:
                        need(dve, "m", it, 16 * g, per=64)
                    dve.tensor_copy(mrow[:, :], pD[0:GH * NT, n % 2, 0:P]).then_inc(s["df"], 1)

                def sum_step(g, c, step):
                    n = g * NC + c
                    if step == 0:
                        need(dve, "od", it, n + 1)
                        if n:
                            need(dve, "an", it, n)
                    else:
                        dve.wait_ge(s["rch"], 4 * n + step)
                    blk = tmp[:, 0, :].rearrange("p (b r) -> p b r", r=32)
                    if step == 0:
                        ins = dve.transpose(tmp[:, 0, :], od[:, 1, :])
                    elif step == 1:
                        ins = dve.reciprocal(rcol[:, :], blk[:, :, 0])
                    elif step == 2:
                        ins = dve.tensor_copy(blk, rcol[:, :].unsqueeze(2).to_broadcast([P, 16, 32]))
                    else:
                        ins = dve.transpose(tmp[:, 1, :], tmp[:, 0, :])
                    ins.then_inc(s["rch"], 1)

                def out_high(g, c):
                    need(dve, "an", it, g * NC + c + 1)
                    dve.tensor_copy(h_hi[:, g, c * CH:(c + 1) * CH], od[:, 0, :]).then_inc(s["ah"], 1)

                for u in range(8):
                    qk_low(u)
                for u in range(8, 16):
                    for k in range((u - 8) * 6, (u - 8) * 6 + 6):
                        unit_max(0, k)
                    qk_low(u)
                group_max(0)
                mid = sum(SHARE[:6])
                for g in range(NG):
                    if g + 1 < NG:
                        for u in range(NU):
                            unit_max(g + 1, u)
                            if g:
                                if u in (2, 4, 6, 8):
                                    sum_step(g - 1, 1, u // 2 - 1)
                                if u == 14:
                                    out_high(g - 1, 1)
                            if u - mid in (0, 2, 4, 6):
                                sum_step(g, 0, (u - mid) // 2)
                            if u - mid == 12:
                                out_high(g, 0)
                        group_max(g + 1)
                    else:
                        for gg, c in ((g - 1, 1), (g, 0), (g, 1)):
                            for step in range(4):
                                sum_step(gg, c, step)
                            out_high(gg, c)

                def tile_sum(i):
                    need(dve, "op", it, i + 1)
                    dve.tensor_tensor(tmp[:, 0, :], pA[:, i % 2, :], ga[:, :], ALU.mult).then_inc(s["of"], 1)
                    need(dve, "of", it, i + 1)
                    need(dve, "xg", it, i + 1)
                    dve.tensor_tensor(x2_rows[:, i, :], tmp[:, 0, :], od[:, i % 2, :], ALU.add).then_inc(s["x2"], 1)
                    need(dve, "x2", it, i + 1)
                    link(dve.bn_stats(stat[:, i, :], x2_rows[:, i, :]))
                    link(dve.bn_aggr(mv[:, i, :], stat[:, i, :]))
                    dve.tensor_scalar(var[:, i:i + 1], mv[:, i, 1:2], EPS, None, ALU.add).then_inc(s["var"], 1)

                def tile_norm(i):
                    need(dve, "rs", it, i + 2)
                    if i:
                        need(dve, "h2", it, i)
                    link(dve.tensor_scalar(tmp[:, 1, :], x2_rows[:, i, :], mv[:, i, 0:1], rstd[:, i:i + 1],
                                           ALU.subtract, ALU.mult))
                    link(dve.tensor_tensor(tmp[:, 1, :], tmp[:, 1, :], cb1[:, :], ALU.mult))
                    if i >= 2:
                        dve.wait_ge(s_hw[i % 2], 16 * (i // 2))
                        need(dve, "tr", it, i - 1)
                    else:
                        dve.wait_ge(s_qkw[i % 2], 256)
                    dve.tensor_tensor(h2b[:, i % 2, :], tmp[:, 1, :], sbm[:, :], ALU.add).then_inc(s["h2"], 1)

                for i in range(NT + 1):
                    if i < NT:
                        tile_sum(i)
                    if i:
                        tile_norm(i - 1)
                for w in range(4):
                    c, fh = w // 2, w % 2
                    need(dve, "tg", it, w + 1)
                    if w:
                        need(dve, "hs", it, w)
                    link(dve.scalar_tensor_tensor(out=tmp[0:FH, 0, :], in0=wk[0:FH, w % 2, :], scalar=1.0,
                                                  in1=pA[0:FH, w % 2, :], op0=ALU.add, op1=ALU.mult))
                    link(dve.scalar_tensor_tensor(out=tmp[0:FH, 1, :], in0=tmp[0:FH, 0, :], scalar=0.5,
                                                  in1=pB[0:FH, w % 2, :], op0=ALU.mult, op1=ALU.mult))
                    hi = hs[0][:, fh, c * CH:(c + 1) * CH]
                    link(dve.tensor_copy(hi, tmp[0:FH, 1, :]))
                    dve.tensor_tensor(hs[1][:, fh, c * CH:(c + 1) * CH], tmp[0:FH, 1, :], hi.bitcast(F32),
                                      ALU.subtract).then_inc(s["hs"], 1)
                need(dve, "hs", it, 4)
                for i in range(NT):
                    need(dve, "dn", it, i + 1)
                    if i:
                        need(dve, "pre", it, i)
                    link(dve.tensor_tensor(tmp[:, 0, :], pC[:, i % 2, :], gb[:, :], ALU.mult))
                    if i >= 2:
                        dve.wait_ge(s_pw[i % 2], 16 * (i // 2))
                    dve.tensor_tensor(pre_s[:, i % 2, :], tmp[:, 0, :], x2_rows[:, i, :], ALU.add).then_inc(s["pre"], 1)

                need(dve, "th", it, NT)
                link(dve.tensor_scalar(sc[:, :, :], th[:, :, :], 0.5, 0.5, ALU.mult, ALU.add))
                link(dve.tensor_tensor(sb_[:, :, :], sc[:, :, :], bias_b[:, :].unsqueeze(1).to_broadcast([P, NT, E]), ALU.add))
                g8 = sb_[:, :, :].rearrange("p i (g e) -> p (i g) e", e=GSIZE)
                dve.tensor_tensor(ta[:, :, :], g8[:, :, 0:4], g8[:, :, 4:8], ALU.max)
                link(dve.tensor_tensor(tb[:, :, :], g8[:, :, 0:4], g8[:, :, 4:8], ALU.min))
                hi_, lo_ = ta, tb
                for wd_, (o1, o2, o3, o4) in ((2, (tc_, td, te, tf)), (1, (ta, tb, ta, tb))):
                    a0, a1 = hi_[:, :, 0:wd_], hi_[:, :, wd_:2 * wd_]
                    b0, b1 = lo_[:, :, 0:wd_], lo_[:, :, wd_:2 * wd_]
                    r1 = o1[:, :, 0:wd_]
                    r2 = o2[:, :, 0:wd_]
                    r3 = o3[:, :, 0:wd_] if wd_ == 2 else ta[:, :, 2:3]
                    r4 = o4[:, :, 0:wd_] if wd_ == 2 else tb[:, :, 2:3]
                    dve.tensor_tensor(r1, a0, a1, ALU.max)
                    dve.tensor_tensor(r2, a0, a1, ALU.min)
                    link(dve.tensor_tensor(r3, b0, b1, ALU.max))
                    link(dve.tensor_tensor(r4, r2, r3, ALU.max))
                    hi_, lo_ = (o1, tf) if wd_ == 2 else (ta[:, :, 0:1], tb[:, :, 2:3])
                link(dve.tensor_tensor(gsum[:, :, :].rearrange("p i (g o) -> p (i g) o", o=1), hi_, lo_, ALU.add))
                other = gsum[:, :, :].unsqueeze(2).to_broadcast([P, NT, GROUPS, GROUPS])
                own = gsum[:, :, :].unsqueeze(3).to_broadcast([P, NT, GROUPS, GROUPS])
                tri_b = tri[:, :].rearrange("p (g h) -> p g h", g=GROUPS).unsqueeze(1).to_broadcast([P, NT, GROUPS, GROUPS])
                dve.tensor_tensor(cmp[:, :, :, :], other, own, ALU.is_gt)
                link(dve.tensor_tensor(ceq[:, :, :, :], other, own, ALU.is_equal))
                link(dve.tensor_tensor(ceq[:, :, :, :], ceq[:, :, :, :], tri_b, ALU.mult))
                link(dve.tensor_tensor(cmp[:, :, :, :], cmp[:, :, :, :], ceq[:, :, :, :], ALU.add))
                link(dve.tensor_reduce(gcnt[:, :, :], cmp[:, :, :, :], AX_X, ALU.add))
                link(dve.tensor_scalar(gsel[:, :, :], gcnt[:, :, :], KGROUPS - 0.5, None, ALU.is_lt))
                link(dve.tensor_scalar(gpen[:, :, :], gsel[:, :, :], BIG, -BIG, ALU.mult, ALU.add))
                ge = "p i (g e) -> p i g e"
                wide = [P, NT, GROUPS, GSIZE]
                link(dve.tensor_tensor(wdn[:, :, :].rearrange(ge, e=GSIZE), sb_[:, :, :].rearrange(ge, e=GSIZE),
                                       gpen[:, :, :].unsqueeze(3).to_broadcast(wide), ALU.add))
                for i in range(NT):
                    last = dve.max(v8[:, i, :], wdn[:, i, :])
                link(last)
                link(dve.memset(v8[:, :, TOPK:8], -BIG))
                for i in range(NT):
                    last = dve.match_replace(rep[:, i, :], v8[:, i, :], wdn[:, i, :], BIG)
                link(last)
                link(dve.scalar_tensor_tensor(out=sel[:, :, :].rearrange(ge, e=GSIZE), in0=rep[:, :, :].rearrange(ge, e=GSIZE),
                                              scalar=BIG, in1=gsel[:, :, :].unsqueeze(3).to_broadcast(wide),
                                              op0=ALU.is_equal, op1=ALU.mult))
                link(dve.tensor_tensor(sc[:, :, :], sel[:, :, :], sc[:, :, :], ALU.mult))
                link(dve.tensor_reduce(wsum[:, :], sc[:, :, :], AX_X, ALU.add))
                link(dve.reciprocal(rws[:, :], wsum[:, :]))
                link(dve.tensor_tensor(valt[:, :, :, :].rearrange("p q h e -> p h q e"),
                                       sel[:, :, :].rearrange("p (h q) e -> p h q e", h=2),
                                       tokn[:, :].rearrange("p (h q) -> p h q", h=2).unsqueeze(3).to_broadcast([P, 2, 4, E]),
                                       ALU.mult))
                dve.scalar_tensor_tensor(out=wdn[:, :, :], in0=sc[:, :, :], scalar=ROUTE_SCALE,
                                         in1=rws[:, :].unsqueeze(2).to_broadcast([P, NT, E]), op0=ALU.mult,
                                         op1=ALU.mult).then_inc(s["val"], 1)
                dve.tensor_scalar(tokn[:, :], tokn[:, :], -float(S), None, ALU.add)
                need(dve, "vt", it, 1)
                link(dve.tensor_copy(keys[:, :], pA[:, 0, :]))
                a, b_ = keys, keys2
                for r in range(ROUNDS):
                    link(dve.max(lb[:, 8 * r:8 * r + 8], a[:, :]))
                    if r + 1 < ROUNDS:
                        link(dve.match_replace(b_[:, :], lb[:, 8 * r:8 * r + 8], a[:, :], 0.0))
                        a, b_ = b_, a
                dve.tensor_copy(lists[:, bass.ds(it * CAP, CAP)], lb[:, :]).then_inc(s["lst"], 1)
                end_of_batch(dve, "dve")

            batches(dve, body)

            dve.wait_ge(s["mrg"], 32)
            a, b_ = mall, mal2
            for r in range(ROUNDS):
                link(dve.max(fin[:, 8 * r:8 * r + 8], a[:, :]))
                if r + 1 < ROUNDS:
                    link(dve.match_replace(b_[:, :], fin[:, 8 * r:8 * r + 8], a[:, :], 0.0))
                    a, b_ = b_, a
            link(dve.scalar_tensor_tensor(out=fz[:, :], in0=fin[:, :], scalar=0.0, in1=slots_f[0:E, :], op0=ALU.is_equal,
                                          op1=ALU.mult))
            link(dve.tensor_scalar(idf[:, :], fin[:, :], -1.0, float(T), ALU.mult, ALU.add))
            link(dve.tensor_tensor(idf[:, :], idf[:, :], fz[:, :], ALU.add))
            dve.drain().then_inc(s["idt"], 1)
            for b in range(B):
                link(dve.tensor_scalar(oge[:, :], idf[:, :], float(b * S), None, ALU.is_ge))
                link(dve.scalar_tensor_tensor(out=ohb[b][:, :], in0=idf[:, :], scalar=float(b * S + S), in1=oge[:, :],
                                              op0=ALU.is_lt, op1=ALU.mult))
            dve.wait_ge(s["fgb"], 16)
            link(dve.tensor_copy(gbp[0][:, :], gbr[:, :]))
            link(dve.tensor_tensor(gbq[0][:, :], gbr[:, :], gbp[0][:, :], ALU.subtract))
            link(dve.tensor_copy(gbp[1][:, :], gbq[0][:, :]))
            link(dve.tensor_tensor(gbq[1][:, :], gbq[0][:, :], gbp[1][:, :], ALU.subtract))
            link(dve.tensor_copy(gbp[2][:, :], gbq[1][:, :]))
            dve.wait_ge(s["vt"], 1)
            dve.tensor_copy(idu[:, :], pA[0:CAP, 0, 0:E]).then_inc(s["idt"], 1)
            dve.drain().then_inc(s["idx"], 1)
            dve.wait_ge(s["g12"], 16 * 15)

            def ohcopy(e, r, early):
                if not early:
                    dve.wait_ge(s["gbm"], e - 1)
                dve.tensor_copy(ohc[r % 2][:, :], oh[:, bass.ds(e * CAP, CAP)]).then_inc(s["oc"], 1)

            def gated(e, r, early):
                dve.wait_ge(s["the"], e + 1)
                if not early:
                    dve.wait_ge(s["hte"], e - 1)
                dve.scalar_tensor_tensor(out=hae[r % 2][:, :], in0=the[r % 2][:, :], scalar=1.0, in1=pA[0:CAP, r % 2, 0:F],
                                         op0=ALU.add, op1=ALU.mult).then_inc(s["ech"], 1)
                dve.wait_ge(s["ech"], e + 1)
                dve.scalar_tensor_tensor(out=hhe[r % 2][:, :], in0=hae[r % 2][:, :], scalar=0.5,
                                         in1=pA[0:CAP, r % 2, F:2 * F], op0=ALU.mult, op1=ALU.mult).then_inc(s["hhe"], 1)

            def weighted(e, r, early):
                dve.wait_ge(s["dne"], e + 1)
                dve.wait_ge(s["gbs"], e + 1)
                if not early:
                    dve.wait_ge(s["sc"], (e - 1) * 16)
                dve.scalar_tensor_tensor(out=ye[r % 2][:, :], in0=pC[0:CAP, r % 2, :], scalar=gath[r % 4][:, bass.ds(e + D, 1)],
                                         in1=gbs[r % 2][:, :], op0=ALU.mult, op1=ALU.mult).then_inc(s["ye"], 1)

            for e in range(3):
                ohcopy(e, e, e < 2)
                gated(e, e, e < 2)
                if e:
                    weighted(e - 1, e - 1, True)
            with dve.Fori(0, (E - NW) // NW) as k:
                for r in range(NW):
                    e = k * NW + (r + 3)
                    ohcopy(e, r + 3, False)
                    gated(e, r + 3, False)
                    weighted(k * NW + (r + 2), r + 2, False)
            ohcopy(E - 1, E - 1, False)
            gated(E - 1, E - 1, False)
            weighted(E - 2, E - 2, False)
            weighted(E - 1, E - 1, False)

        @block.tensor
        def _(pe):
            pe.wait_ge(s["csil"], 2)
            for n in range(6):
                if n >= 4:
                    pe.wait_ge(s["modc"], n - 3)
                for k in range(KT):
                    last = pe.matmul(AB[n // 2 % 2][0:B, n % 2, :], cts[:, k, :], wm[:, k, n * D:(n + 1) * D], start=k == 0,
                                     stop=k == KT - 1)
                last.then_inc(s["modm"], 1)
            pe.wait_ge(s["cst_v"], 14)
            pe.wait_ge(s["modc"], 6)

            def split_mm(dst, lhs, rhs, n):
                terms = [(k, a, b) for k in range(n) for a, b in ((0, 0), (1, 0), (0, 1))]
                for t, (k, a, b) in enumerate(terms):
                    last = pe.matmul(dst, lhs(a, k), rhs(b, k), start=t == 0, stop=t == len(terms) - 1)
                return last

            hT = (h_hi, h_lo)

            def body(it):
                for n in range(2 * KT):
                    h, k = n // KT, n % KT
                    need(pe, "xn", it, 4 * h + 4)
                    if h:
                        need(pe, "hh", it, k + 1)
                    for i in range(4):
                        last = pe.transpose(AB[k // 2][:, k % 2, i * P:i * P + P], x_rows[:, 4 * h + i, k * P:k * P + P],
                                            ident[:, :])
                    last.then_inc(s["xt"], 1)
                pe.wait_ge(s["wv"], 32)
                for i in range(NT):
                    need(pe, "hl", it, KT * (i // 4) + KT)
                    if i >= 2:
                        need(pe, "vr", it, i - 1)
                    split_mm(pC[:, i % 2, :], lambda a, k: hT[a][:, k, i * P:i * P + P], lambda b, k: wv[b][:, k, :],
                             KT).then_inc(s["vp"], 1)
                pe.wait_ge(s["wqk"], 64)

                def qk_unit(u):
                    m, t, c = u // 4, u // 2 % 2, u % 2
                    w = (wq, wk_)[t]
                    if u < 2:
                        need(pe, "vr", it, NT - 1 + u)
                    else:
                        need(pe, "hi", it, u - 1)
                    split_mm(pC[:, u % 2, :], lambda a, k: w[a][:, k, m * P:m * P + P],
                             lambda b, k: hT[b][:, k, c * CH:(c + 1) * CH], KT).then_inc(s["qk"], 1)

                def unit(g, u):
                    i, kc, j, w = UNITS[u]
                    n = g * DPG + u
                    if u == 0:
                        pe.wait_ge(s_stk[g % 3], 128 * (g // 3 + 1))
                    if n >= 2:
                        need(pe, "df", it, n - 1)
                    pe.matmul(pD[:, n % 2, 0:w], q_stk[g % 3][0:STK, j, i * P:i * P + P],
                              k_stk[g % 3][0:STK, j, kc * CH:kc * CH + w], start=True, stop=True).then_inc(s["dq"], 1)

                def turn_max(g):
                    n = g * DPG + NU
                    need(pe, "negm", it, g + 1)
                    pe.transpose(pD[0:GH * NT, n % 2, 0:P], negm[:, :], ident[:, :]).then_inc(s["dq"], 1)

                def scores(g, st):
                    c, kt, q0 = STEPS[st]
                    if st == 0:
                        pe.wait_ge(s["m"], 16 * (g + 1))
                    for hp in range(2):
                        v = 2 * (g * NS + st) + hp
                        if v >= 2:
                            need(pe, "ex", it, v - 1)
                        for t in range(2):
                            j = 2 * hp + t
                            last = pe.matmul(AB[v % 2][:, t, q0:CH], k_stk[g % 3][0:STK, j, kt * P:kt * P + P],
                                             q_stk[g % 3][0:STK, j, c * CH + q0:(c + 1) * CH], start=True, stop=True,
                                             skip_group_check=True)
                            if kt * P >= c * CH:
                                last = pe.matmul(AB[v % 2][:, t, q0:q0 + P], ident_b[:, :], mask_t[:, :], start=False,
                                                 stop=True, skip_group_check=True)
                        last.then_inc(s["st"], 1)

                def values(g, st):
                    c, kt, q0 = STEPS[st]
                    need(pe, "ex", it, 2 * (g * NS + st) + 2)
                    if kt == 0 and g * NC + c >= 1:
                        need(pe, "od", it, g * NC + c)
                    first, final = kt == 0, kt == (c + 1) * CH // P - 1
                    for bank in range(2):
                        for j in range(GH):
                            h = GH * g + j
                            lhs = v_rows[:, kt, h * DH:(h + 1) * DH] if bank == 0 else ones[:, :]
                            last = pe.matmul(pC[j * DH:(j + 1) * DH, bank, q0:CH], lhs, p_buf[:, st % 2, j, q0:CH],
                                             start=first, stop=final, skip_group_check=True)
                    last.then_inc(s["pv"], 1)

                for u in range(8):
                    qk_unit(u)
                for u in range(8, 16):
                    qk_unit(u)
                    for k in range((u - 8) * 6, (u - 8) * 6 + 6):
                        unit(0, k)
                turn_max(0)
                need(pe, "vr", it, NT)
                need(pe, "hi", it, 16)
                for g in range(NG):
                    at_u = 0
                    for st in range(NS):
                        n = SHARE[st] if g + 1 < NG else 0
                        for _ in range(n // 2):
                            unit(g + 1, at_u)
                            at_u += 1
                        scores(g, st)
                        for _ in range(n - n // 2):
                            unit(g + 1, at_u)
                            at_u += 1
                        if st == NS - 1 and g + 1 < NG:
                            turn_max(g + 1)
                        if st:
                            values(g, st - 1)
                    values(g, NS - 1)

                pe.wait_ge(s["wo"], 64)
                need(pe, "at", it, NG * NC)
                need(pe, "ex", it, 2 * NG * NS)

                def project(i):
                    if i >= 2:
                        need(pe, "of", it, i - 1)
                    split_mm(pA[:, i % 2, :], lambda a, k: hT[a][:, k, i * P:i * P + P], lambda b, k: wo[b][:, k, :],
                             KT).then_inc(s["op"], 1)

                def turn(i):
                    need(pe, "h2", it, i + 1)
                    if i >= 2:
                        need(pe, "h2h", it, i - 1)
                    for k in range(KT):
                        last = pe.transpose(pB[:, i % 2, k * P:k * P + P], h2b[:, i % 2, k * P:k * P + P], ident[:, :])
                    last.then_inc(s["tr"], 1)

                def logits(i):
                    need(pe, "wk", it, i + 1)
                    if i >= 2:
                        need(pe, "th", it, i - 1)
                    for k in range(KT):
                        last = pe.matmul(pC[:, i % 2, 0:E], wk[:, i % 2, k * P:k * P + P], gw[:, k, :], start=k == 0,
                                         stop=k == KT - 1)
                    last.then_inc(s["lg"], 1)

                project(0)
                project(1)
                for i in range(NT):
                    if i + 2 < NT:
                        project(i + 2)
                    turn(i)
                    logits(i)
                need(pe, "h2l", it, NT)
                need(pe, "th", it, NT)
                for w in range(4):
                    c, fh = w // 2, w % 2
                    if w >= 2:
                        need(pe, "hs", it, w - 1)
                    for dst, off in ((pA, 0), (pB, F)):
                        last = split_mm(dst[0:FH, w % 2, :], lambda a, k: wsg[a][:, k, off + fh * FH:off + fh * FH + FH],
                                        lambda b, k: hT[b][:, k, c * CH:(c + 1) * CH], KT)
                    last.then_inc(s["gu"], 1)
                pe.wait_ge(s["wsd"], 32)
                for i in range(NT):
                    need(pe, "hs", it, 2 if i < 4 else 4)
                    if i >= 2:
                        need(pe, "pre", it, i - 1)
                    split_mm(pC[:, i % 2, :], lambda a, k: hs[a][:, k, i * P:i * P + P], lambda b, k: wsd[b][:, k, :],
                             2).then_inc(s["dn"], 1)
                need(pe, "val", it, 1)
                for q in range(4):
                    last = pe.transpose(pA[:, 0, q * P:q * P + P], valt[:, q, :, :].rearrange("p h e -> p (h e)"), ident[:, :])
                last.then_inc(s["vt"], 1)
                end_of_batch(pe, "pe")

            batches(pe, body)

            pe.wait_ge(s["idt"], 1)
            pe.transpose(pA[0:CAP, 0, 0:E], idf[:, :], ident[0:E, 0:E]).then_inc(s["vt"], 1)
            pe.wait_ge(s["idt"], 2)

            def turn_x(e, r, uses):
                pe.wait_ge(s_ga[r % 4], uses)
                for k in range(KT):
                    last = pe.transpose(pB[:, r % 2, k * CAP:(k + 1) * CAP], gath[r % 4][:, k * P:k * P + P],
                                        ident[0:CAP, 0:CAP])
                last.then_inc(s["xte"], 1)

            def gate_up(e, r, uses):
                pe.wait_ge(s["gte"], e + 1)
                pe.wait_ge(s_we[r % 4], uses)
                for k in range(KT):
                    last = pe.matmul(pA[0:CAP, r % 2, 0:2 * F], gt[r % 2][:, k, :], weg[r % 4][:, k, :], start=k == 0,
                                     stop=k == KT - 1)
                last.then_inc(s["gue"], 1)

            def down(e, r, early):
                pe.wait_ge(s["htc"], e + 1)
                if not early:
                    pe.wait_ge(s["ye"], e - 1)
                for k in range(2):
                    last = pe.matmul(pC[0:CAP, r % 2, :], hte[r % 2][:, k, :], wed[r % 4][:, k, :], start=k == 0, stop=k == 1)
                last.then_inc(s["dne"], 1)
                pe.wait_ge(s["oc"], e + 1)
                if not (early and r == 0):
                    pe.wait_ge(s["gbs"], e)
                pe.matmul(pD[0:CAP, 0, :], ohc[r % 2][:, :], gb12[:, :], start=True, stop=True).then_inc(s["gbm"], 1)

            def turn_h(e, r, first):
                pe.wait_ge(s["hhe"], e + 1)
                if not first:
                    pe.wait_ge(s["htc"], e)
                for k in range(2):
                    last = pe.transpose(pD[0:FH, 1, k * CAP:(k + 1) * CAP], hhe[r % 2][:, k * FH:(k + 1) * FH],
                                        ident[0:CAP, 0:CAP])
                last.then_inc(s["hte"], 1)

            pe.wait_ge(s["ez"], NW + 2)
            turn_x(0, 0, 16)
            for e in range(3):
                gate_up(e, e, 32)
                turn_x(e + 1, e + 1, 16)
                if e:
                    down(e - 1, e - 1, True)
                turn_h(e, e, e == 0)
            with pe.Fori(0, (E - NW) // NW) as k:
                for r in range(NW):
                    e = k * NW + (r + 3)
                    gate_up(e, r + 3, k * 32 + 32 * ((r + 3) // 4 + 1))
                    turn_x(k * NW + (r + 4), r + 4, k * 16 + 16 * ((r + 4) // 4 + 1))
                    down(k * NW + (r + 2), r + 2, False)
                    turn_h(e, r + 3, False)
            gate_up(E - 1, E - 1, 32 * (E // 4))
            down(E - 2, E - 2, False)
            turn_h(E - 1, E - 1, False)
            down(E - 1, E - 1, False)


def _tiles(a):
    import numpy as np
    k = a.shape[-2] // P
    a = a.reshape(*a.shape[:-2], k, P, a.shape[-1])
    return np.ascontiguousarray(np.moveaxis(a, -3, -2))


def kernel(**inputs):
    import numpy as np
    import concourse.bacc as bacc
    from concourse.bass_utils import run_bass_kernel_spmd as run

    g = {k: np.asarray(v) for k, v in inputs.items()}
    w = {k[7:]: v for k, v in g.items() if k.startswith("L0_ffn_")}
    gate_up = np.concatenate([w["w_gate"], w["w_up"]], axis=-1)
    shared = np.concatenate([w["ws_gate"], w["ws_up"]], axis=-1)
    arrays = {
        "x": np.ascontiguousarray(g["L0_attn_X"].reshape(T, D)),
        "wqkvo": np.stack([_tiles(g["L0_attn_" + n].T).reshape(P, KT * D) for n in ("Wq", "Wk", "Wv", "Wo")]),
        "bq": g["L0_attn_bq"].reshape(KT, P).T, "bk": g["L0_attn_bk"].reshape(KT, P).T, "bv": g["L0_attn_bv"], "bo": g["L0_attn_bo"],
        "gate_w": _tiles(w["gate_w"]),
        "bias": w["bias"],
        "w_gu": _tiles(gate_up),
        "w_dn": np.ascontiguousarray(np.moveaxis(w["w_down"].reshape(E, 2, FH, D), 1, 2)),
        "ws_gu": _tiles(shared).reshape(P, KT * 2 * F),
        "ws_dn": np.ascontiguousarray(np.moveaxis(w["ws_down"].reshape(2, FH, D), 0, 1)).reshape(FH, 2 * D),
        "c_t": _tiles(g["L0_c"].T),
        "wmod": _tiles(g["L0_wmod"]),
    }
    nc = bacc.Bacc("TRN2", target_bir_lowering=False, num_devices=1)
    args = []
    feed = {}
    for name, a in arrays.items():
        a = np.ascontiguousarray(a)
        feed["in_" + name] = a
        args.append(nc.dram_tensor("in_" + name, a.shape, mybir.dt.from_np(a.dtype), kind="ExternalInput").ap())
    out = nc.dram_tensor("out_0", (T + CAP, D), F32, kind="ExternalOutput").ap()
    build(nc, *args, out)
    r = run(nc, [feed], core_ids=[0])
    return r.results[0]["out_0"][:T].reshape(B, S, D)
```

```python
from contextlib import ExitStack

import concourse.bass as bass
from concourse import mybir

ALU = mybir.AluOpType
ACT = mybir.ActivationFunctionType
AX_X = mybir.AxisListType.X
F32 = mybir.dt.float32
F32R = mybir.dt.float32r
BF16 = mybir.dt.bfloat16
U32 = mybir.dt.uint32

P = 128
B, S, D = 4, 1024, 512
T = B * S
HEADS, DH = 16, 32
KT = D // P
NT = S // P
CH = 512
NC = S // CH
GH = P // DH
NG = HEADS // GH
E, TOPK, F = 64, 6, 192
FH = F // 2
GROUPS, GSIZE, KGROUPS = 8, 8, 4
CAP = 2 * (2 * 256 * TOPK // E)
ROUNDS = CAP // 8
EPS = 1e-5
QSCALE = float(DH) ** -0.25
ROUTE_SCALE = 2.5
BIG = 1e30
KiB = 1024
STK = 3 * DH + 1


def chunk_steps():
    return [(c, kt, max(0, kt * P - c * CH)) for c in range(NC) for kt in range((c + 1) * CH // P)]


def max_units():
    return [(i, kc, j, min(CH, (i + 1) * P - kc * CH))
            for i in reversed(range(NT)) for kc in range(i * P // CH + 1) for j in range(GH)]


STEPS = chunk_steps()
UNITS = max_units()
NS, NU = len(STEPS), len(UNITS)
DPG = NU + 1


def share_units():
    total = sum(u[3] for u in UNITS)
    work = sum(CH - q0 for _, _, q0 in STEPS)
    out, done, at, seen = [], 0, 0, 0
    for _, _, q0 in STEPS:
        seen += CH - q0
        n = 0
        while at < NU and done < total * min(1.0, 1.2 * seen / work):
            done += UNITS[at][3]
            at += 1
            n += 1
        out.append(n)
    out[-1] += NU - at
    return out


SHARE = share_units()
QK_FIRST = 8
V_ALONE = 5


def beside(n):
    slots = NT + 16 - QK_FIRST - V_ALONE
    n -= V_ALONE
    return list(range(NU * n // slots, NU * (n + 1) // slots)) if n >= 0 else []

BATCH_SIGNALS = """xn xt hh hl vp vr qk hi lo dq df negm st ex pv od rch an ah at of x2 op xg var rs h2 tr wk h2h h2l lg th gu tg hs dn pre
    val vt lst vch x0 x1 mod wv wqk qkw0 qkw1 stk0 stk1 stk2 m col wq up lbd key sg wo wsd xi0 xi1 hw0 hw1 ww pw0 pw1 gabo""".split()


def build(nc, x, wqkvo, bq, bk, bv, bo, gate_w, bias, w_gu, w_dn, ws_gu, ws_dn, c_t, wmod, out):
    scr_w = nc.dram_tensor("scr_w", [4, 2, P, KT * D], F32, kind="Internal").ap()
    scr_gu = nc.dram_tensor("scr_gu", [2, P, KT * 2 * F], F32, kind="Internal").ap()
    scr_dn = nc.dram_tensor("scr_dn", [2, FH, 2 * D], F32, kind="Internal").ap()
    scr_qk = nc.dram_tensor("scr_qk", [2, 2, D, S], F32, kind="Internal").ap()
    scr_row = nc.dram_tensor("scr_row", [2, GH * S], F32, kind="Internal").ap()
    scr_mod = nc.dram_tensor("scr_mod", [B, 6, D], F32, kind="Internal").ap()
    HW = D + E
    htab = nc.dram_tensor("htab", [T + CAP, HW], F32, kind="Internal").ap()

    ctx = ExitStack()
    with ctx:
        arena = ctx.enter_context(nc.sbuf_tensor("arena", [P, 207 * KiB // 4], F32))
        del arena
        base = nc.sbuf_base - 207 * KiB

        def at(name, off, shape, dt=F32):
            return nc.alloc_sbuf_tensor_at(name, shape, dt, offset=base + off)

        def pair(name):
            return ctx.enter_context(nc.psum_tensor(name, [P, 2, 512], F32))

        sems = {}

        def sem(name):
            sems[name] = ctx.enter_context(nc.semaphore("s_" + name))
            return sems[name]

        pA, pB, pC, pD = (pair(n) for n in ("pA", "pB", "pC", "pD"))
        AB, AD = [pA, pB], [pA, pD]

        h_hi = at("h_hi", 0, [P, KT, S], F32R)
        h_lo = at("h_lo", 16 * KiB, [P, KT, S], F32R)
        v_rows = at("v_rows", 32 * KiB, [P, NT, D])
        x2_rows = at("x2_rows", 32 * KiB, [P, NT, D])
        STK0 = 48 * KiB
        q_stk = [at(f"q_stk{n}", STK0 + 32 * KiB * n, [P, GH, S], F32R) for n in range(3)]
        k_stk = [at(f"k_stk{n}", STK0 + 32 * KiB * n + 16 * KiB, [P, GH, S], F32R) for n in range(3)]
        wv = [at(f"wv{n}", STK0 + 64 * KiB + 8 * KiB * n, [P, KT, D], F32R) for n in range(2)]
        wq = [at(f"wq{n}", 144 * KiB + 8 * KiB * n, [P, KT, D], F32R) for n in range(2)]
        wk_ = [at(f"wk{n}", STK0 + 80 * KiB + 8 * KiB * n, [P, KT, D], F32R) for n in range(2)]
        wo = [at(f"wo{n}", STK0 + 32 * KiB + 8 * KiB * n, [P, KT, D], F32R) for n in range(2)]
        wsg = [at(f"wsg{n}", STK0 + 48 * KiB + 6 * KiB * n, [P, KT, 2 * F], F32R) for n in range(2)]
        wsd = [at(f"wsd{n}", STK0 + 80 * KiB + 4 * KiB * n, [FH, 2, D], F32R) for n in range(2)]
        hs = [at(f"hs{n}", STK0 + (88, 24)[n] * KiB, [FH, 2, S], F32R) for n in range(2)]
        p_buf = at("p_buf", 144 * KiB, [P, 2, GH, CH])
        x_rows = at("x_rows", STK0 + 64 * KiB, [P, NT, D])
        mask = at("mask", 160 * KiB, [P, S])
        x_in = at("x_in", 164 * KiB, [P, 2, D])
        wk = at("wk", 168 * KiB, [P, 2, 512])
        hi_s = at("hi_s", 172 * KiB, [P, 2, 512], F32R)
        lo_s = at("lo_s", 176 * KiB, [P, 2, 512], F32R)
        pre_s = at("pre_s", 172 * KiB, [P, 2, 512])
        od = at("od", 180 * KiB, [P, 2, CH])
        tmp = at("tmp", 184 * KiB, [P, 2, 512])
        h2b = at("h2b", 176 * KiB, [P, 2, 512])
        ga = at("ga", 188 * KiB, [P, D])
        gabo = at("gabo", 190 * KiB, [P, D])
        cb1 = at("cb1", 192 * KiB, [P, D])
        sbm = at("sbm", 194 * KiB, [P, D])
        gb = at("gb", 196 * KiB, [P, D])
        bv_b = at("bv_b", 198 * KiB, [P, D])
        gw = at("gw", 200 * KiB, [P, KT, E])
        ident_b = at("ident_b", 201 * KiB, [P, P], BF16)
        mask_t = at("mask_t", 201 * KiB + 256, [P, P], BF16)
        run_a = at("run_a", 201 * KiB + 512, [E, 3 * CAP])
        run_b = at("run_b", 168 * KiB + 512, [E, 3 * CAP])
        first = at("first", 170 * KiB, [E, CAP])
        ident = at("ident", 203 * KiB + 512, [P, P])
        m0 = 204 * KiB
        ones = at("ones", m0, [P, DH])
        mx = at("mx", m0 + 128, [P, GH, NT, 2])
        negm = at("negm", m0 + 384, [P, GH * NT])
        mrow = at("mrow", m0 + 512, [GH * NT, P], F32R)
        stat = at("stat", m0 + 1024, [P, NT, 6])
        mv = at("mv", m0 + 1216, [P, NT, 2])
        var = at("var", m0 + 1280, [P, NT])
        rstd = at("rstd", m0 + 1312, [P, NT])
        nhalf = at("nhalf", m0 + 1344, [P, NT])
        tokn = at("tokn", m0 + 1376, [P, NT])
        sa_c = at("sa_c", m0 + 1408, [P, KT])
        ca_c = at("ca_c", m0 + 1424 + 16, [P, KT])
        bq_c = at("bq_c", m0 + 1472, [P, KT])
        bk_c = at("bk_c", m0 + 1504, [P, KT])
        bqs = at("bqs", m0 + 1536, [P, KT])
        bks = at("bks", m0 + 1568, [P, KT])
        bias_b = at("bias_b", m0 + 1600, [P, E])
        tri = at("tri", m0 + 1856, [P, GROUPS * GROUPS])
        slots_f = at("slots_f", m0 + 2112, [P, CAP])
        v8 = at("v8", m0 + 2496, [P, NT, 8])
        wsum = at("wsum", m0 + 2752, [P, NT])
        rws = at("rws", m0 + 2784, [P, NT])
        rcol = at("rcol", m0 + 2816, [P, CH // 32])

        def rt(name, off, shape, dt=F32):
            return at(name, STK0 + off, shape, dt)
        th = rt("th", 0, [P, NT, E])
        sc = rt("sc", 2048, [P, NT, E])
        sb_ = rt("sb_", 4096, [P, NT, E])
        cmp = rt("cmp", 6144, [P, NT, GROUPS, GROUPS])
        ceq = rt("ceq", 8192, [P, NT, GROUPS, GROUPS])
        rep = rt("rep", 10240, [P, NT, E])
        sel = rt("sel", 12288, [P, NT, E])
        wdn = rt("wdn", 14336, [P, NT, E])
        valt = rt("valt", 16384, [P, 4, 2, E])
        ta = rt("ta", 18432, [P, E, 4])
        tb = rt("tb", 19456, [P, E, 4])
        tc_ = rt("tc_", 20480, [P, E, 2])
        td = rt("td", 20992, [P, E, 2])
        te = rt("te", 21504, [P, E, 2])
        tf = rt("tf", 22016, [P, E, 2])
        gsum = rt("gsum", 22528, [P, NT, GROUPS])
        gcnt = rt("gcnt", 22784, [P, NT, GROUPS])
        gsel = rt("gsel", 23040, [P, NT, GROUPS])
        gpen = rt("gpen", 23296, [P, NT, GROUPS])
        keys = at("keys", 164 * KiB, [P, 512])
        keys2 = at("keys2", 166 * KiB, [P, 512])
        lb = at("lb", 168 * KiB, [P, CAP])

        wstage = [at(f"wstage{n}", STK0 + 48 * KiB + 8 * KiB * n, [P, KT * D]) for n in range(2)]
        wsh = [at(f"wsh{n}", STK0 + 64 * KiB + 8 * KiB * n, [P, KT * D], F32R) for n in range(2)]
        wsl = [at(f"wsl{n}", STK0 + 80 * KiB + 8 * KiB * n, [P, KT * D], F32R) for n in range(2)]
        wm = at("wm", STK0, [P, KT, 6 * D])
        modr = at("modr", 144 * KiB, [B, 6, D])
        modn = at("modn", 156 * KiB, [B, D])
        ct = at("ct", 32 * KiB, [P, KT, B])
        ctt = at("ctt", 32 * KiB + 64, [P, KT, B])
        cts = at("cts", 32 * KiB + 128, [P, KT, B])
        zrow = at("zrow", 33 * KiB, [CAP, HW])
        onev = at("onev", 0, [1, 2 * GH * S])

        NW = 4
        weg = [at(f"weg{n}", 6 * KiB * n, [P, KT, 2 * F]) for n in range(NW)]
        wed = [at(f"wed{n}", 24 * KiB + 4 * KiB * n, [FH + 1, 2, D]) for n in range(NW)]
        gath = [at(f"gath{n}", 48 * KiB + 2304 * n, [CAP, HW]) for n in range(NW)]
        gt = [at(f"gt{n}", 58 * KiB + 1536 * n, [P, KT, CAP]) for n in range(2)]
        the = [at(f"the{n}", 62 * KiB + 768 * n, [CAP, F]) for n in range(2)]
        hae = [at(f"hae{n}", 64 * KiB + 768 * n, [CAP, F]) for n in range(2)]
        hhe = [at(f"hhe{n}", 66 * KiB + 768 * n, [CAP, F]) for n in range(2)]
        hte = [at(f"hte{n}", 68 * KiB + 768 * n, [FH + 1, 2, CAP]) for n in range(2)]
        gbs = [at(f"gbs{n}", 70 * KiB + 2048 * n, [CAP, D]) for n in range(2)]
        ye = [at(f"ye{n}", 74 * KiB + 2048 * n, [CAP, D]) for n in range(2)]
        idg = [at(f"idg{n}", 78 * KiB + 32 * n, [CAP, 1], U32) for n in range(NW)]
        ids = [at(f"ids{n}", 78 * KiB + 32 * NW + 32 * n, [CAP, 1], U32) for n in range(NW)]
        ohc = [at(f"ohc{n}", 79 * KiB + 256 * n, [3 * B, CAP], BF16) for n in range(2)]
        idu = at("idu", 80 * KiB, [CAP, E], U32)
        oh = at("oh", 81 * KiB, [3 * B, E * CAP], BF16)
        gb12 = at("gb12", 94 * KiB, [3 * B, D], BF16)
        fz = at("fz", 103 * KiB, [E, CAP])
        idf = at("idf", 104 * KiB, [E, CAP])
        oge = at("oge", 105 * KiB, [E, CAP])
        ohb = [at(f"ohb{n}", 106 * KiB + 256 * n, [E, CAP], BF16) for n in range(B)]
        gbr = at("gbr", 108 * KiB, [B, D])
        gbp = [at(f"gbp{n}", 110 * KiB + 1024 * n, [B, D], BF16) for n in range(3)]
        gbq = [at(f"gbq{n}", 114 * KiB + 2048 * n, [B, D]) for n in range(2)]

        for n in BATCH_SIGNALS:
            sem(n)
        batch_sems = [sems[n] for n in BATCH_SIGNALS]
        for n in ("x_1st", "col_1st", "wq_1st", "var_1st", "rs_1st", "xn_1st", "key_1st", "cst", "cst_v", "ld", "wst0", "wst1", "wsp_h", "wsp_l", "wwr0", "wwr1", "modm", "modc", "modv", "mw",
                  "csil", "zr",
                  "mrg", "mch", "idt", "idx", "ohd", "g12", "pre_idx",
                  "we0", "we1", "we2", "we3", "ga0", "ga1", "ga2", "ga3", "ic", "is", "xte", "gte", "gue", "the", "hhe",
                  "hte", "htc", "dne", "gbm", "gbs", "ye", "sc", "oc", "ech", "fgb", "ez", "pas", "w_last", "vt_last",
                  "lb_last", "end", "cleared", "go_sp", "go_act", "go_dve", "go_pe", "on_sp", "on_act", "on_dve", "on_pe"):
            sem(n)
        s = sems
        s_x, s_qkw, s_stk = [s["x0"], s["x1"]], [s["qkw0"], s["qkw1"]], [s["stk0"], s["stk1"], s["stk2"]]
        s_xi, s_hw, s_pw = [s["xi0"], s["xi1"]], [s["hw0"], s["hw1"]], [s["pw0"], s["pw1"]]
        s_we, s_ga = [s[f"we{n}"] for n in range(4)], [s[f"ga{n}"] for n in range(4)]
        s_wst, s_wwr = [s["wst0"], s["wst1"]], [s["wwr0"], s["wwr1"]]

        VCH_PER = 183

        def need(eng, name, it, n, per=None):
            eng.wait_ge(s[name], n)

        def batches(eng, body):
            with eng.Fori(0, B) as it:
                body(it)

        def end_of_batch(eng, name):
            share = ("sp", "act", "dve", "pe").index(name)
            eng.drain().then_inc(s["end"], 1)
            eng.wait_ge(s["go_" + name], 1)
            eng.sem_clear(s["go_" + name])
            for x in batch_sems[share::5]:
                eng.sem_clear(x)
            eng.sem_inc(s["cleared"], 1)
            eng.wait_ge(s["on_" + name], 1)
            eng.sem_clear(s["on_" + name])

        splits = [(wqkvo[k], KT * D, P, scr_w[k]) for k in range(4)]
        splits += [(ws_gu, KT * 2 * F, P, scr_gu), (ws_dn, 2 * D, FH, scr_dn)]

        def store_split(sp, k):
            src, n, rows, dst = splits[k]
            sp.wait_ge(s["wsp_l"], k + 1)
            for part, t in ((0, wsh), (1, wsl)):
                sp.dma_start(dst[part], t[k % 2][0:rows, 0:n].bitcast(F32)).then_inc(s_wwr[k % 2], 16)

        def load_expert(sp, e, r, reused):
            src_g = w_gu[bass.ds(e, 1)].rearrange("o p k f -> (o p) k f")
            src_d = w_dn[bass.ds(e, 1)].rearrange("o p k f -> (o p) k f")
            if reused:
                sp.wait_ge(s["dne"], e - (NW - 1))
            sp.dma_start(weg[r][:, :, :], src_g).then_inc(s_we[r], 16)
            sp.dma_start(wed[r][0:FH, :, :], src_d).then_inc(s_we[r], 16)

        def evac_chunk(act, it, g, c):
            need(act, "pv", it, g * NS + (4 if c == 0 else NS))
            n = g * NC + c
            if n >= 1:
                need(act, "at", it, n)
            act.activation(od[:, :, :], pC[:, :, :], ACT.Copy).then_inc(s["od"], 1)

        block = ctx.enter_context(nc.Block())

        @block.sync
        def _(sp):
            sp.dma_start(ct[:, :, :], c_t).then_inc(s["ld"], 16)
            sp.dma_start(wm[:, :, :], wmod).then_inc(s["ld"], 16)
            for k, (src, n, rows, dst) in enumerate(splits):
                if k >= 2:
                    sp.wait_ge(s["wsp_l"], k - 1)
                sp.dma_start(wstage[k % 2][0:rows, 0:n], src).then_inc(s_wst[k % 2], 16)
                if k >= 1:
                    store_split(sp, k - 1)
            store_split(sp, len(splits) - 1)
            sp.dma_start(bq_c[:, :], bq).then_inc(s["cst"], 16)
            sp.dma_start(bk_c[:, :], bk).then_inc(s["cst"], 16)
            sp.dma_start(bv_b[:, :], bv.partition_broadcast(P)).then_inc(s["cst"], 16)
            sp.dma_start(bias_b[:, :], bias.partition_broadcast(P)).then_inc(s["cst"], 16)
            sp.dma_start(gw[:, :, :], gate_w).then_inc(s["cst"], 16)
            sp.wait_ge(s["zr"], 3)
            sp.dma_start(htab[T:T + CAP, :], zrow[:, :]).then_inc(s["pre_idx"], 16)
            sp.dma_start(out[T:T + CAP, :], zrow[:, 0:D]).then_inc(s["pre_idx"], 16)
            for r in range(2):
                sp.dma_start(scr_row[r:r + 1, :], onev[:, r * GH * S:(r + 1) * GH * S]).then_inc(s["pre_idx"], 16)
            sp.wait_ge(s["modv"], 1)
            sp.dma_start(scr_mod, modr[:, :, :]).then_inc(s["mw"], 16)
            sp.wait_ge(s["mw"], 16)
            sp.wait_ge(s["pre_idx"], 64)
            for n in range(2):
                sp.wait_ge(s_wwr[n], 32 * 3)

            def rows_of(b):
                return x.rearrange("(b t p) d -> b p t d", b=B, p=P)[bass.ds(b, 1)].rearrange("o p t d -> (o p) t d")

            def table_rows(b):
                return htab[0:T, :].rearrange("(b t p) d -> b t p d", b=B, p=P)[bass.ds(b, 1)].rearrange("o t p d -> (o t) p d")

            def store_weights(b, signal):
                sp.dma_start(table_rows(b).rearrange("t p d -> p t d")[:, :, D:HW], wdn[:, :, :]).then_inc(signal, 16)

            def load_columns(b, signal):
                mod = scr_mod[bass.ds(b, 1)].rearrange("o m d -> (o m) d")
                for n, dst in ((0, sa_c), (1, ca_c)):
                    sp.dma_start(dst[:, :], mod[n].rearrange("(k p) -> p k", p=P), allow_slow_non_contiguous=True).then_inc(signal, 16)

            def load_split(dst, src, signal, k=KT):
                for n in range(2):
                    sp.dma_start(dst[n][:, :, :].bitcast(F32), src[n].rearrange("p (k d) -> p k d", k=k)).then_inc(signal, 16)

            for h in range(2):
                sp.dma_start(x_rows[:, 4 * h:4 * h + 4, :], rows_of(0)[:, 4 * h:4 * h + 4, :]).then_inc(s["x_1st"], 16)
            load_columns(0, s["col_1st"])
            load_split(wq, scr_w[0], s["wq_1st"])
            sp.wait_ge(s["key_1st"], 3)

            def body(it):
                xb = rows_of((it + 1) % B)
                xt = x.rearrange("(b t p) d -> b t p d", b=B, p=P)[bass.ds(it, 1)].rearrange("o t p d -> (o t) p d")
                ht = table_rows(it)
                ot = out[0:T, :].rearrange("(b t p) d -> b t p d", b=B, p=P)[bass.ds(it, 1)].rearrange(
                    "o t p d -> (o t) p d")
                mod = scr_mod[bass.ds(it, 1)].rearrange("o m d -> (o m) d")
                load_split(wk_, scr_w[1], s["wqk"])
                store_weights((it + B - 1) % B, s["ww"])
                for n, dst in ((2, ga), (4, cb1), (3, sbm), (5, gb)):
                    sp.dma_start(dst[:, :], mod[n].partition_broadcast(P)).then_inc(s["mod"], 16)
                sp.dma_start(gabo[:, :], bo.partition_broadcast(P)).then_inc(s["mod"], 16)
                need(sp, "xt", it, 2 * KT)
                load_split(wv, scr_w[2], s["wv"])

                def load_stack(g):
                    for u in range(2):
                        sp.wait_ge(s_qkw[u], 32 * (2 * g + 2))
                    for dst, t, parts in ((q_stk[g % 3], 0, (0, 1, 0)), (k_stk[g % 3], 1, (0, 0, 1))):
                        for r, part in enumerate(parts):
                            src = scr_qk[t, part, g * P:(g + 1) * P, :].rearrange("(j d) s -> d j s", d=DH)
                            sp.dma_start(dst[r * DH:(r + 1) * DH, :, :].bitcast(F32), src).then_inc(s_stk[g % 3], 16)
                    for r, dst in enumerate((q_stk[g % 3], k_stk[g % 3])):
                        sp.dma_start(dst[3 * DH:STK, :, :].rearrange("p j s -> p (j s)").bitcast(F32), scr_row[r:r + 1, :]).then_inc(
                            s_stk[g % 3], 16)

                for u in range(16):
                    m, t, c = u // 4, u // 2 % 2, u % 2
                    need(sp, "lo", it, u + 1)
                    for part, src in ((0, hi_s), (1, lo_s)):
                        sp.dma_start(scr_qk[t, part, m * P:(m + 1) * P, c * CH:(c + 1) * CH],
                                     src[:, u % 2, :].bitcast(F32)).then_inc(s_qkw[u % 2], 16)
                    if u == 3:
                        sp.wait_ge(s["ww"], 16)
                        need(sp, "vt", it, 1)
                        load_stack(0)
                    if u == 7:
                        load_stack(1)

                def shift_row(g):
                    need(sp, "df", it, DPG * (g + 1))
                    sp.dma_start(q_stk[g % 3][3 * DH:STK, :, :].rearrange("p j s -> p (j s)").bitcast(F32),
                                 mrow[:, :].bitcast(F32)).then_inc(s["m"], 16)

                shift_row(0)
                need(sp, "qk", it, 16)
                load_stack(2)
                shift_row(1)
                need(sp, "st", it, 2 * NS)
                load_stack(3)
                shift_row(2)
                need(sp, "st", it, 2 * NS * 2)
                load_split(wo, scr_w[3], s["wo"])
                load_split(wsg, scr_gu, s["wo"])
                shift_row(3)
                need(sp, "st", it, 2 * NS * 3)
                for h in range(2):
                    sp.dma_start(x_rows[:, 4 * h:4 * h + 4, :], xb[:, 4 * h:4 * h + 4, :]).then_inc(s_x[h], 16)
                load_columns((it + 1) % B, s["col"])
                load_split(wsd, scr_dn, s["wsd"], 2)
                need(sp, "lbd", it, 1)
                sp.dma_start(run_a[:, 2 * CAP:3 * CAP], lb[E:2 * E, :]).then_inc(s["up"], 16)

                def load_x(i):
                    if i >= 2:
                        need(sp, "xg", it, i - 1)
                    sp.dma_start(x_in[:, i % 2, :], xt[i]).then_inc(s_xi[i % 2], 16)

                load_x(0)
                load_x(1)
                need(sp, "pv", it, NG * NS)
                load_split(wq, scr_w[0], s["wq"])
                for i in range(NT):
                    if i + 2 < NT:
                        load_x(i + 2)
                    need(sp, "h2", it, i + 1)
                    sp.dma_start(ht[i][:, 0:D], h2b[:, i % 2, :]).then_inc(s_hw[i % 2], 16)
                for i in range(NT):
                    need(sp, "pre", it, i + 1)
                    sp.dma_start(ot[i], pre_s[:, i % 2, :]).then_inc(s_pw[i % 2], 16)
                for n in range(2):
                    sp.wait_ge(s_hw[n], 64)
                    sp.wait_ge(s_pw[n], 64)
                sp.wait_ge(s["col"], 32)
                sp.wait_ge(s["wq"], 32)
                end_of_batch(sp, "sp")

            batches(sp, body)

            store_weights(B - 1, s["w_last"])
            sp.dma_start(gbr[:, :], scr_mod[:, 5, :]).then_inc(s["fgb"], 16)
            for e in range(NW - 1):
                load_expert(sp, e, e, False)
            sp.wait_ge(s["lb_last"], 1)
            sp.dma_start(run_a[:, 2 * CAP:3 * CAP], lb[E:2 * E, :]).then_inc(s["mrg"], 16)
            sp.wait_ge(s["idx"], 1)
            for n in range(3):
                sp.dma_start(gb12[B * n:B * n + B, :], gbp[n][:, :]).then_inc(s["g12"], 16)
                for b in range(B):
                    sp.dma_start(oh[B * n + b:B * n + b + 1, :], ohb[b][:, :]).then_inc(s["g12"], 16)
            load_expert(sp, 3, 3, False)
            with sp.Fori(0, (E - NW) // NW) as k:
                for r in range(NW):
                    load_expert(sp, k * NW + (NW + r), r, True)

        @block.gpsimd
        def _(pool):
            pool.memset(ident[:, :], 0.0).then_inc(s["cst_v"], 1)
            pool.memset(mask[:, :], 0.0).then_inc(s["cst_v"], 1)
            pool.memset(tri[:, :], 1.0).then_inc(s["cst_v"], 1)
            pool.memset(ones[:, :], 1.0).then_inc(s["cst_v"], 1)
            pool.memset(nhalf[:, :], -0.5).then_inc(s["cst_v"], 1)
            pool.memset(ident_b[:, :], 0.0).then_inc(s["cst_v"], 1)
            pool.memset(mask_t[:, :], 0.0).then_inc(s["cst_v"], 1)
            pool.memset(zrow[:, :], 0.0).then_inc(s["zr"], 1)
            pool.memset(onev[:, 0:GH * S], 0.0).then_inc(s["zr"], 1)
            pool.memset(onev[:, GH * S:2 * GH * S], 1.0).then_inc(s["zr"], 1)
            pool.wait_ge(s["cst_v"], 7)
            pool.affine_select(out=ident[:, :], in_=ident[:, :], compare_op=ALU.not_equal, fill=1.0, base=0,
                               pattern=[[-1, P]], channel_multiplier=1).then_inc(s["cst_v"], 1)
            pool.affine_select(out=ident_b[:, :], in_=ident_b[:, :], compare_op=ALU.not_equal, fill=1.0, base=0,
                               pattern=[[-1, P]], channel_multiplier=1).then_inc(s["cst_v"], 1)
            pool.affine_select(out=mask_t[:, :], in_=mask_t[:, :], compare_op=ALU.is_ge, fill=-BIG, base=0,
                               pattern=[[1, P]], channel_multiplier=-1).then_inc(s["cst_v"], 1)
            pool.affine_select(out=mask[:, :], in_=mask[:, :], compare_op=ALU.is_ge, fill=-BIG, base=S - P,
                               pattern=[[-1, S]], channel_multiplier=1).then_inc(s["cst_v"], 1)
            pool.affine_select(out=tri[:, :].rearrange("p (g h) -> p g h", g=GROUPS),
                               in_=tri[:, :].rearrange("p (g h) -> p g h", g=GROUPS), compare_op=ALU.is_ge, fill=0.0,
                               base=-1, pattern=[[1, GROUPS], [-1, GROUPS]], channel_multiplier=0).then_inc(s["cst_v"], 1)
            pool.iota(tokn[:, :], pattern=[[-P, NT]], base=T, channel_multiplier=-1,
                      allow_small_or_imprecise_dtypes=True).then_inc(s["cst_v"], 1)
            pool.iota(slots_f[:, :], pattern=[[1, CAP]], base=0, channel_multiplier=0,
                      allow_small_or_imprecise_dtypes=True).then_inc(s["cst_v"], 1)

            pool.wait_ge(s["var_1st"], NT)
            pool.tensor_tensor(rstd[:, :], var[:, :], nhalf[:, :], ALU.pow).then_inc(s["rs_1st"], 1)

            def body(it):
                def tile_x(i):
                    pool.wait_ge(s_xi[i % 2], 16 * (i // 2) + 16)
                    if i >= 2:
                        need(pool, "x2", it, i - 1)
                    pool.tensor_tensor(od[:, (i + 1) % 2, :], x_in[:, i % 2, :], gabo[:, :], ALU.add).then_inc(s["xg"], 1)

                for n in range(NG * NC):
                    g, c = n // NC, n % NC
                    if n == (NG - 1) * NC:
                        need(pool, "var", it, NT)
                        pool.tensor_tensor(rstd[:, :], var[:, :], nhalf[:, :], ALU.pow).then_inc(s["rs"], 1)
                        need(pool, "mod", it, 16 * 5)
                        pool.tensor_tensor(gabo[:, :], gabo[:, :], ga[:, :], ALU.mult).then_inc(s["gabo"], 1)
                        pool.wait_ge(s["gabo"], 1)
                    if n == NG * NC - 1:
                        pool.wait_ge(s["rch"], 4 * n + 1)
                        tile_x(0)
                    pool.wait_ge(s["rch"], 4 * n + 4)
                    pool.tensor_tensor(od[:, 0, :], od[:, 0, :], tmp[:, 1, :], ALU.mult).then_inc(s["an"], 1)
                    need(pool, "ah", it, n + 1)
                    pool.tensor_tensor(h_lo[:, g, c * CH:(c + 1) * CH], od[:, 0, :],
                                       h_hi[:, g, c * CH:(c + 1) * CH].bitcast(F32), ALU.subtract).then_inc(s["at"], 1)
                def tile_low(i):
                    need(pool, "h2h", it, i + 1)
                    pool.tensor_tensor(h_lo[:, :, i * P:i * P + P], wk[:, i % 2, :].rearrange("p (k q) -> p k q", k=KT),
                                       h_hi[:, :, i * P:i * P + P].bitcast(F32), ALU.subtract).then_inc(s["h2l"], 1)

                need(pool, "at", it, NG * NC)
                for i in range(NT):
                    need(pool, "var", it, NT + i + 1)
                    pool.tensor_tensor(rstd[:, i:i + 1], var[:, i:i + 1], nhalf[:, i:i + 1], ALU.pow).then_inc(s["rs"], 1)
                    if i + 1 < NT:
                        tile_x(i + 1)
                    if i >= 2:
                        tile_low(i - 2)
                tile_low(NT - 2)
                tile_low(NT - 1)
                for i in range(NT):
                    need(pool, "sg", it, i + 1)
                    if i >= 2:
                        pool.wait_ge(s_pw[i % 2], 16 * (i // 2))
                    pool.tensor_tensor(pre_s[:, i % 2, :], tmp[:, i % 2, :], x2_rows[:, i, :], ALU.add).then_inc(s["pre"], 1)
                pool.drain()
                pool.wait_ge(s["end"], 4)
                pool.sem_clear(s["end"])
                for n in ("sp", "act", "dve", "pe"):
                    pool.sem_inc(s["go_" + n], 1)
                for x in batch_sems[4::5]:
                    pool.sem_clear(x)
                pool.wait_ge(s["cleared"], 4)
                pool.sem_clear(s["cleared"])
                for n in ("sp", "act", "dve", "pe"):
                    pool.sem_inc(s["on_" + n], 1)

            batches(pool, body)

            def gather(e, r, reused):
                if reused:
                    pool.wait_ge(s["ye"], e - (NW - 1))
                pool.tensor_copy(idg[r][:, :], idu[:, bass.ds(e, 1)]).then_inc(s["ic"], 1)
                pool.wait_ge(s["ic"], e + 1)
                pool.sem_inc(s["pas"], 1)
                pool.indirect_dma_start(gath[r][:, :], None, htab, bass.IndirectOffsetOnAxis(ap=idg[r][:, :], axis=0)).then_inc(
                    s_ga[r], 16)

            def scatter(e, r, first):
                pool.tensor_copy(ids[r][:, :], idu[:, bass.ds(e, 1)]).then_inc(s["is"], 1)
                pool.wait_ge(s["is"], e + 1)
                pool.wait_ge(s["ye"], e + 1)
                if not first:
                    pool.wait_ge(s["sc"], e * 16)
                pool.sem_inc(s["pas"], 1)
                pool.indirect_dma_start(out, bass.IndirectOffsetOnAxis(ap=ids[r][:, :], axis=0), ye[r % 2][:, :], None,
                                        compute_op=ALU.add).then_inc(s["sc"], 16)

            for z in wed + hte:
                pool.memset(z[FH:FH + 1, :, :], 0.0).then_inc(s["ez"], 1)
            pool.wait_ge(s["w_last"], 16)
            pool.wait_ge(s["idt"], 2)
            for e in range(NW):
                gather(e, e, False)
            scatter(0, 0, True)
            with pool.Fori(0, (E - NW) // NW) as k:
                for r in range(NW):
                    gather(k * NW + (r + 4), r, True)
                    scatter(k * NW + (r + 1), (r + 1) % NW, False)
            for e in range(E - NW + 1, E):
                scatter(e, e % NW, False)
            pool.wait_ge(s["sc"], 16 * E)

        @block.scalar
        def _(act):
            act.wait_ge(s["ld"], 32)
            act.activation(ctt[:, :, :], ct[:, :, :], ACT.Tanh, scale=0.5).then_inc(s["csil"], 1)
            for k, (src, n, rows, dst) in enumerate(splits):
                act.wait_ge(s_wst[k % 2], 16 * (k // 2) + 16)
                if k >= 2:
                    act.wait_ge(s_wwr[k % 2], 32 * (k // 2))
                act.activation(wsh[k % 2][0:rows, 0:n], wstage[k % 2][0:rows, 0:n], ACT.Copy).then_inc(s["wsp_h"], 1)
            for n in range(6):
                act.wait_ge(s["modm"], n + 1)
                act.activation(modr[:, n, :], AB[n // 2 % 2][0:B, n % 2, :], ACT.Copy).then_inc(s["modc"], 1)
            act.wait_ge(s["cst"], 80)
            act.mul(bqs[:, :], bq_c[:, :], QSCALE).then_inc(s["csil"], 1)
            act.mul(bks[:, :], bk_c[:, :], QSCALE).then_inc(s["csil"], 1)
            act.wait_ge(s["csil"], 4)
            act.wait_ge(s["col_1st"], 32)

            def body(it):
                for n in range(2 * KT):
                    h, k = n // KT, n % KT
                    need(act, "xt", it, n + 1)
                    if n >= 2:
                        need(act, "hl", it, n - 1)
                    src = AB[k // 2][:, k % 2, :]
                    act.activation(wk[:, n % 2, :], src, ACT.Identity, bias=sa_c[:, k:k + 1], scale=ca_c[:, k:k + 1])
                    act.activation(h_hi[:, k, h * 512:h * 512 + 512], src, ACT.Identity, bias=sa_c[:, k:k + 1],
                                   scale=ca_c[:, k:k + 1]).then_inc(s["hh"], 1)
                for u in range(16):
                    m, t = u // 4, u // 2 % 2
                    need(act, "qk", it, u + 1)
                    if u >= 2:
                        need(act, "lo", it, u - 1)
                        act.wait_ge(s_qkw[u % 2], 32 * (u // 2))
                    else:
                        need(act, "hl", it, 2 * KT)
                    b_ = (bqs, bks)[t][:, m:m + 1]
                    act.activation(wk[:, u % 2, :], pC[:, u % 2, :], ACT.Identity, bias=b_, scale=QSCALE)
                    act.activation(hi_s[:, u % 2, :], pC[:, u % 2, :], ACT.Identity, bias=b_, scale=QSCALE).then_inc(s["hi"], 1)
                for g in range(NG):
                    for st, (c, kt, q0) in enumerate(STEPS):
                        for hp in range(2):
                            v = 2 * (g * NS + st) + hp
                            need(act, "st", it, v + 1)
                            if g * NS + st >= 2:
                                need(act, "pv", it, g * NS + st - 1)
                            act.activation(p_buf[:, st % 2, 2 * hp:2 * hp + 2, q0:CH], AB[v % 2][:, :, q0:CH],
                                           ACT.Exp).then_inc(s["ex"], 1)
                        if st == NC * 2:
                            evac_chunk(act, it, g, 0)
                    evac_chunk(act, it, g, 1)
                for i in range(NT):
                    need(act, "tr", it, i + 1)
                    if i >= 2:
                        need(act, "lg", it, i - 1)
                        need(act, "h2l", it, i - 1)
                    else:
                        need(act, "lo", it, 16)
                        need(act, "lst", it, 1)
                    src = pB[:, i % 2, :].rearrange("p (k q) -> p k q", k=KT)
                    act.activation(wk[:, i % 2, :].rearrange("p (k q) -> p k q", k=KT), src, ACT.Copy).then_inc(s["wk"], 1)
                    act.activation(h_hi[:, :, i * P:i * P + P], src, ACT.Copy).then_inc(s["h2h"], 1)
                    need(act, "lg", it, i + 1)
                    act.activation(th[:, i, :], pC[:, i % 2, 0:E], ACT.Tanh, scale=0.5).then_inc(s["th"], 1)
                for w in range(4):
                    need(act, "gu", it, w + 1)
                    if w >= 2:
                        need(act, "hs", it, w - 1)
                    else:
                        need(act, "h2l", it, NT)
                    act.activation(wk[0:FH, w % 2, :], pA[0:FH, w % 2, :], ACT.Tanh, scale=0.5).then_inc(s["tg"], 1)
                end_of_batch(act, "act")

            batches(act, body)

            def xcopy(e, r):
                act.wait_ge(s["xte"], e + 1)
                act.activation(gt[r % 2][:, :, :], pB[:, r % 2, 0:KT * CAP].rearrange("p (k q) -> p k q", k=KT),
                               ACT.Copy).then_inc(s["gte"], 1)

            def gbcopy(e, r, early):
                act.wait_ge(s["gbm"], e + 1)
                if not early:
                    act.wait_ge(s["ye"], e - 1)
                act.activation(gbs[r % 2][:, :], pD[0:CAP, 0, :], ACT.Copy).then_inc(s["gbs"], 1)

            def htcopy(e, r, early):
                act.wait_ge(s["hte"], e + 1)
                if not early:
                    act.wait_ge(s["dne"], e - 1)
                act.activation(hte[r % 2][0:FH, :, :], pD[0:FH, 1, 0:2 * CAP].rearrange("p (k q) -> p k q", k=2),
                               ACT.Copy).then_inc(s["htc"], 1)

            def slot(e, r, more, early=False):
                act.wait_ge(s["gue"], e + 1)
                if not early:
                    act.wait_ge(s["hhe"], e - 1)
                act.activation(the[r % 2][:, :], pA[0:CAP, r % 2, 0:F], ACT.Tanh, scale=0.5).then_inc(s["the"], 1)
                if more:
                    xcopy(e + 1, r + 1)

            xcopy(0, 0)
            slot(0, 0, True, True)
            htcopy(0, 0, True)
            slot(1, 1, True, True)
            gbcopy(0, 0, True)
            htcopy(1, 1, True)
            slot(2, 2, True)
            gbcopy(1, 1, True)
            htcopy(2, 2, False)
            with act.Fori(0, (E - NW) // NW) as k:
                for r in range(NW):
                    e = k * NW + (r + 3)
                    slot(e, r + 3, True)
                    gbcopy(k * NW + (r + 2), r + 2, False)
                    htcopy(e, r + 3, False)
            slot(E - 1, E - 1, False)
            gbcopy(E - 2, E - 2, False)
            htcopy(E - 1, E - 1, False)
            gbcopy(E - 1, E - 1, False)

        @block.vector
        def _(dve):
            dve.wait_ge(s["csil"], 1)
            dve.scalar_tensor_tensor(out=cts[:, :, :], in0=ctt[:, :, :], scalar=1.0, in1=ct[:, :, :], op0=ALU.add,
                                     op1=ALU.mult).then_inc(s["mch"], 1)
            dve.wait_ge(s["mch"], 1)
            dve.tensor_scalar(cts[:, :, :], cts[:, :, :], 0.5, None, ALU.mult).then_inc(s["csil"], 1)
            for k, (src, n, rows, dst) in enumerate(splits):
                dve.wait_ge(s["wsp_h"], k + 1)
                dve.tensor_tensor(wsl[k % 2][0:rows, 0:n], wstage[k % 2][0:rows, 0:n],
                                  wsh[k % 2][0:rows, 0:n].bitcast(F32), ALU.subtract).then_inc(s["wsp_l"], 1)
            dve.wait_ge(s["modc"], 6)
            chain = [1]

            def link(ins):
                chain[0] += 1
                ins.then_inc(s["mch"], 1)
                dve.wait_ge(s["mch"], chain[0])

            for n in (1, 4):
                link(dve.tensor_scalar(modr[:, n, :], modr[:, n, :], 1.0, None, ALU.add))
            for n in (2, 5):
                link(dve.tensor_scalar(modn[:, :], modr[:, n, :], -1.0, None, ALU.mult))
                link(dve.tensor_tensor(modn[:, :], modn[:, :], modr[:, n, :], ALU.max))
                link(dve.tensor_scalar(modn[:, :], modn[:, :], 0.25, None, ALU.max))
                link(dve.tensor_scalar(modr[:, n, :], modr[:, n, :], 0.0, None, ALU.is_ge))
                link(dve.tensor_scalar(modr[:, n, :], modr[:, n, :], 2.0, -1.0, ALU.mult, ALU.add))
                link(dve.tensor_tensor(modr[:, n, :], modr[:, n, :], modn[:, :], ALU.mult))
            dve.drain().then_inc(s["modv"], 1)
            dve.wait_ge(s["cst_v"], 14)
            dve.wait_ge(s["cst"], 80)

            for t in (valt[:, :, :, :], wdn[:, :, :], run_a[:, :]):
                dve.memset(t, 0.0).then_inc(s["key_1st"], 1)
            dve.wait_ge(s["key_1st"], 3)

            def row_stats(link, var_ready, i):
                link(dve.bn_stats(stat[:, i, :], x_rows[:, i, :]))
                link(dve.bn_aggr(mv[:, i, :], stat[:, i, :]))
                dve.tensor_scalar(var[:, i:i + 1], mv[:, i, 1:2], EPS, None, ALU.add).then_inc(var_ready, 1)

            def row_norm(normed, i):
                dve.tensor_scalar(x_rows[:, i, :], x_rows[:, i, :], mv[:, i, 0:1], rstd[:, i:i + 1], ALU.subtract,
                                  ALU.mult).then_inc(normed, 1)

            def extraction(link):
                a, b_ = keys, keys2
                for r in range(ROUNDS):
                    link(dve.max(lb[:, 8 * r:8 * r + 8], a[:, :]))
                    if r + 1 < ROUNDS:
                        link(dve.match_replace(b_[:, :], lb[:, 8 * r:8 * r + 8], a[:, :], 0.0))
                        a, b_ = b_, a
                    yield

            def merge(link):
                a, b_ = run_a, run_b
                for r in range(ROUNDS):
                    link(dve.max(first[:, 8 * r:8 * r + 8], a[:, :]))
                    if r + 1 < ROUNDS:
                        link(dve.match_replace(b_[:, :], first[:, 8 * r:8 * r + 8], a[:, :], 0.0))
                        a, b_ = b_, a

            dve.wait_ge(s["x_1st"], 32)
            for i in range(NT):
                row_stats(link, s["var_1st"], i)
            dve.wait_ge(s["rs_1st"], 1)
            for i in range(NT):
                row_norm(s["xn_1st"], i)

            def body(it):
                n_ch = [0]

                def link(ins):
                    n_ch[0] += 1
                    ins.then_inc(s["vch"], 1)
                    dve.wait_ge(s["vch"], n_ch[0])

                for n in range(2 * KT):
                    h, k = n // KT, n % KT
                    need(dve, "hh", it, n + 1)
                    dve.tensor_tensor(h_lo[:, k, h * 512:h * 512 + 512], wk[:, n % 2, :],
                                      h_hi[:, k, h * 512:h * 512 + 512].bitcast(F32), ALU.subtract).then_inc(s["hl"], 1)
                    if n == KT:
                        need(dve, "vt", it, 1)
                        dve.tensor_copy(keys[:, :], pD[:, 0, :]).then_inc(s["key"], 1)
                def qk_low(u):
                    need(dve, "hi", it, u + 1)
                    dve.tensor_tensor(lo_s[:, u % 2, :], wk[:, u % 2, :], hi_s[:, u % 2, :].bitcast(F32),
                                      ALU.subtract).then_inc(s["lo"], 1)

                def unit_max(g, u):
                    i, kc, j, w = UNITS[u]
                    n = g * DPG + u
                    need(dve, "dq", it, n + 1)
                    x0 = kc * CH - i * P + S - P
                    dve.tensor_tensor_reduce(pD[:, n % 2, 0:w], pD[:, n % 2, 0:w], mask[:, x0:x0 + w], 1.0, -3e38, ALU.add,
                                             ALU.max, mx[:, j, i, kc:kc + 1]).then_inc(s["df"], 1)

                def group_max(g):
                    need(dve, "df", it, g * DPG + NU)
                    link(dve.tensor_tensor(mx[:, :, 4:8, 0], mx[:, :, 4:8, 0], mx[:, :, 4:8, 1], ALU.max))
                    dve.tensor_scalar(negm[:, :].rearrange("p (j i) -> p j i", j=GH), mx[:, :, :, 0], -1.0, None,
                                      ALU.mult).then_inc(s["negm"], 1)
                    if g:
                        for _ in range(ROUNDS // (NG - 1)):
                            next(rounds)
                    n = g * DPG + NU
                    need(dve, "dq", it, n + 1)
                    if g:
                        need(dve, "m", it, 16 * g, per=64)
                    dve.tensor_copy(mrow[:, :], pD[0:GH * NT, n % 2, 0:P]).then_inc(s["df"], 1)

                def sum_step(g, c, step):
                    n = g * NC + c
                    if step == 0:
                        need(dve, "od", it, n + 1)
                        if n:
                            need(dve, "an", it, n)
                    else:
                        dve.wait_ge(s["rch"], 4 * n + step)
                    blk = tmp[:, 0, :].rearrange("p (b r) -> p b r", r=32)
                    if step == 0:
                        ins = dve.transpose(tmp[:, 0, :], od[:, 1, :])
                    elif step == 1:
                        ins = dve.reciprocal(rcol[:, :], blk[:, :, 0])
                    elif step == 2:
                        ins = dve.tensor_copy(blk, rcol[:, :].unsqueeze(2).to_broadcast([P, 16, 32]))
                    else:
                        ins = dve.transpose(tmp[:, 1, :], tmp[:, 0, :])
                    ins.then_inc(s["rch"], 1)

                def out_high(g, c):
                    need(dve, "an", it, g * NC + c + 1)
                    dve.tensor_copy(h_hi[:, g, c * CH:(c + 1) * CH], od[:, 0, :]).then_inc(s["ah"], 1)

                for u in range(QK_FIRST):
                    qk_low(u)
                for i in range(NT):
                    for k in beside(i):
                        unit_max(0, k)
                    need(dve, "vp", it, i + 1)
                    dve.tensor_tensor(v_rows[:, i, :], pC[:, i % 2, :], bv_b[:, :], ALU.add).then_inc(s["vr"], 1)
                for u in range(QK_FIRST, 16):
                    ks = beside(NT + u - QK_FIRST)
                    for k in ks:
                        unit_max(0, k)
                        if k == ks[0] and u > QK_FIRST:
                            qk_low(u - 1)
                qk_low(15)
                rounds = extraction(link)
                group_max(0)
                need(dve, "key", it, 1)
                need(dve, "lo", it, 16)
                mid = sum(SHARE[:6])
                for g in range(NG):
                    if g + 1 < NG:
                        for u in range(NU):
                            unit_max(g + 1, u)
                            if g:
                                if u in (2, 4, 6, 8):
                                    sum_step(g - 1, 1, u // 2 - 1)
                                if u == 14:
                                    out_high(g - 1, 1)
                            if u - mid in (0, 2, 4, 6):
                                sum_step(g, 0, (u - mid) // 2)
                            if u - mid == 12:
                                out_high(g, 0)
                        group_max(g + 1)
                        if g + 2 == NG:
                            dve.tensor_copy(run_a[:, CAP:2 * CAP], lb[0:E, :]).then_inc(s["lbd"], 1)
                    else:

                        def norm_chunk(gg, c):
                            for step in range(4):
                                sum_step(gg, c, step)
                            out_high(gg, c)

                        norm_chunk(g - 1, 1)
                        for i in range(NT):
                            if i % 4 == 0:
                                dve.wait_ge(s_x[i // 4], 16)
                            row_stats(link, s["var"], i)
                        need(dve, "rs", it, 1)
                        for i in range(NT):
                            row_norm(s["xn"], i)
                        norm_chunk(g, 0)
                        need(dve, "up", it, 16)
                        merge(link)
                        dve.tensor_copy(run_a[:, 0:CAP], first[:, :]).then_inc(s["lst"], 1)
                        norm_chunk(g, 1)

                def tile_sum(i):
                    need(dve, "op", it, i + 1)
                    if i == 0:
                        need(dve, "mod", it, 16 * 5)
                    dve.tensor_tensor(tmp[:, 0, :], AD[i // 2 % 2][:, i % 2, :], ga[:, :], ALU.mult).then_inc(s["of"], 1)
                    need(dve, "of", it, i + 1)
                    need(dve, "xg", it, i + 1)
                    dve.tensor_tensor(x2_rows[:, i, :], tmp[:, 0, :], od[:, (i + 1) % 2, :], ALU.add).then_inc(s["x2"], 1)
                    need(dve, "x2", it, i + 1)
                    link(dve.bn_stats(stat[:, i, :], x2_rows[:, i, :]))
                    link(dve.bn_aggr(mv[:, i, :], stat[:, i, :]))
                    dve.tensor_scalar(var[:, i:i + 1], mv[:, i, 1:2], EPS, None, ALU.add).then_inc(s["var"], 1)

                def tile_norm(i):
                    need(dve, "rs", it, i + 2)
                    if i:
                        need(dve, "h2", it, i)
                    link(dve.tensor_scalar(tmp[:, 1, :], x2_rows[:, i, :], mv[:, i, 0:1], rstd[:, i:i + 1],
                                           ALU.subtract, ALU.mult))
                    link(dve.tensor_tensor(tmp[:, 1, :], tmp[:, 1, :], cb1[:, :], ALU.mult))
                    if i >= 2:
                        dve.wait_ge(s_hw[i % 2], 16 * (i // 2))
                        need(dve, "tr", it, i - 1)
                    else:
                        dve.wait_ge(s_qkw[i % 2], 256)
                    dve.tensor_tensor(h2b[:, i % 2, :], tmp[:, 1, :], sbm[:, :], ALU.add).then_inc(s["h2"], 1)

                for i in range(NT + 1):
                    if i < NT:
                        tile_sum(i)
                    if i:
                        tile_norm(i - 1)
                def router():
                    need(dve, "th", it, NT)
                    link(dve.tensor_scalar(sc[:, :, :], th[:, :, :], 0.5, 0.5, ALU.mult, ALU.add))
                    yield
                    link(dve.tensor_tensor(sb_[:, :, :], sc[:, :, :], bias_b[:, :].unsqueeze(1).to_broadcast([P, NT, E]), ALU.add))
                    yield
                    g8 = sb_[:, :, :].rearrange("p i (g e) -> p (i g) e", e=GSIZE)
                    dve.tensor_tensor(ta[:, :, :], g8[:, :, 0:4], g8[:, :, 4:8], ALU.max)
                    link(dve.tensor_tensor(tb[:, :, :], g8[:, :, 0:4], g8[:, :, 4:8], ALU.min))
                    yield
                    hi_, lo_ = ta, tb
                    for wd_, (o1, o2, o3, o4) in ((2, (tc_, td, te, tf)), (1, (ta, tb, ta, tb))):
                        a0, a1 = hi_[:, :, 0:wd_], hi_[:, :, wd_:2 * wd_]
                        b0, b1 = lo_[:, :, 0:wd_], lo_[:, :, wd_:2 * wd_]
                        r1 = o1[:, :, 0:wd_]
                        r2 = o2[:, :, 0:wd_]
                        r3 = o3[:, :, 0:wd_] if wd_ == 2 else ta[:, :, 2:3]
                        r4 = o4[:, :, 0:wd_] if wd_ == 2 else tb[:, :, 2:3]
                        dve.tensor_tensor(r1, a0, a1, ALU.max)
                        dve.tensor_tensor(r2, a0, a1, ALU.min)
                        link(dve.tensor_tensor(r3, b0, b1, ALU.max))
                        yield
                        link(dve.tensor_tensor(r4, r2, r3, ALU.max))
                        yield
                        hi_, lo_ = (o1, tf) if wd_ == 2 else (ta[:, :, 0:1], tb[:, :, 2:3])
                    link(dve.tensor_tensor(gsum[:, :, :].rearrange("p i (g o) -> p (i g) o", o=1), hi_, lo_, ALU.add))
                    yield
                    other = gsum[:, :, :].unsqueeze(2).to_broadcast([P, NT, GROUPS, GROUPS])
                    own = gsum[:, :, :].unsqueeze(3).to_broadcast([P, NT, GROUPS, GROUPS])
                    tri_b = tri[:, :].rearrange("p (g h) -> p g h", g=GROUPS).unsqueeze(1).to_broadcast([P, NT, GROUPS, GROUPS])
                    dve.tensor_tensor(cmp[:, :, :, :], other, own, ALU.is_gt)
                    link(dve.tensor_tensor(ceq[:, :, :, :], other, own, ALU.is_equal))
                    yield
                    link(dve.tensor_tensor(ceq[:, :, :, :], ceq[:, :, :, :], tri_b, ALU.mult))
                    yield
                    link(dve.tensor_tensor(cmp[:, :, :, :], cmp[:, :, :, :], ceq[:, :, :, :], ALU.add))
                    yield
                    link(dve.tensor_reduce(gcnt[:, :, :], cmp[:, :, :, :], AX_X, ALU.add))
                    yield
                    link(dve.tensor_scalar(gsel[:, :, :], gcnt[:, :, :], KGROUPS - 0.5, None, ALU.is_lt))
                    yield
                    link(dve.tensor_scalar(gpen[:, :, :], gsel[:, :, :], BIG, -BIG, ALU.mult, ALU.add))
                    yield
                    ge = "p i (g e) -> p i g e"
                    wide = [P, NT, GROUPS, GSIZE]
                    link(dve.tensor_tensor(wdn[:, :, :].rearrange(ge, e=GSIZE), sb_[:, :, :].rearrange(ge, e=GSIZE),
                                           gpen[:, :, :].unsqueeze(3).to_broadcast(wide), ALU.add))
                    yield
                    for i in range(NT):
                        last = dve.max(v8[:, i, :], wdn[:, i, :])
                    link(last)
                    yield
                    link(dve.memset(v8[:, :, TOPK:8], -BIG))
                    yield
                    for i in range(NT):
                        last = dve.match_replace(rep[:, i, :], v8[:, i, :], wdn[:, i, :], BIG)
                    link(last)
                    yield
                    link(dve.scalar_tensor_tensor(out=sel[:, :, :].rearrange(ge, e=GSIZE), in0=rep[:, :, :].rearrange(ge, e=GSIZE),
                                                  scalar=BIG, in1=gsel[:, :, :].unsqueeze(3).to_broadcast(wide),
                                                  op0=ALU.is_equal, op1=ALU.mult))
                    yield
                    link(dve.tensor_tensor(sc[:, :, :], sel[:, :, :], sc[:, :, :], ALU.mult))
                    yield
                    link(dve.tensor_reduce(wsum[:, :], sc[:, :, :], AX_X, ALU.add))
                    yield
                    link(dve.reciprocal(rws[:, :], wsum[:, :]))
                    yield
                    link(dve.tensor_tensor(valt[:, :, :, :].rearrange("p q h e -> p h q e"),
                                           sel[:, :, :].rearrange("p (h q) e -> p h q e", h=2),
                                           tokn[:, :].rearrange("p (h q) -> p h q", h=2).unsqueeze(3).to_broadcast([P, 2, 4, E]),
                                           ALU.mult))
                    yield
                    dve.scalar_tensor_tensor(out=wdn[:, :, :], in0=sc[:, :, :], scalar=ROUTE_SCALE,
                                             in1=rws[:, :].unsqueeze(2).to_broadcast([P, NT, E]), op0=ALU.mult,
                                             op1=ALU.mult).then_inc(s["val"], 1)
                    dve.tensor_scalar(tokn[:, :], tokn[:, :], -float(S), None, ALU.add)

                pieces = router()

                def pump(n):
                    for _ in range(n):
                        next(pieces, None)

                pump(13)
                for w in range(4):
                    c, fh = w // 2, w % 2
                    need(dve, "tg", it, w + 1)
                    if w:
                        need(dve, "hs", it, w)
                    link(dve.scalar_tensor_tensor(out=tmp[0:FH, 0, :], in0=wk[0:FH, w % 2, :], scalar=1.0,
                                                  in1=pA[0:FH, w % 2, :], op0=ALU.add, op1=ALU.mult))
                    link(dve.scalar_tensor_tensor(out=tmp[0:FH, 1, :], in0=tmp[0:FH, 0, :], scalar=0.5,
                                                  in1=pB[0:FH, w % 2, :], op0=ALU.mult, op1=ALU.mult))
                    hi = hs[0][:, fh, c * CH:(c + 1) * CH]
                    link(dve.tensor_copy(hi, tmp[0:FH, 1, :]))
                    dve.tensor_tensor(hs[1][:, fh, c * CH:(c + 1) * CH], tmp[0:FH, 1, :], hi.bitcast(F32),
                                      ALU.subtract).then_inc(s["hs"], 1)
                    pump((3, 3, 1, 0)[w])
                need(dve, "hs", it, 4)
                for i in range(NT):
                    need(dve, "dn", it, i + 1)
                    if i >= 2:
                        need(dve, "pre", it, i - 1)
                    dve.tensor_tensor(tmp[:, i % 2, :], pC[:, i % 2, :], gb[:, :], ALU.mult).then_inc(s["sg"], 1)
                    pump(1)
                for _ in pieces:
                    pass

                end_of_batch(dve, "dve")

            batches(dve, body)

            dve.wait_ge(s["vt_last"], 1)
            link(dve.tensor_copy(keys[:, :], pD[:, 0, :]))
            for _ in extraction(link):
                pass
            dve.tensor_copy(run_a[:, CAP:2 * CAP], lb[0:E, :]).then_inc(s["lb_last"], 1)
            dve.wait_ge(s["fgb"], 16)
            link(dve.tensor_copy(gbp[0][:, :], gbr[:, :]))
            link(dve.tensor_tensor(gbq[0][:, :], gbr[:, :], gbp[0][:, :], ALU.subtract))
            link(dve.tensor_copy(gbp[1][:, :], gbq[0][:, :]))
            link(dve.tensor_tensor(gbq[1][:, :], gbq[0][:, :], gbp[1][:, :], ALU.subtract))
            link(dve.tensor_copy(gbp[2][:, :], gbq[1][:, :]))
            dve.wait_ge(s["mrg"], 16)
            merge(link)
            link(dve.scalar_tensor_tensor(out=fz[:, :], in0=first[:, :], scalar=0.0, in1=slots_f[0:E, :], op0=ALU.is_equal,
                                          op1=ALU.mult))
            link(dve.tensor_scalar(idf[:, :], first[:, :], -1.0, float(T), ALU.mult, ALU.add))
            dve.tensor_tensor(idf[:, :], idf[:, :], fz[:, :], ALU.add).then_inc(s["idt"], 1)
            dve.wait_ge(s["vt_last"], 2)
            dve.tensor_copy(idu[:, :], pA[0:CAP, 0, 0:E]).then_inc(s["idt"], 1)
            for b in range(B):
                link(dve.tensor_scalar(oge[:, :], idf[:, :], float(b * S), None, ALU.is_ge))
                link(dve.scalar_tensor_tensor(out=ohb[b][:, :], in0=idf[:, :], scalar=float(b * S + S), in1=oge[:, :],
                                              op0=ALU.is_lt, op1=ALU.mult))
            dve.drain().then_inc(s["idx"], 1)
            dve.wait_ge(s["g12"], 16 * 15)

            def ohcopy(e, r, early):
                if not early:
                    dve.wait_ge(s["gbm"], e - 1)
                dve.tensor_copy(ohc[r % 2][:, :], oh[:, bass.ds(e * CAP, CAP)]).then_inc(s["oc"], 1)

            def gated(e, r, early):
                dve.wait_ge(s["the"], e + 1)
                if not early:
                    dve.wait_ge(s["hte"], e - 1)
                dve.scalar_tensor_tensor(out=hae[r % 2][:, :], in0=the[r % 2][:, :], scalar=1.0, in1=pA[0:CAP, r % 2, 0:F],
                                         op0=ALU.add, op1=ALU.mult).then_inc(s["ech"], 1)
                dve.wait_ge(s["ech"], e + 1)
                dve.scalar_tensor_tensor(out=hhe[r % 2][:, :], in0=hae[r % 2][:, :], scalar=0.5,
                                         in1=pA[0:CAP, r % 2, F:2 * F], op0=ALU.mult, op1=ALU.mult).then_inc(s["hhe"], 1)

            def weighted(e, r, early):
                dve.wait_ge(s["dne"], e + 1)
                dve.wait_ge(s["gbs"], e + 1)
                if not early:
                    dve.wait_ge(s["sc"], (e - 1) * 16)
                dve.scalar_tensor_tensor(out=ye[r % 2][:, :], in0=pC[0:CAP, r % 2, :], scalar=gath[r % 4][:, bass.ds(e + D, 1)],
                                         in1=gbs[r % 2][:, :], op0=ALU.mult, op1=ALU.mult).then_inc(s["ye"], 1)

            for e in range(3):
                ohcopy(e, e, e < 2)
                gated(e, e, e < 2)
                if e:
                    weighted(e - 1, e - 1, True)
            with dve.Fori(0, (E - NW) // NW) as k:
                for r in range(NW):
                    e = k * NW + (r + 3)
                    ohcopy(e, r + 3, False)
                    gated(e, r + 3, False)
                    weighted(k * NW + (r + 2), r + 2, False)
            ohcopy(E - 1, E - 1, False)
            gated(E - 1, E - 1, False)
            weighted(E - 2, E - 2, False)
            weighted(E - 1, E - 1, False)

        @block.tensor
        def _(pe):
            pe.wait_ge(s["csil"], 2)
            for n in range(6):
                if n >= 4:
                    pe.wait_ge(s["modc"], n - 3)
                for k in range(KT):
                    last = pe.matmul(AB[n // 2 % 2][0:B, n % 2, :], cts[:, k, :], wm[:, k, n * D:(n + 1) * D], start=k == 0,
                                     stop=k == KT - 1)
                last.then_inc(s["modm"], 1)
            pe.wait_ge(s["cst_v"], 14)
            pe.wait_ge(s["modc"], 6)

            def split_mm(dst, lhs, rhs, n, between=()):
                terms = [(k, a, b) for k in range(n) for a, b in ((0, 0), (1, 0), (0, 1))]
                for t, (k, a, b) in enumerate(terms):
                    if t % 2 and t // 2 < len(between):
                        between[t // 2]()
                    last = pe.matmul(dst, lhs(a, k), rhs(b, k), start=t == 0, stop=t == len(terms) - 1)
                return last

            hT = (h_hi, h_lo)
            pe.wait_ge(s["xn_1st"], NT)
            pe.wait_ge(s["key_1st"], 3)
            pe.wait_ge(s["wq_1st"], 32)

            def turn_keys(turned):
                for q in range(4):
                    last = pe.transpose(pD[:, 0, q * P:q * P + P], valt[:, q, :, :].rearrange("p h e -> p (h e)"), ident[:, :])
                last.then_inc(turned, 1)

            def body(it):
                for n in range(2 * KT):
                    h, k = n // KT, n % KT
                    if h:
                        need(pe, "hh", it, k + 1)
                    for i in range(4):
                        last = pe.transpose(AB[k // 2][:, k % 2, i * P:i * P + P], x_rows[:, 4 * h + i, k * P:k * P + P],
                                            ident[:, :])
                    last.then_inc(s["xt"], 1)
                    if n == KT - 1:
                        turn_keys(s["vt"])
                def qk_unit(u, between=()):
                    m, t, c = u // 4, u // 2 % 2, u % 2
                    w = (wq, wk_)[t]
                    if u < 2:
                        need(pe, "hl", it, (u + 1) * KT)
                    if u == 2:
                        pe.wait_ge(s["wqk"], 32)
                    if u in (QK_FIRST, QK_FIRST + 1):
                        need(pe, "vr", it, NT - 1 + u - QK_FIRST)
                    elif u >= 2:
                        need(pe, "hi", it, u - 1)
                    split_mm(pC[:, u % 2, :], lambda a, k: w[a][:, k, m * P:m * P + P],
                             lambda b, k: hT[b][:, k, c * CH:(c + 1) * CH], KT, between).then_inc(s["qk"], 1)

                def unit(g, u):
                    i, kc, j, w = UNITS[u]
                    n = g * DPG + u
                    if u == 0:
                        pe.wait_ge(s_stk[g % 3], 128 * (g // 3 + 1))
                    if n >= 2:
                        need(pe, "df", it, n - 1)
                    elif n == 0:
                        need(pe, "key", it, 1)
                    pe.matmul(pD[:, n % 2, 0:w], q_stk[g % 3][0:STK, j, i * P:i * P + P],
                              k_stk[g % 3][0:STK, j, kc * CH:kc * CH + w], start=True, stop=True).then_inc(s["dq"], 1)

                def turn_max(g):
                    n = g * DPG + NU
                    need(pe, "negm", it, g + 1)
                    pe.transpose(pD[0:GH * NT, n % 2, 0:P], negm[:, :], ident[:, :]).then_inc(s["dq"], 1)

                def scores(g, st, more_units):
                    c, kt, q0 = STEPS[st]
                    if st == 0:
                        pe.wait_ge(s["m"], 16 * (g + 1))
                    for hp in range(2):
                        v = 2 * (g * NS + st) + hp
                        if v >= 2:
                            need(pe, "ex", it, v - 1)
                        for t in range(2):
                            j = 2 * hp + t
                            last = pe.matmul(AB[v % 2][:, t, q0:CH], k_stk[g % 3][0:STK, j, kt * P:kt * P + P],
                                             q_stk[g % 3][0:STK, j, c * CH + q0:(c + 1) * CH], start=True, stop=True,
                                             skip_group_check=True)
                            if kt * P >= c * CH:
                                last = pe.matmul(AB[v % 2][:, t, q0:q0 + P], ident_b[:, :], mask_t[:, :], start=False,
                                                 stop=True, skip_group_check=True)
                        last.then_inc(s["st"], 1)
                        more_units(hp + 1)

                def values(g, st, more_units):
                    c, kt, q0 = STEPS[st]
                    need(pe, "ex", it, 2 * (g * NS + st) + 2)
                    if kt == 0 and g * NC + c >= 1:
                        need(pe, "od", it, g * NC + c)
                    first, final = kt == 0, kt == (c + 1) * CH // P - 1
                    for bank in range(2):
                        for j in range(GH):
                            h = GH * g + j
                            lhs = v_rows[:, kt, h * DH:(h + 1) * DH] if bank == 0 else ones[:, :]
                            last = pe.matmul(pC[j * DH:(j + 1) * DH, bank, q0:CH], lhs, p_buf[:, st % 2, j, q0:CH],
                                             start=first, stop=final, skip_group_check=True)
                        if bank == 0:
                            more_units(3)
                    last.then_inc(s["pv"], 1)

                def units_beside(n):
                    return [lambda k=k: unit(0, k) for k in beside(n)]

                for u in range(QK_FIRST):
                    qk_unit(u)
                pe.wait_ge(s["wv"], 32)
                for i in range(NT):
                    if i < 2:
                        need(pe, "hi", it, QK_FIRST - 1 + i)
                    else:
                        need(pe, "vr", it, i - 1)
                    split_mm(pC[:, i % 2, :], lambda a, k: hT[a][:, k, i * P:i * P + P], lambda b, k: wv[b][:, k, :],
                             KT, units_beside(i)).then_inc(s["vp"], 1)
                for u in range(QK_FIRST, 16):
                    qk_unit(u, units_beside(NT + u - QK_FIRST))
                turn_max(0)
                need(pe, "vr", it, NT)
                need(pe, "hi", it, 16)
                for g in range(NG):
                    done = [0]
                    for st in range(NS):
                        n = SHARE[st] if g + 1 < NG else 0

                        def more_units(slot, n=n, st=st, g=g, done=done):
                            upto = sum(SHARE[:st]) + (n if st == 0 else -(-n * (slot + 1) // 4)) if n else 0
                            while done[0] < upto:
                                unit(g + 1, done[0])
                                done[0] += 1

                        more_units(0)
                        scores(g, st, more_units)
                        if st == NS - 1 and g + 1 < NG:
                            more_units(3)
                            turn_max(g + 1)
                        if st:
                            values(g, st - 1, more_units)
                    values(g, NS - 1, lambda slot: None)

                pe.wait_ge(s["wo"], 64)
                need(pe, "ex", it, 2 * NG * NS)

                def project(i):
                    need(pe, "at", it, NG * NC - (1 if i < NT // NC else 0))
                    if i >= 4:
                        need(pe, "of", it, i - 3)
                    split_mm(AD[i // 2 % 2][:, i % 2, :], lambda a, k: hT[a][:, k, i * P:i * P + P], lambda b, k: wo[b][:, k, :],
                             KT).then_inc(s["op"], 1)

                def turn(i):
                    need(pe, "h2", it, i + 1)
                    if i >= 2:
                        need(pe, "h2h", it, i - 1)
                    for k in range(KT):
                        last = pe.transpose(pB[:, i % 2, k * P:k * P + P], h2b[:, i % 2, k * P:k * P + P], ident[:, :])
                    last.then_inc(s["tr"], 1)

                def logits(i):
                    need(pe, "wk", it, i + 1)
                    if i >= 2:
                        need(pe, "th", it, i - 1)
                    for k in range(KT):
                        last = pe.matmul(pC[:, i % 2, 0:E], wk[:, i % 2, k * P:k * P + P], gw[:, k, :], start=k == 0,
                                         stop=k == KT - 1)
                    last.then_inc(s["lg"], 1)

                for i in range(3):
                    project(i)
                for i in range(NT):
                    if i + 3 < NT:
                        project(i + 3)
                    turn(i)
                    logits(i)
                need(pe, "h2l", it, NT)
                need(pe, "th", it, NT)
                for w in range(4):
                    c, fh = w // 2, w % 2
                    if w >= 2:
                        need(pe, "hs", it, w - 1)
                    for dst, off in ((pA, 0), (pB, F)):
                        last = split_mm(dst[0:FH, w % 2, :], lambda a, k: wsg[a][:, k, off + fh * FH:off + fh * FH + FH],
                                        lambda b, k: hT[b][:, k, c * CH:(c + 1) * CH], KT)
                    last.then_inc(s["gu"], 1)
                pe.wait_ge(s["wsd"], 32)
                for i in range(NT):
                    need(pe, "hs", it, 2 if i < 4 else 4)
                    if i >= 2:
                        need(pe, "sg", it, i - 1)
                    split_mm(pC[:, i % 2, :], lambda a, k: hs[a][:, k, i * P:i * P + P], lambda b, k: wsd[b][:, k, :],
                             2).then_inc(s["dn"], 1)
                end_of_batch(pe, "pe")

            batches(pe, body)

            turn_keys(s["vt_last"])
            pe.wait_ge(s["idt"], 1)
            pe.transpose(pA[0:CAP, 0, 0:E], idf[:, :], ident[0:E, 0:E]).then_inc(s["vt_last"], 1)
            pe.wait_ge(s["idt"], 2)

            def turn_x(e, r, uses):
                pe.wait_ge(s_ga[r % 4], uses)
                for k in range(KT):
                    last = pe.transpose(pB[:, r % 2, k * CAP:(k + 1) * CAP], gath[r % 4][:, k * P:k * P + P],
                                        ident[0:CAP, 0:CAP])
                last.then_inc(s["xte"], 1)

            def gate_up(e, r, uses):
                pe.wait_ge(s["gte"], e + 1)
                pe.wait_ge(s_we[r % 4], uses)
                for k in range(KT):
                    last = pe.matmul(pA[0:CAP, r % 2, 0:2 * F], gt[r % 2][:, k, :], weg[r % 4][:, k, :], start=k == 0,
                                     stop=k == KT - 1)
                last.then_inc(s["gue"], 1)

            def down(e, r, early):
                pe.wait_ge(s["htc"], e + 1)
                if not early:
                    pe.wait_ge(s["ye"], e - 1)
                for k in range(2):
                    last = pe.matmul(pC[0:CAP, r % 2, :], hte[r % 2][:, k, :], wed[r % 4][:, k, :], start=k == 0, stop=k == 1)
                last.then_inc(s["dne"], 1)
                pe.wait_ge(s["oc"], e + 1)
                if not (early and r == 0):
                    pe.wait_ge(s["gbs"], e)
                pe.matmul(pD[0:CAP, 0, :], ohc[r % 2][:, :], gb12[:, :], start=True, stop=True).then_inc(s["gbm"], 1)

            def turn_h(e, r, first):
                pe.wait_ge(s["hhe"], e + 1)
                if not first:
                    pe.wait_ge(s["htc"], e)
                for k in range(2):
                    last = pe.transpose(pD[0:FH, 1, k * CAP:(k + 1) * CAP], hhe[r % 2][:, k * FH:(k + 1) * FH],
                                        ident[0:CAP, 0:CAP])
                last.then_inc(s["hte"], 1)

            pe.wait_ge(s["ez"], NW + 2)
            turn_x(0, 0, 16)
            for e in range(3):
                gate_up(e, e, 32)
                turn_x(e + 1, e + 1, 16)
                if e:
                    down(e - 1, e - 1, True)
                turn_h(e, e, e == 0)
            with pe.Fori(0, (E - NW) // NW) as k:
                for r in range(NW):
                    e = k * NW + (r + 3)
                    gate_up(e, r + 3, k * 32 + 32 * ((r + 3) // 4 + 1))
                    turn_x(k * NW + (r + 4), r + 4, k * 16 + 16 * ((r + 4) // 4 + 1))
                    down(k * NW + (r + 2), r + 2, False)
                    turn_h(e, r + 3, False)
            gate_up(E - 1, E - 1, 32 * (E // 4))
            down(E - 2, E - 2, False)
            turn_h(E - 1, E - 1, False)
            down(E - 1, E - 1, False)


def _tiles(a):
    import numpy as np
    k = a.shape[-2] // P
    a = a.reshape(*a.shape[:-2], k, P, a.shape[-1])
    return np.ascontiguousarray(np.moveaxis(a, -3, -2))


def kernel(**inputs):
    import numpy as np
    import concourse.bacc as bacc
    from concourse.bass_utils import run_bass_kernel_spmd as run

    g = {k: np.asarray(v) for k, v in inputs.items()}
    w = {k[7:]: v for k, v in g.items() if k.startswith("L0_ffn_")}
    gate_up = np.concatenate([w["w_gate"], w["w_up"]], axis=-1)
    shared = np.concatenate([w["ws_gate"], w["ws_up"]], axis=-1)
    arrays = {
        "x": np.ascontiguousarray(g["L0_attn_X"].reshape(T, D)),
        "wqkvo": np.stack([_tiles(g["L0_attn_" + n].T).reshape(P, KT * D) for n in ("Wq", "Wk", "Wv", "Wo")]),
        "bq": g["L0_attn_bq"].reshape(KT, P).T, "bk": g["L0_attn_bk"].reshape(KT, P).T, "bv": g["L0_attn_bv"], "bo": g["L0_attn_bo"],
        "gate_w": _tiles(w["gate_w"]),
        "bias": w["bias"],
        "w_gu": _tiles(gate_up),
        "w_dn": np.ascontiguousarray(np.moveaxis(w["w_down"].reshape(E, 2, FH, D), 1, 2)),
        "ws_gu": _tiles(shared).reshape(P, KT * 2 * F),
        "ws_dn": np.ascontiguousarray(np.moveaxis(w["ws_down"].reshape(2, FH, D), 0, 1)).reshape(FH, 2 * D),
        "c_t": _tiles(g["L0_c"].T),
        "wmod": _tiles(g["L0_wmod"]),
    }
    nc = bacc.Bacc("TRN2", target_bir_lowering=False, num_devices=1)
    args = []
    feed = {}
    for name, a in arrays.items():
        a = np.ascontiguousarray(a)
        feed["in_" + name] = a
        args.append(nc.dram_tensor("in_" + name, a.shape, mybir.dt.from_np(a.dtype), kind="ExternalInput").ap())
    out = nc.dram_tensor("out_0", (T + CAP, D), F32, kind="ExternalOutput").ap()
    build(nc, *args, out)
    r = run(nc, [feed], core_ids=[0])
    return r.results[0]["out_0"][:T].reshape(B, S, D)
```

```python
from contextlib import ExitStack

import concourse.bass as bass
from concourse import mybir

ALU = mybir.AluOpType
ACT = mybir.ActivationFunctionType
AX_X = mybir.AxisListType.X
F32 = mybir.dt.float32
F32R = mybir.dt.float32r
BF16 = mybir.dt.bfloat16
U32 = mybir.dt.uint32

P = 128
B, S, D = 4, 1024, 512
T = B * S
HEADS, DH = 16, 32
KT = D // P
NT = S // P
CH = 512
NC = S // CH
GH = P // DH
NG = HEADS // GH
E, TOPK, F = 64, 6, 192
FH = F // 2
GROUPS, GSIZE, KGROUPS = 8, 8, 4
CAP = 2 * (2 * 256 * TOPK // E)
ROUNDS = CAP // 8
EPS = 1e-5
QSCALE = float(DH) ** -0.25
ROUTE_SCALE = 2.5
BIG = 1e30
KiB = 1024
STK = 3 * DH + 1


def chunk_steps():
    return [(c, kt, max(0, kt * P - c * CH)) for c in range(NC) for kt in range((c + 1) * CH // P)]


def max_units():
    return [(i, kc, j, min(CH, (i + 1) * P - kc * CH))
            for i in reversed(range(NT)) for kc in range(i * P // CH + 1) for j in range(GH)]


STEPS = chunk_steps()
UNITS = max_units()
NS, NU = len(STEPS), len(UNITS)
DPG = NU + 1


def qk_part(u):
    if u < 4:
        return u % 2, 0, u // 2
    return (u // 2 % 2, 1, u % 2) if u < 8 else (u // 4, u // 2 % 2, u % 2)


def share_units():
    unit_time = [w + 48 for _, _, _, w in UNITS]
    step_time = [CH - q0 + 350 for _, _, q0 in STEPS]
    out, at = [], 0
    for n in range(NS):
        upto = min(1.0, AHEAD * sum(step_time[:n + 1]) / sum(step_time))
        first = at
        while at < NU and sum(unit_time[:at]) < upto * sum(unit_time):
            at += 1
        out.append(at - first)
    out[-1] += NU - at
    return out


AHEAD = 1.3
EARLY = 1
PARTS = (0.2, 0.4, 0.8)
SHARE = share_units()
TURN = min(NS - 1, 1 + max(n for n in range(NS) if SHARE[n]))
PRE_POOL = NT - 2
QK_FIRST = 8
V_ALONE = 5


def beside(n):
    slots = NT + 16 - QK_FIRST - V_ALONE
    n -= V_ALONE
    return list(range(NU * n // slots, NU * (n + 1) // slots)) if n >= 0 else []

BATCH_SIGNALS = {
    "xn": "rows of the next batch normed",
    "xt": "normed rows turned (PSUM)",
    "hh": "high part of the modulated, turned rows",
    "hl": "their low part",
    "vp": "value tile multiplied",
    "vr": "value tile in SBUF",
    "qk": "unit of queries/keys multiplied",
    "hi": "its high part",
    "lo": "its low part",
    "dq": "first-pass unit (or turned maxima) in PSUM",
    "df": "its maxima taken (or the turned maxima copied)",
    "negm": "a group's negated maxima",
    "st": "scores of a head's step in PSUM",
    "ex": "their exponentials",
    "pv": "values and sums of a step accumulated",
    "od": "outputs and sums of a chunk in SBUF",
    "rch": "steps towards 1/sum",
    "an": "outputs of a chunk normed",
    "ah": "their high part",
    "at": "their low part",
    "of": "output projection times ga",
    "x2": "x + attention of a tile",
    "op": "output projection of a tile",
    "xg": "x + ga * bo of a tile",
    "var": "variance of a tile",
    "rs": "1/deviation",
    "h2": "second normed, modulated rows",
    "tr": "those rows turned (PSUM)",
    "wk": "turned rows in SBUF",
    "h2h": "their high part",
    "h2l": "their low part",
    "lg": "router logits",
    "th": "their tanh",
    "gu": "shared gate and up products",
    "tg": "tanh of the gate",
    "hs": "shared hidden rows, both parts",
    "dn": "shared down products",
    "pre": "rows without the routed experts (GpSimd's tiles)",
    "val": "keys and dense weights of the router",
    "vt": "keys turned (PSUM)",
    "lst": "running lists merged",
    "vch": "links of VectorE's chain",
    "x0": "x, first half, loaded",
    "x1": "x, second half, loaded",
    "mod": "modulation rows loaded",
    "wv": "value weights loaded",
    "wqk": "key weights loaded",
    "qkw0": "even units in DRAM",
    "qkw1": "odd units in DRAM",
    "stk0": "stacks in buffer 0 loaded",
    "stk1": "in buffer 1",
    "stk2": "in buffer 2",
    "m": "shift row of a group in place",
    "col": "next modulation columns loaded",
    "wq": "next query weights loaded",
    "up": "upper half's lists moved",
    "lbd": "lists of the batch before",
    "key": "keys in SBUF",
    "sg": "gb * shared experts",
    "wo": "output and shared gate/up weights loaded",
    "wsd": "shared down weights loaded",
    "xi0": "x of an even tile loaded",
    "xi1": "of an odd one",
    "hw0": "h2 of an even tile in DRAM",
    "hw1": "of an odd one",
    "ww": "dense weights in DRAM",
    "gabo": "ga * bo ready",
    "landed": "last batch's rows in DRAM",
    "prv": "the same (VectorE's tiles)",
}

OTHER_SIGNALS = {
    "ld": "inputs of the modulation loaded",
    "csil": "its silu; scaled biases",
    "modm": "a sixth of the modulation (PSUM)",
    "modc": "the same in SBUF",
    "modv": "modulation rows ready",
    "mw": "modulation rows in DRAM",
    "wst0": "weight in staging buffer 0",
    "wst1": "in buffer 1",
    "wsp_h": "high part of a weight",
    "wsp_l": "its low part",
    "wwr0": "split weight of buffer 0 in DRAM",
    "wwr1": "of buffer 1",
    "cst": "bias vectors loaded",
    "cst_v": "masks and constants set",
    "zr": "zero rows and rows of ones set",
    "pre_idx": "those in DRAM",
    "x_1st": "batch 0: x loaded",
    "var_1st": "variances",
    "rs_1st": "1/deviations",
    "xn_1st": "normed rows",
    "col_1st": "modulation columns",
    "wq_1st": "query weights",
    "key_1st": "empty router state",
    "pw0": "rows without the routed experts in DRAM, by buffer",
    "pw1": "",
    "pw2": "",
    "pw3": "",
    "end": "engines done with a batch",
    "cleared": "engines that cleared their signals",
    "go_sp": "clear your signals",
    "go_act": "",
    "go_dve": "",
    "go_pe": "",
    "on_sp": "go on with the next batch",
    "on_act": "",
    "on_dve": "",
    "on_pe": "",
    "val_last": "after the last batch: keys and dense weights",
    "vt_last": "turned keys, then turned indices",
    "w_last": "dense weights in DRAM",
    "lb_last": "lists of the last batch",
    "mrg": "upper half's lists moved",
    "fgb": "gb rows loaded",
    "mch": "links of VectorE's chain",
    "idt": "table of token indices: turned way, then by slot",
    "idx": "one-hot rows and gb's parts",
    "g12": "those side by side",
    "ez": "zero rows of the down products",
    "we0": "gate/up weights of an expert loaded, by buffer",
    "we1": "",
    "we2": "",
    "we3": "",
    "wd0": "down weights, by buffer",
    "wd1": "",
    "wd2": "",
    "wd3": "",
    "ga0": "an expert's rows gathered, by buffer",
    "ga1": "",
    "ga2": "",
    "ga3": "",
    "ic": "index column for the gather",
    "pas": "passes of GpSimd",
    "xte": "rows turned (PSUM)",
    "gte": "their high part",
    "gtl": "their low part",
    "wgh": "high part of gate/up weights",
    "wgl": "their low part",
    "gue": "gate and up products",
    "the": "tanh of the gate",
    "ech": "gate half of the hidden rows",
    "hhe": "hidden rows",
    "hte": "hidden rows turned (PSUM)",
    "htc": "the same in SBUF",
    "dne": "down products",
    "oc": "one-hot columns",
    "gbm": "gb of each slot (PSUM)",
    "gbs": "the same in SBUF",
    "ye": "weighted rows",
    "sc": "rows added to the output",
    "is": "index column for the sum",
}


def build(nc, x, wqkvo, bq, bk, bv, bo, gate_w, bias, w_gu, w_dn, ws_gu, ws_dn, c_t, wmod, out):
    scr_w = nc.dram_tensor("scr_w", [4, 2, P, KT * D], F32, kind="Internal").ap()
    scr_gu = nc.dram_tensor("scr_gu", [2, P, KT * 2 * F], F32, kind="Internal").ap()
    scr_dn = nc.dram_tensor("scr_dn", [2, FH, 2 * D], F32, kind="Internal").ap()
    scr_qk = nc.dram_tensor("scr_qk", [2, 2, D, S], F32, kind="Internal").ap()
    scr_row = nc.dram_tensor("scr_row", [2, GH * S], F32, kind="Internal").ap()
    scr_mod = nc.dram_tensor("scr_mod", [B, 6, D], F32, kind="Internal").ap()
    HW = D + E
    htab = nc.dram_tensor("htab", [T + CAP, HW], F32, kind="Internal").ap()

    ctx = ExitStack()
    with ctx:
        arena = ctx.enter_context(nc.sbuf_tensor("arena", [P, 207 * KiB // 4], F32))
        del arena
        base = nc.sbuf_base - 207 * KiB

        def at(name, off, shape, dt=F32):
            return nc.alloc_sbuf_tensor_at(name, shape, dt, offset=base + off)

        def pair(name):
            return ctx.enter_context(nc.psum_tensor(name, [P, 2, 512], F32))

        sems = {}

        def sem(name):
            sems[name] = ctx.enter_context(nc.semaphore("s_" + name))
            return sems[name]

        pA, pB, pC, pD = (pair(n) for n in ("pA", "pB", "pC", "pD"))
        AB, AD = [pA, pB], [pA, pD]
        score_bank = [pA[:, 0, :], pA[:, 1, :], pB[:, 0, :]]
        unit_bank = [pB[:, 1, :], pD[:, 0, :], pD[:, 1, :]]

        h_hi = at("h_hi", 0, [P, KT, S], F32R)
        h_lo = at("h_lo", 16 * KiB, [P, KT, S], F32R)
        v_rows = at("v_rows", 32 * KiB, [P, NT, D])
        x2_rows = at("x2_rows", 32 * KiB, [P, NT, D])
        STK0 = 48 * KiB
        q_stk = [at(f"q_stk{n}", STK0 + 32 * KiB * n, [P, GH, S], F32R) for n in range(3)]
        k_stk = [at(f"k_stk{n}", STK0 + 32 * KiB * n + 16 * KiB, [P, GH, S], F32R) for n in range(3)]
        wv = [at(f"wv{n}", STK0 + 64 * KiB + 8 * KiB * n, [P, KT, D], F32R) for n in range(2)]
        wq = [at(f"wq{n}", 144 * KiB + 8 * KiB * n, [P, KT, D], F32R) for n in range(2)]
        wk_ = [at(f"wk{n}", STK0 + 80 * KiB + 8 * KiB * n, [P, KT, D], F32R) for n in range(2)]
        wo = [at(f"wo{n}", STK0 + 32 * KiB + 8 * KiB * n, [P, KT, D], F32R) for n in range(2)]
        wsg = [at(f"wsg{n}", STK0 + 48 * KiB + 6 * KiB * n, [P, KT, 2 * F], F32R) for n in range(2)]
        wsd = [at(f"wsd{n}", STK0 + 80 * KiB + 4 * KiB * n, [FH, 2, D], F32R) for n in range(2)]
        hs = [at(f"hs{n}", STK0 + (88, 24)[n] * KiB, [FH, 2, S], F32R) for n in range(2)]
        p_buf = at("p_buf", 144 * KiB, [P, 2, GH, CH])
        x_rows = at("x_rows", STK0 + 64 * KiB, [P, NT, D])
        mask = at("mask", 160 * KiB, [P, S])
        x_in = at("x_in", 164 * KiB, [P, 2, D])
        wk = at("wk", 168 * KiB, [P, 2, 512])
        hi_s = at("hi_s", 172 * KiB, [P, 2, 512], F32R)
        lo_s = at("lo_s", 176 * KiB, [P, 2, 512], F32R)
        pre_s = [at(f"pre_s{n}", (172, 174, 164, 166)[n] * KiB, [P, D]) for n in range(4)]
        od = at("od", 180 * KiB, [P, 2, CH])
        tmp = at("tmp", 184 * KiB, [P, 2, 512])
        h2b = at("h2b", 176 * KiB, [P, 2, 512])
        ga = at("ga", 188 * KiB, [P, D])
        gabo = at("gabo", 190 * KiB, [P, D])
        cb1 = at("cb1", 192 * KiB, [P, D])
        sbm = at("sbm", 194 * KiB, [P, D])
        gb = at("gb", 196 * KiB, [P, D])
        bv_b = at("bv_b", 198 * KiB, [P, D])
        gw = at("gw", 200 * KiB, [P, KT, E])
        ident_b = at("ident_b", 201 * KiB, [P, P], BF16)
        mask_t = at("mask_t", 201 * KiB + 256, [P, P], BF16)
        run_a = at("run_a", 201 * KiB + 512, [E, 3 * CAP])
        run_b = at("run_b", 168 * KiB + 512, [E, 3 * CAP])
        first = at("first", 170 * KiB, [E, CAP])
        ident = at("ident", 203 * KiB + 512, [P, P])
        m0 = 204 * KiB
        ones = at("ones", m0, [P, DH])
        mx = at("mx", m0 + 128, [P, GH, NT, 2])
        negm = at("negm", m0 + 384, [P, GH * NT])
        mrow = at("mrow", m0 + 512, [GH * NT, P], F32R)
        stat = at("stat", m0 + 1024, [P, NT, 6])
        mv = at("mv", m0 + 1216, [P, NT, 2])
        var = at("var", m0 + 1280, [P, NT])
        rstd = at("rstd", m0 + 1312, [P, NT])
        nhalf = at("nhalf", m0 + 1344, [P, NT])
        tokn = at("tokn", m0 + 1376, [P, NT])
        sa_c = at("sa_c", m0 + 1408, [P, KT])
        ca_c = at("ca_c", m0 + 1424 + 16, [P, KT])
        bq_c = at("bq_c", m0 + 1472, [P, KT])
        bk_c = at("bk_c", m0 + 1504, [P, KT])
        bqs = at("bqs", m0 + 1536, [P, KT])
        bks = at("bks", m0 + 1568, [P, KT])
        bias_b = at("bias_b", m0 + 1600, [P, E])
        tri = at("tri", m0 + 1856, [P, GROUPS * GROUPS])
        slots_f = at("slots_f", m0 + 2112, [P, CAP])
        v8 = at("v8", m0 + 2496, [P, NT, 8])
        wsum = at("wsum", m0 + 2752, [P, NT])
        rws = at("rws", m0 + 2784, [P, NT])
        tokv = at("tokv", m0 + 2880, [P, NT])
        rcol = at("rcol", m0 + 2816, [P, CH // 32])

        def rt(name, off, shape, dt=F32):
            return at(name, STK0 + off, shape, dt)
        th = rt("th", 0, [P, NT, E])
        sc = rt("sc", 2048, [P, NT, E])
        sb_ = rt("sb_", 4096, [P, NT, E])
        cmp = rt("cmp", 6144, [P, NT, GROUPS, GROUPS])
        ceq = rt("ceq", 8192, [P, NT, GROUPS, GROUPS])
        rep = rt("rep", 10240, [P, NT, E])
        sel = rt("sel", 12288, [P, NT, E])
        wdn = rt("wdn", 14336, [P, NT, E])
        valt = rt("valt", 16384, [P, 4, 2, E])
        ta = rt("ta", 18432, [P, E, 4])
        tb = rt("tb", 19456, [P, E, 4])
        tc_ = rt("tc_", 20480, [P, E, 2])
        td = rt("td", 20992, [P, E, 2])
        te = rt("te", 21504, [P, E, 2])
        tf = rt("tf", 22016, [P, E, 2])
        gsum = rt("gsum", 22528, [P, NT, GROUPS])
        gcnt = rt("gcnt", 22784, [P, NT, GROUPS])
        gsel = rt("gsel", 23040, [P, NT, GROUPS])
        gpen = rt("gpen", 23296, [P, NT, GROUPS])
        keys = at("keys", 164 * KiB, [P, 512])
        keys2 = at("keys2", 166 * KiB, [P, 512])
        lb = at("lb", 168 * KiB, [P, CAP])

        wstage = [at(f"wstage{n}", STK0 + 48 * KiB + 8 * KiB * n, [P, KT * D]) for n in range(2)]
        wsh = [at(f"wsh{n}", 8 * KiB * n, [P, KT * D], F32R) for n in range(2)]
        wsl = [at(f"wsl{n}", 16 * KiB + 8 * KiB * n, [P, KT * D], F32R) for n in range(2)]
        wm = at("wm", STK0, [P, KT, 6 * D])
        modr = at("modr", 144 * KiB, [B, 6, D])
        modn = at("modn", 156 * KiB, [B, D])
        ct = at("ct", 32 * KiB, [P, KT, B])
        ctt = at("ctt", 32 * KiB + 64, [P, KT, B])
        cts = at("cts", 32 * KiB + 128, [P, KT, B])
        zrow = at("zrow", 33 * KiB, [CAP, HW])
        onev = [at(f"onev{n}", (STK0 + 80 * KiB, 164 * KiB)[n], [1, GH * S]) for n in range(2)]

        NW = 4
        weg = [at(f"weg{n}", 6 * KiB * n, [P, KT, 2 * F]) for n in range(NW)]
        wed = [at(f"wed{n}", 24 * KiB + 4 * KiB * n, [FH + 1, 2, D]) for n in range(NW)]
        gath = [at(f"gath{n}", 48 * KiB + 2304 * n, [CAP, HW]) for n in range(NW)]
        gt = [[at(f"gt{n}_{m}", (58, 118)[n] * KiB + 1536 * m, [P, KT, CAP], F32R) for m in range(2)] for n in range(2)]
        wgs = [[at(f"wgs{n}_{m}", (120 + 12 * n + 6 * m + 1) * KiB, [P, KT, 2 * F], F32R) for m in range(2)] for n in range(2)]
        the = [at(f"the{n}", 62 * KiB + 768 * n, [CAP, F]) for n in range(2)]
        hae = [at(f"hae{n}", 64 * KiB + 768 * n, [CAP, F]) for n in range(2)]
        hhe = [at(f"hhe{n}", 66 * KiB + 768 * n, [CAP, F]) for n in range(2)]
        hte = [at(f"hte{n}", 68 * KiB + 768 * n, [FH + 1, 2, CAP]) for n in range(2)]
        gbs = [at(f"gbs{n}", 70 * KiB + 2048 * n, [CAP, D]) for n in range(2)]
        ye = [at(f"ye{n}", 74 * KiB + 2048 * n, [CAP, D]) for n in range(2)]
        idg = [at(f"idg{n}", 78 * KiB + 32 * n, [CAP, 1], U32) for n in range(NW)]
        ids = [at(f"ids{n}", 78 * KiB + 32 * NW + 32 * n, [CAP, 1], U32) for n in range(NW)]
        ohc = [at(f"ohc{n}", 79 * KiB + 256 * n, [3 * B, CAP], BF16) for n in range(2)]
        idu = at("idu", 80 * KiB, [CAP, E], U32)
        oh = at("oh", 81 * KiB, [3 * B, E * CAP], BF16)
        gb12 = at("gb12", 94 * KiB, [3 * B, D], BF16)
        fz = at("fz", 103 * KiB, [E, CAP])
        idf = at("idf", 104 * KiB, [E, CAP])
        oge = at("oge", 105 * KiB, [E, CAP])
        ohb = [at(f"ohb{n}", 106 * KiB + 256 * n, [E, CAP], BF16) for n in range(B)]
        gbr = at("gbr", 108 * KiB, [B, D])
        gbp = [at(f"gbp{n}", 110 * KiB + 1024 * n, [B, D], BF16) for n in range(3)]
        gbq = [at(f"gbq{n}", 114 * KiB + 2048 * n, [B, D]) for n in range(2)]

        for n in BATCH_SIGNALS:
            sem(n)
        batch_sems = [sems[n] for n in BATCH_SIGNALS]
        for n in OTHER_SIGNALS:
            sem(n)
        s = sems
        s_x, s_qkw, s_stk = [s["x0"], s["x1"]], [s["qkw0"], s["qkw1"]], [s["stk0"], s["stk1"], s["stk2"]]
        s_xi, s_hw, s_pw = [s["xi0"], s["xi1"]], [s["hw0"], s["hw1"]], [s[f"pw{n}"] for n in range(4)]
        s_we, s_wd, s_ga = ([s[f"{x}{n}"] for n in range(4)] for x in ("we", "wd", "ga"))
        s_wst, s_wwr = [s["wst0"], s["wst1"]], [s["wwr0"], s["wwr1"]]


        def need(eng, name, n):
            eng.wait_ge(s[name], n)

        def batches(eng, body):
            with eng.Fori(0, B) as it:
                body(it)

        def end_of_batch(eng, name):
            share = ("sp", "act", "dve", "pe").index(name)
            eng.drain().then_inc(s["end"], 1)
            eng.wait_ge(s["go_" + name], 1)
            eng.sem_clear(s["go_" + name])
            for x in batch_sems[share::5]:
                eng.sem_clear(x)
            eng.sem_inc(s["cleared"], 1)
            eng.wait_ge(s["on_" + name], 1)
            eng.sem_clear(s["on_" + name])

        splits = [(wqkvo[k], KT * D, P, scr_w[k]) for k in range(4)]
        splits += [(ws_gu, KT * 2 * F, P, scr_gu), (ws_dn, 2 * D, FH, scr_dn)]

        def store_split(sp, k):
            src, n, rows, dst = splits[k]
            sp.wait_ge(s["wsp_l"], k + 1)
            for part, t in ((0, wsh), (1, wsl)):
                sp.dma_start(dst[part], t[k % 2][0:rows, 0:n].bitcast(F32)).then_inc(s_wwr[k % 2], 16)

        def load_gate_up(sp, e, r, reused):
            if reused:
                sp.wait_ge(s["wgl"], e - (NW - 1))
            sp.dma_start(weg[r][:, :, :], w_gu[bass.ds(e, 1)].rearrange("o p k f -> (o p) k f")).then_inc(s_we[r], 16)

        def load_down(sp, e, r, reused):
            if reused:
                sp.wait_ge(s["dne"], e - (NW - 1))
            sp.dma_start(wed[r][0:FH, :, :], w_dn[bass.ds(e, 1)].rearrange("o p k f -> (o p) k f")).then_inc(s_wd[r], 16)

        def evac_chunk(act, g, c):
            need(act, "pv", g * NS + (4 if c == 0 else NS))
            n = g * NC + c
            if n >= 1:
                need(act, "at", n)
            act.activation(od[:, :, :], pC[:, :, :], ACT.Copy).then_inc(s["od"], 1)

        block = ctx.enter_context(nc.Block())

        @block.sync
        def _(sp):
            sp.dma_start(ct[:, :, :], c_t).then_inc(s["ld"], 16)
            sp.dma_start(wm[:, :, :], wmod).then_inc(s["ld"], 16)
            for k, (src, n, rows, dst) in enumerate(splits):
                if k >= 2:
                    sp.wait_ge(s["wsp_l"], k - 1)
                sp.dma_start(wstage[k % 2][0:rows, 0:n], src).then_inc(s_wst[k % 2], 16)
                if k >= 1:
                    store_split(sp, k - 1)
                if k == 3:
                    for h in range(2):
                        xb = x.rearrange("(b t p) d -> b p t d", b=B, p=P)[0]
                        sp.dma_start(x_rows[:, 4 * h:4 * h + 4, :], xb[:, 4 * h:4 * h + 4, :]).then_inc(s["x_1st"], 16)
                    sp.wait_ge(s["modv"], 1)
                    sp.dma_start(scr_mod, modr[:, :, :]).then_inc(s["mw"], 16)
            store_split(sp, len(splits) - 1)
            sp.dma_start(bq_c[:, :], bq).then_inc(s["cst"], 16)
            sp.dma_start(bk_c[:, :], bk).then_inc(s["cst"], 16)
            sp.dma_start(bv_b[:, :], bv.partition_broadcast(P)).then_inc(s["cst"], 16)
            sp.dma_start(bias_b[:, :], bias.partition_broadcast(P)).then_inc(s["cst"], 16)
            sp.dma_start(gw[:, :, :], gate_w).then_inc(s["cst"], 16)
            sp.wait_ge(s["zr"], 3)
            sp.dma_start(htab[T:T + CAP, :], zrow[:, :]).then_inc(s["pre_idx"], 16)
            sp.dma_start(out[T:T + CAP, :], zrow[:, 0:D]).then_inc(s["pre_idx"], 16)
            for r in range(2):
                sp.dma_start(scr_row[r:r + 1, :], onev[r][:, :]).then_inc(s["pre_idx"], 16)
            sp.wait_ge(s["mw"], 16)
            sp.wait_ge(s["pre_idx"], 64)
            for n in range(2):
                sp.wait_ge(s_wwr[n], 32 * 3)

            def rows_of(b):
                return x.rearrange("(b t p) d -> b p t d", b=B, p=P)[bass.ds(b, 1)].rearrange("o p t d -> (o p) t d")

            def table_rows(b):
                return htab[0:T, :].rearrange("(b t p) d -> b t p d", b=B, p=P)[bass.ds(b, 1)].rearrange("o t p d -> (o t) p d")

            def store_weights(b, signal):
                sp.dma_start(table_rows(b).rearrange("t p d -> p t d")[:, :, D:HW], wdn[:, :, :]).then_inc(signal, 16)

            def load_columns(b, signal):
                mod = scr_mod[bass.ds(b, 1)].rearrange("o m d -> (o m) d")
                for n, dst in ((0, sa_c), (1, ca_c)):
                    sp.dma_start(dst[:, :], mod[n].rearrange("(k p) -> p k", p=P), allow_slow_non_contiguous=True).then_inc(signal, 16)

            def load_split(dst, src, signal, k=KT):
                for n in range(2):
                    sp.dma_start(dst[n][:, :, :].bitcast(F32), src[n].rearrange("p (k d) -> p k d", k=k)).then_inc(signal, 16)

            load_columns(0, s["col_1st"])
            load_split(wq, scr_w[0], s["wq_1st"])

            for n in range(4):
                sp.sem_inc(s_pw[n], 32)

            def body(it):
                xb = rows_of((it + 1) % B)
                xt = x.rearrange("(b t p) d -> b t p d", b=B, p=P)[bass.ds(it, 1)].rearrange("o t p d -> (o t) p d")
                ht = table_rows(it)
                ot = out[0:T, :].rearrange("(b t p) d -> b t p d", b=B, p=P)[bass.ds(it, 1)].rearrange(
                    "o t p d -> (o t) p d")
                mod = scr_mod[bass.ds(it, 1)].rearrange("o m d -> (o m) d")
                load_split(wk_, scr_w[1], s["wqk"])
                for n in range(4):
                    sp.wait_ge(s_pw[n], 32)
                    sp.sem_clear(s_pw[n])
                sp.sem_inc(s["landed"], 1)
                need(sp, "xt", 2 * KT)
                load_split(wv, scr_w[2], s["wv"])

                def load_stack(g):
                    for u in range(2):
                        sp.wait_ge(s_qkw[u], 32 * (3, 4, 6, 8)[g])
                    for dst, t, parts in ((q_stk[g % 3], 0, (0, 1, 0)), (k_stk[g % 3], 1, (0, 0, 1))):
                        for r, part in enumerate(parts):
                            src = scr_qk[t, part, g * P:(g + 1) * P, :].rearrange("(j d) s -> d j s", d=DH)
                            sp.dma_start(dst[r * DH:(r + 1) * DH, :, :].bitcast(F32), src).then_inc(s_stk[g % 3], 16)
                    for r, dst in enumerate((q_stk[g % 3], k_stk[g % 3])):
                        sp.dma_start(dst[3 * DH:STK, :, :].rearrange("p j s -> p (j s)").bitcast(F32), scr_row[r:r + 1, :]).then_inc(
                            s_stk[g % 3], 16)

                for u in range(16):
                    m, t, c = qk_part(u)
                    need(sp, "lo", u + 1)
                    for part, src in ((0, hi_s), (1, lo_s)):
                        sp.dma_start(scr_qk[t, part, m * P:(m + 1) * P, c * CH:(c + 1) * CH],
                                     src[:, u % 2, :].bitcast(F32)).then_inc(s_qkw[u % 2], 16)
                    if u == 5:
                        need(sp, "val", 1)
                        store_weights((it + B - 1) % B, s["ww"])
                        sp.wait_ge(s["ww"], 16)
                        need(sp, "vt", 1)
                        load_stack(0)
                    if u == 7:
                        load_stack(1)
                        for n, dst in ((2, ga), (4, cb1), (3, sbm), (5, gb)):
                            sp.dma_start(dst[:, :], mod[n].partition_broadcast(P)).then_inc(s["mod"], 16)
                        sp.dma_start(gabo[:, :], bo.partition_broadcast(P)).then_inc(s["mod"], 16)

                def shift_row(g):
                    need(sp, "df", DPG * (g + 1))
                    sp.dma_start(q_stk[g % 3][3 * DH:STK, :, :].rearrange("p j s -> p (j s)").bitcast(F32),
                                 mrow[:, :].bitcast(F32)).then_inc(s["m"], 16)

                shift_row(0)
                need(sp, "qk", 16)
                load_stack(2)
                shift_row(1)
                need(sp, "st", GH * NS)
                load_stack(3)
                shift_row(2)
                need(sp, "st", GH * NS * 2)
                load_split(wo, scr_w[3], s["wo"])
                load_split(wsg, scr_gu, s["wo"])
                shift_row(3)
                need(sp, "st", GH * NS * 3)
                for h in range(2):
                    sp.dma_start(x_rows[:, 4 * h:4 * h + 4, :], xb[:, 4 * h:4 * h + 4, :]).then_inc(s_x[h], 16)
                load_columns((it + 1) % B, s["col"])
                load_split(wsd, scr_dn, s["wsd"], 2)
                need(sp, "lbd", 1)
                sp.dma_start(run_a[:, 2 * CAP:3 * CAP], lb[E:2 * E, :]).then_inc(s["up"], 16)

                def load_x(i):
                    if i >= 2:
                        need(sp, "xg", i - 1)
                    sp.dma_start(x_in[:, i % 2, :], xt[i]).then_inc(s_xi[i % 2], 16)

                load_x(0)
                load_x(1)
                need(sp, "pv", NG * NS)
                load_split(wq, scr_w[0], s["wq"])
                for i in range(NT):
                    if i + 2 < NT:
                        load_x(i + 2)
                    need(sp, "h2", i + 1)
                    sp.dma_start(ht[i][:, 0:D], h2b[:, i % 2, :]).then_inc(s_hw[i % 2], 16)
                for i in range(NT):
                    if i < PRE_POOL:
                        need(sp, "pre", i + 1)
                    else:
                        need(sp, "prv", i + 1 - PRE_POOL)
                    sp.dma_start(ot[i], pre_s[i % 4][:, :]).then_inc(s_pw[i % 4], 16)
                for n in range(2):
                    sp.wait_ge(s_hw[n], 64)
                sp.wait_ge(s["col"], 32)
                sp.wait_ge(s["wq"], 32)
                end_of_batch(sp, "sp")

            batches(sp, body)

            for n in range(4):
                sp.wait_ge(s_pw[n], 32)
            sp.wait_ge(s["val_last"], 1)
            store_weights(B - 1, s["w_last"])
            sp.dma_start(gbr[:, :], scr_mod[:, 5, :]).then_inc(s["fgb"], 16)
            for e in range(NW):
                load_gate_up(sp, e, e, False)
                if e < NW - 1:
                    load_down(sp, e, e, False)
            sp.wait_ge(s["lb_last"], 1)
            sp.dma_start(run_a[:, 2 * CAP:3 * CAP], lb[E:2 * E, :]).then_inc(s["mrg"], 16)
            sp.wait_ge(s["idx"], 1)
            for n in range(3):
                sp.dma_start(gb12[B * n:B * n + B, :], gbp[n][:, :]).then_inc(s["g12"], 16)
                for b in range(B):
                    sp.dma_start(oh[B * n + b:B * n + b + 1, :], ohb[b][:, :]).then_inc(s["g12"], 16)
            load_down(sp, NW - 1, NW - 1, False)
            load_gate_up(sp, NW, 0, True)
            with sp.Fori(0, (E - NW) // NW - 1) as k:
                for r in range(NW):
                    load_down(sp, k * NW + (NW + r), r, True)
                    load_gate_up(sp, k * NW + (NW + r + 1), (r + 1) % NW, True)
            for e in range(E - NW, E):
                load_down(sp, e, e % NW, True)
                if e + 1 < E:
                    load_gate_up(sp, e + 1, (e + 1) % NW, True)

        @block.gpsimd
        def _(pool):
            pool.memset(ident[:, :], 0.0).then_inc(s["cst_v"], 1)
            pool.memset(mask[:, :], 0.0).then_inc(s["cst_v"], 1)
            pool.memset(tri[:, :], 1.0).then_inc(s["cst_v"], 1)
            pool.memset(ones[:, :], 1.0).then_inc(s["cst_v"], 1)
            pool.memset(nhalf[:, :], -0.5).then_inc(s["cst_v"], 1)
            pool.memset(ident_b[:, :], 0.0).then_inc(s["cst_v"], 1)
            pool.memset(mask_t[:, :], 0.0).then_inc(s["cst_v"], 1)
            pool.memset(zrow[:, :], 0.0).then_inc(s["zr"], 1)
            pool.memset(onev[0][:, :], 0.0).then_inc(s["zr"], 1)
            pool.memset(onev[1][:, :], 1.0).then_inc(s["zr"], 1)
            pool.wait_ge(s["cst_v"], 7)
            pool.affine_select(out=ident[:, :], in_=ident[:, :], compare_op=ALU.not_equal, fill=1.0, base=0,
                               pattern=[[-1, P]], channel_multiplier=1).then_inc(s["cst_v"], 1)
            pool.affine_select(out=ident_b[:, :], in_=ident_b[:, :], compare_op=ALU.not_equal, fill=1.0, base=0,
                               pattern=[[-1, P]], channel_multiplier=1).then_inc(s["cst_v"], 1)
            pool.affine_select(out=mask_t[:, :], in_=mask_t[:, :], compare_op=ALU.is_ge, fill=-BIG, base=0,
                               pattern=[[1, P]], channel_multiplier=-1).then_inc(s["cst_v"], 1)
            pool.affine_select(out=mask[:, :], in_=mask[:, :], compare_op=ALU.is_ge, fill=-BIG, base=S - P,
                               pattern=[[-1, S]], channel_multiplier=1).then_inc(s["cst_v"], 1)
            pool.affine_select(out=tri[:, :].rearrange("p (g h) -> p g h", g=GROUPS),
                               in_=tri[:, :].rearrange("p (g h) -> p g h", g=GROUPS), compare_op=ALU.is_ge, fill=0.0,
                               base=-1, pattern=[[1, GROUPS], [-1, GROUPS]], channel_multiplier=0).then_inc(s["cst_v"], 1)
            pool.iota(tokn[:, :], pattern=[[-P, NT]], base=T + S, channel_multiplier=-1,
                      allow_small_or_imprecise_dtypes=True).then_inc(s["cst_v"], 1)
            pool.iota(slots_f[:, :], pattern=[[1, CAP]], base=0, channel_multiplier=0,
                      allow_small_or_imprecise_dtypes=True).then_inc(s["cst_v"], 1)

            pool.wait_ge(s["var_1st"], NT)
            pool.tensor_tensor(rstd[:, :], var[:, :], nhalf[:, :], ALU.pow).then_inc(s["rs_1st"], 1)

            def body(it):
                def tile_x(i):
                    pool.wait_ge(s_xi[i % 2], 16 * (i // 2) + 16)
                    if i >= 2:
                        need(pool, "x2", i - 1)
                    pool.tensor_tensor(od[:, (i + 1) % 2, :], x_in[:, i % 2, :], gabo[:, :], ALU.add).then_inc(s["xg"], 1)

                for n in range(NG * NC):
                    g, c = n // NC, n % NC
                    if n == (NG - 1) * NC:
                        need(pool, "var", NT)
                        pool.tensor_tensor(rstd[:, :], var[:, :], nhalf[:, :], ALU.pow).then_inc(s["rs"], 1)
                        need(pool, "mod", 16 * 5)
                        pool.tensor_tensor(gabo[:, :], gabo[:, :], ga[:, :], ALU.mult).then_inc(s["gabo"], 1)
                        pool.wait_ge(s["gabo"], 1)
                    if n == NG * NC - 1:
                        pool.wait_ge(s["rch"], 4 * n + 1)
                        tile_x(0)
                    pool.wait_ge(s["rch"], 4 * n + 4)
                    pool.tensor_tensor(od[:, 0, :], od[:, 0, :], tmp[:, 1, :], ALU.mult).then_inc(s["an"], 1)
                    need(pool, "ah", n + 1)
                    pool.tensor_tensor(h_lo[:, g, c * CH:(c + 1) * CH], od[:, 0, :],
                                       h_hi[:, g, c * CH:(c + 1) * CH].bitcast(F32), ALU.subtract).then_inc(s["at"], 1)
                def tile_low(i):
                    need(pool, "h2h", i + 1)
                    pool.tensor_tensor(h_lo[:, :, i * P:i * P + P], wk[:, i % 2, :].rearrange("p (k q) -> p k q", k=KT),
                                       h_hi[:, :, i * P:i * P + P].bitcast(F32), ALU.subtract).then_inc(s["h2l"], 1)

                need(pool, "at", NG * NC)
                for i in range(NT):
                    need(pool, "var", NT + i + 1)
                    pool.tensor_tensor(rstd[:, i:i + 1], var[:, i:i + 1], nhalf[:, i:i + 1], ALU.pow).then_inc(s["rs"], 1)
                    if i + 1 < NT:
                        tile_x(i + 1)
                    if i >= 2:
                        tile_low(i - 2)
                tile_low(NT - 2)
                tile_low(NT - 1)
                for i in range(PRE_POOL):
                    need(pool, "sg", i + 1)
                    if i >= 4:
                        pool.wait_ge(s_pw[i % 4], 16)
                    pool.tensor_tensor(pre_s[i % 4][:, :], tmp[:, i % 2, :], x2_rows[:, i, :], ALU.add).then_inc(s["pre"], 1)
                pool.drain()
                pool.wait_ge(s["end"], 4)
                pool.sem_clear(s["end"])
                for n in ("sp", "act", "dve", "pe"):
                    pool.sem_inc(s["go_" + n], 1)
                for x in batch_sems[4::5]:
                    pool.sem_clear(x)
                pool.wait_ge(s["cleared"], 4)
                pool.sem_clear(s["cleared"])
                for n in ("sp", "act", "dve", "pe"):
                    pool.sem_inc(s["on_" + n], 1)

            batches(pool, body)

            def gather(e, r, reused):
                if reused:
                    pool.wait_ge(s["ye"], e - (NW - 1))
                pool.tensor_copy(idg[r][:, :], idu[:, bass.ds(e, 1)]).then_inc(s["ic"], 1)
                pool.wait_ge(s["ic"], e + 1)
                pool.sem_inc(s["pas"], 1)
                pool.indirect_dma_start(gath[r][:, :], None, htab, bass.IndirectOffsetOnAxis(ap=idg[r][:, :], axis=0)).then_inc(
                    s_ga[r], 16)

            def scatter(e, r, first):
                pool.tensor_copy(ids[r][:, :], idu[:, bass.ds(e, 1)]).then_inc(s["is"], 1)
                pool.wait_ge(s["is"], e + 1)
                pool.wait_ge(s["ye"], e + 1)
                if not first:
                    pool.wait_ge(s["sc"], e * 16)
                pool.sem_inc(s["pas"], 1)
                pool.indirect_dma_start(out, bass.IndirectOffsetOnAxis(ap=ids[r][:, :], axis=0), ye[r % 2][:, :], None,
                                        compute_op=ALU.add).then_inc(s["sc"], 16)

            for z in wed + hte:
                pool.memset(z[FH:FH + 1, :, :], 0.0).then_inc(s["ez"], 1)
            pool.wait_ge(s["w_last"], 16)
            pool.wait_ge(s["idt"], 2)
            for e in range(NW):
                gather(e, e, False)
            scatter(0, 0, True)
            with pool.Fori(0, (E - NW) // NW) as k:
                for r in range(NW):
                    gather(k * NW + (r + 4), r, True)
                    scatter(k * NW + (r + 1), (r + 1) % NW, False)
            for e in range(E - NW + 1, E):
                scatter(e, e % NW, False)
            pool.wait_ge(s["sc"], 16 * E)

        @block.scalar
        def _(act):
            act.wait_ge(s["ld"], 32)
            act.activation(ctt[:, :, :], ct[:, :, :], ACT.Tanh, scale=0.5).then_inc(s["csil"], 1)
            for k, (src, n, rows, dst) in enumerate(splits):
                act.wait_ge(s_wst[k % 2], 16 * (k // 2) + 16)
                if k >= 2:
                    act.wait_ge(s_wwr[k % 2], 32 * (k // 2))
                act.activation(wsh[k % 2][0:rows, 0:n], wstage[k % 2][0:rows, 0:n], ACT.Copy).then_inc(s["wsp_h"], 1)
                for m in ((0,), (1, 2, 3), (4, 5), (), (), ())[k]:
                    act.wait_ge(s["modm"], m + 1)
                    act.activation(modr[:, m, :], AB[m // 2 % 2][0:B, m % 2, :], ACT.Copy).then_inc(s["modc"], 1)
            act.wait_ge(s["cst"], 80)
            act.mul(bqs[:, :], bq_c[:, :], QSCALE).then_inc(s["csil"], 1)
            act.mul(bks[:, :], bk_c[:, :], QSCALE).then_inc(s["csil"], 1)
            act.wait_ge(s["csil"], 4)
            act.wait_ge(s["col_1st"], 32)

            def body(it):
                for n in range(2 * KT):
                    h, k = n // KT, n % KT
                    need(act, "xt", n + 1)
                    if n >= 2:
                        need(act, "hl", n - 1)
                    src = AB[k // 2][:, k % 2, :]
                    act.activation(wk[:, n % 2, :], src, ACT.Identity, bias=sa_c[:, k:k + 1], scale=ca_c[:, k:k + 1])
                    act.activation(h_hi[:, k, h * 512:h * 512 + 512], src, ACT.Identity, bias=sa_c[:, k:k + 1],
                                   scale=ca_c[:, k:k + 1]).then_inc(s["hh"], 1)
                for u in range(16):
                    m, t, _ = qk_part(u)
                    need(act, "qk", u + 1)
                    if u >= 2:
                        need(act, "lo", u - 1)
                        act.wait_ge(s_qkw[u % 2], 32 * (u // 2))
                    else:
                        need(act, "hl", 2 * KT)
                        need(act, "landed", 1)
                    b_ = (bqs, bks)[t][:, m:m + 1]
                    act.activation(wk[:, u % 2, :], pC[:, u % 2, :], ACT.Identity, bias=b_, scale=QSCALE)
                    act.activation(hi_s[:, u % 2, :], pC[:, u % 2, :], ACT.Identity, bias=b_, scale=QSCALE).then_inc(s["hi"], 1)
                for g in range(NG):
                    for st, (c, kt, q0) in enumerate(STEPS):
                        for j in range(GH):
                            v = GH * (g * NS + st) + j
                            need(act, "st", v + 1)
                            if g * NS + st >= 2:
                                need(act, "pv", g * NS + st - 1)
                            act.activation(p_buf[:, st % 2, j, q0:CH], score_bank[v % 3][:, q0:CH],
                                           ACT.Exp).then_inc(s["ex"], 1)
                        if st == NC * 2:
                            evac_chunk(act, g, 0)
                    evac_chunk(act, g, 1)
                for i in range(NT):
                    need(act, "tr", i + 1)
                    if i >= 2:
                        need(act, "lg", i - 1)
                        need(act, "h2l", i - 1)
                    else:
                        need(act, "lo", 16)
                        need(act, "lst", 1)
                    src = pB[:, i % 2, :].rearrange("p (k q) -> p k q", k=KT)
                    act.activation(wk[:, i % 2, :].rearrange("p (k q) -> p k q", k=KT), src, ACT.Copy).then_inc(s["wk"], 1)
                    act.activation(h_hi[:, :, i * P:i * P + P], src, ACT.Copy).then_inc(s["h2h"], 1)
                    need(act, "lg", i + 1)
                    act.activation(th[:, i, :], pC[:, i % 2, 0:E], ACT.Tanh, scale=0.5).then_inc(s["th"], 1)
                for w in range(4):
                    need(act, "gu", w + 1)
                    if w >= 2:
                        need(act, "hs", w - 1)
                    else:
                        need(act, "h2l", NT)
                    act.activation(wk[0:FH, w % 2, :], pA[0:FH, w % 2, :], ACT.Tanh, scale=0.5).then_inc(s["tg"], 1)
                end_of_batch(act, "act")

            batches(act, body)

            def xcopy(e, r):
                act.wait_ge(s["xte"], e + 1)
                act.activation(gt[0][r % 2][:, :, :], pB[:, r % 2, 0:KT * CAP].rearrange("p (k q) -> p k q", k=KT),
                               ACT.Copy).then_inc(s["gte"], 1)

            def gbcopy(e, r, early):
                act.wait_ge(s["gbm"], e + 1)
                if not early:
                    act.wait_ge(s["ye"], e - 1)
                act.activation(gbs[r % 2][:, :], pD[0:CAP, 0, :], ACT.Copy).then_inc(s["gbs"], 1)

            def htcopy(e, r, early):
                act.wait_ge(s["hte"], e + 1)
                if not early:
                    act.wait_ge(s["dne"], e - 1)
                act.activation(hte[r % 2][0:FH, :, :], pD[0:FH, 1, 0:2 * CAP].rearrange("p (k q) -> p k q", k=2),
                               ACT.Copy).then_inc(s["htc"], 1)

            def weights_high(e, r, uses):
                act.wait_ge(s_we[r % 4], uses)
                if r >= 2:
                    act.wait_ge(s["gue"], e - 1)
                act.activation(wgs[0][r % 2][:, :, :], weg[r % 4][:, :, :], ACT.Copy).then_inc(s["wgh"], 1)

            def slot(e, r, more, early=False):
                act.wait_ge(s["gue"], e + 1)
                if not early:
                    act.wait_ge(s["hhe"], e - 1)
                act.activation(the[r % 2][:, :], pA[0:CAP, r % 2, 0:F], ACT.Tanh, scale=0.5).then_inc(s["the"], 1)
                if more:
                    xcopy(e + 1, r + 1)

            weights_high(0, 0, 16)
            xcopy(0, 0)
            weights_high(1, 1, 16)
            slot(0, 0, True, True)
            weights_high(2, 2, 16)
            htcopy(0, 0, True)
            slot(1, 1, True, True)
            weights_high(3, 3, 16)
            gbcopy(0, 0, True)
            htcopy(1, 1, True)
            slot(2, 2, True)
            weights_high(4, 4, 32)
            gbcopy(1, 1, True)
            htcopy(2, 2, False)
            with act.Fori(0, (E - NW) // NW - 1) as k:
                for r in range(NW):
                    e = k * NW + (r + 3)
                    slot(e, r + 3, True)
                    weights_high(k * NW + (r + 5), r + 5, k * 16 + 16 * ((r + 5) // 4 + 1))
                    gbcopy(k * NW + (r + 2), r + 2, False)
                    htcopy(e, r + 3, False)
            for e in range(E - NW - 1, E):
                slot(e, e, e + 1 < E)
                if e + 2 < E:
                    weights_high(e + 2, e + 2, 16 * ((e + 2) // 4 + 1))
                gbcopy(e - 1, e - 1, False)
                htcopy(e, e, False)
            gbcopy(E - 1, E - 1, False)

        @block.vector
        def _(dve):
            dve.wait_ge(s["csil"], 1)
            dve.scalar_tensor_tensor(out=cts[:, :, :], in0=ctt[:, :, :], scalar=1.0, in1=ct[:, :, :], op0=ALU.add,
                                     op1=ALU.mult).then_inc(s["mch"], 1)
            dve.wait_ge(s["mch"], 1)
            dve.tensor_scalar(cts[:, :, :], cts[:, :, :], 0.5, None, ALU.mult).then_inc(s["csil"], 1)

            def low_part(k):
                src, n, rows, dst = splits[k]
                dve.wait_ge(s["wsp_h"], k + 1)
                dve.tensor_tensor(wsl[k % 2][0:rows, 0:n], wstage[k % 2][0:rows, 0:n],
                                  wsh[k % 2][0:rows, 0:n].bitcast(F32), ALU.subtract).then_inc(s["wsp_l"], 1)

            for k in range(3):
                low_part(k)
            chain = [1]

            def link(ins):
                chain[0] += 1
                ins.then_inc(s["mch"], 1)
                dve.wait_ge(s["mch"], chain[0])

            dve.wait_ge(s["modc"], 6)
            for n in (1, 4):
                link(dve.tensor_scalar(modr[:, n, :], modr[:, n, :], 1.0, None, ALU.add))
            for n in (2, 5):
                link(dve.tensor_scalar(modn[:, :], modr[:, n, :], -1.0, None, ALU.mult))
                link(dve.tensor_tensor(modn[:, :], modn[:, :], modr[:, n, :], ALU.max))
                link(dve.tensor_scalar(modn[:, :], modn[:, :], 0.25, None, ALU.max))
                link(dve.tensor_scalar(modr[:, n, :], modr[:, n, :], 0.0, None, ALU.is_ge))
                link(dve.tensor_scalar(modr[:, n, :], modr[:, n, :], 2.0, -1.0, ALU.mult, ALU.add))
                link(dve.tensor_tensor(modr[:, n, :], modr[:, n, :], modn[:, :], ALU.mult))
            dve.drain().then_inc(s["modv"], 1)
            for k in range(3, len(splits)):
                low_part(k)

            for t in (sb_[:, :, :], gsum[:, :, :], run_a[:, :]):
                dve.memset(t, 0.0).then_inc(s["key_1st"], 1)
            dve.memset(sc[:, :, :], 1.0).then_inc(s["key_1st"], 1)
            dve.wait_ge(s["key_1st"], 4)

            def row_stats(link, var_ready, i):
                link(dve.bn_stats(stat[:, i, :], x_rows[:, i, :]))
                link(dve.bn_aggr(mv[:, i, :], stat[:, i, :]))
                dve.tensor_scalar(var[:, i:i + 1], mv[:, i, 1:2], EPS, None, ALU.add).then_inc(var_ready, 1)

            def row_norm(normed, i):
                dve.tensor_scalar(x_rows[:, i, :], x_rows[:, i, :], mv[:, i, 0:1], rstd[:, i:i + 1], ALU.subtract,
                                  ALU.mult).then_inc(normed, 1)

            def extraction(link):
                a, b_ = keys, keys2
                for r in range(ROUNDS):
                    link(dve.max(lb[:, 8 * r:8 * r + 8], a[:, :]))
                    if r + 1 < ROUNDS:
                        link(dve.match_replace(b_[:, :], lb[:, 8 * r:8 * r + 8], a[:, :], 0.0))
                        a, b_ = b_, a
                    yield

            def merge(link):
                a, b_ = run_a, run_b
                for r in range(ROUNDS):
                    link(dve.max(first[:, 8 * r:8 * r + 8], a[:, :]))
                    if r + 1 < ROUNDS:
                        link(dve.match_replace(b_[:, :], first[:, 8 * r:8 * r + 8], a[:, :], 0.0))
                        a, b_ = b_, a

            def router_sums(link):
                need(dve, "th", NT)
                link(dve.tensor_scalar(sc[:, :, :], th[:, :, :], 0.5, 0.5, ALU.mult, ALU.add))
                yield
                link(dve.tensor_tensor(sb_[:, :, :], sc[:, :, :], bias_b[:, :].unsqueeze(1).to_broadcast([P, NT, E]), ALU.add))
                yield
                g8 = sb_[:, :, :].rearrange("p i (g e) -> p (i g) e", e=GSIZE)
                dve.tensor_tensor(ta[:, :, :], g8[:, :, 0:4], g8[:, :, 4:8], ALU.max)
                link(dve.tensor_tensor(tb[:, :, :], g8[:, :, 0:4], g8[:, :, 4:8], ALU.min))
                yield
                hi_, lo_ = ta, tb
                for wd_, (o1, o2, o3, o4) in ((2, (tc_, td, te, tf)), (1, (ta, tb, ta, tb))):
                    a0, a1 = hi_[:, :, 0:wd_], hi_[:, :, wd_:2 * wd_]
                    b0, b1 = lo_[:, :, 0:wd_], lo_[:, :, wd_:2 * wd_]
                    r1 = o1[:, :, 0:wd_]
                    r2 = o2[:, :, 0:wd_]
                    r3 = o3[:, :, 0:wd_] if wd_ == 2 else ta[:, :, 2:3]
                    r4 = o4[:, :, 0:wd_] if wd_ == 2 else tb[:, :, 2:3]
                    dve.tensor_tensor(r1, a0, a1, ALU.max)
                    dve.tensor_tensor(r2, a0, a1, ALU.min)
                    link(dve.tensor_tensor(r3, b0, b1, ALU.max))
                    yield
                    link(dve.tensor_tensor(r4, r2, r3, ALU.max))
                    yield
                    hi_, lo_ = (o1, tf) if wd_ == 2 else (ta[:, :, 0:1], tb[:, :, 2:3])
                link(dve.tensor_tensor(gsum[:, :, :].rearrange("p i (g o) -> p (i g) o", o=1), hi_, lo_, ALU.add))
                yield

            def router_choice(link, val):
                other = gsum[:, :, :].unsqueeze(2).to_broadcast([P, NT, GROUPS, GROUPS])
                own = gsum[:, :, :].unsqueeze(3).to_broadcast([P, NT, GROUPS, GROUPS])
                tri_b = tri[:, :].rearrange("p (g h) -> p g h", g=GROUPS).unsqueeze(1).to_broadcast([P, NT, GROUPS, GROUPS])
                dve.tensor_tensor(cmp[:, :, :, :], other, own, ALU.is_gt)
                link(dve.tensor_tensor(ceq[:, :, :, :], other, own, ALU.is_equal))
                yield
                link(dve.tensor_tensor(ceq[:, :, :, :], ceq[:, :, :, :], tri_b, ALU.mult))
                yield
                link(dve.tensor_tensor(cmp[:, :, :, :], cmp[:, :, :, :], ceq[:, :, :, :], ALU.add))
                yield
                link(dve.tensor_reduce(gcnt[:, :, :], cmp[:, :, :, :], AX_X, ALU.add))
                yield
                link(dve.tensor_scalar(gsel[:, :, :], gcnt[:, :, :], KGROUPS - 0.5, None, ALU.is_lt))
                yield
                link(dve.tensor_scalar(gpen[:, :, :], gsel[:, :, :], BIG, -BIG, ALU.mult, ALU.add))
                yield
                ge = "p i (g e) -> p i g e"
                wide = [P, NT, GROUPS, GSIZE]
                link(dve.tensor_tensor(wdn[:, :, :].rearrange(ge, e=GSIZE), sb_[:, :, :].rearrange(ge, e=GSIZE),
                                       gpen[:, :, :].unsqueeze(3).to_broadcast(wide), ALU.add))
                yield
                for i in range(NT):
                    last = dve.max(v8[:, i, :], wdn[:, i, :])
                link(last)
                yield
                link(dve.memset(v8[:, :, TOPK:8], -BIG))
                yield
                for i in range(NT):
                    last = dve.match_replace(rep[:, i, :], v8[:, i, :], wdn[:, i, :], BIG)
                link(last)
                yield
                link(dve.scalar_tensor_tensor(out=sel[:, :, :].rearrange(ge, e=GSIZE), in0=rep[:, :, :].rearrange(ge, e=GSIZE),
                                              scalar=BIG, in1=gsel[:, :, :].unsqueeze(3).to_broadcast(wide),
                                              op0=ALU.is_equal, op1=ALU.mult))
                yield
                link(dve.tensor_tensor(sc[:, :, :], sel[:, :, :], sc[:, :, :], ALU.mult))
                yield
                link(dve.tensor_reduce(wsum[:, :], sc[:, :, :], AX_X, ALU.add))
                yield
                link(dve.reciprocal(rws[:, :], wsum[:, :]))
                yield
                link(dve.scalar_tensor_tensor(out=tokv[:, :], in0=tokn[:, :], scalar=float(T), in1=tokn[:, :],
                                              op0=ALU.is_le, op1=ALU.mult))
                yield
                link(dve.tensor_tensor(valt[:, :, :, :].rearrange("p q h e -> p h q e"),
                                       sel[:, :, :].rearrange("p (h q) e -> p h q e", h=2),
                                       tokv[:, :].rearrange("p (h q) -> p h q", h=2).unsqueeze(3).to_broadcast([P, 2, 4, E]),
                                       ALU.mult))
                yield
                dve.scalar_tensor_tensor(out=wdn[:, :, :], in0=sc[:, :, :], scalar=ROUTE_SCALE,
                                         in1=rws[:, :].unsqueeze(2).to_broadcast([P, NT, E]), op0=ALU.mult,
                                         op1=ALU.mult).then_inc(val, 1)
                dve.tensor_scalar(tokn[:, :], tokn[:, :], -float(S), None, ALU.add)

            dve.wait_ge(s["x_1st"], 32)
            for i in range(NT):
                row_stats(link, s["var_1st"], i)
            dve.wait_ge(s["rs_1st"], 1)
            for i in range(NT):
                row_norm(s["xn_1st"], i)
            dve.wait_ge(s["cst_v"], 14)
            dve.wait_ge(s["cst"], 80)

            def body(it):
                n_ch = [0]

                def link(ins):
                    n_ch[0] += 1
                    ins.then_inc(s["vch"], 1)
                    dve.wait_ge(s["vch"], n_ch[0])

                pieces = router_choice(link, s["val"])

                def pump(n):
                    for _ in range(n):
                        next(pieces, None)

                for n in range(2 * KT):
                    h, k = n // KT, n % KT
                    need(dve, "hh", n + 1)
                    dve.tensor_tensor(h_lo[:, k, h * 512:h * 512 + 512], wk[:, n % 2, :],
                                      h_hi[:, k, h * 512:h * 512 + 512].bitcast(F32), ALU.subtract).then_inc(s["hl"], 1)
                    pump(n % 2)
                def qk_low(u):
                    need(dve, "hi", u + 1)
                    dve.tensor_tensor(lo_s[:, u % 2, :], wk[:, u % 2, :], hi_s[:, u % 2, :].bitcast(F32),
                                      ALU.subtract).then_inc(s["lo"], 1)

                def unit_max(g, u):
                    i, kc, j, w = UNITS[u]
                    n = g * DPG + u
                    need(dve, "dq", n + 1)
                    x0 = kc * CH - i * P + S - P
                    dve.tensor_tensor_reduce(unit_bank[n % 3][:, 0:w], unit_bank[n % 3][:, 0:w], mask[:, x0:x0 + w], 1.0, -3e38, ALU.add,
                                             ALU.max, mx[:, j, i, kc:kc + 1]).then_inc(s["df"], 1)

                def group_max(g):
                    need(dve, "df", g * DPG + NU)
                    link(dve.tensor_tensor(mx[:, :, 4:8, 0], mx[:, :, 4:8, 0], mx[:, :, 4:8, 1], ALU.max))
                    dve.tensor_scalar(negm[:, :].rearrange("p (j i) -> p j i", j=GH), mx[:, :, :, 0], -1.0, None,
                                      ALU.mult).then_inc(s["negm"], 1)
                    n = g * DPG + NU
                    need(dve, "dq", n + 1)
                    if g:
                        need(dve, "m", 16 * g)
                    dve.tensor_copy(mrow[:, :], unit_bank[n % 3][0:GH * NT, 0:P]).then_inc(s["df"], 1)

                def sum_step(g, c, step):
                    n = g * NC + c
                    if step == 0:
                        need(dve, "od", n + 1)
                        if n:
                            need(dve, "an", n)
                    else:
                        dve.wait_ge(s["rch"], 4 * n + step)
                    blk = tmp[:, 0, :].rearrange("p (b r) -> p b r", r=32)
                    if step == 0:
                        ins = dve.transpose(tmp[:, 0, :], od[:, 1, :])
                    elif step == 1:
                        ins = dve.reciprocal(rcol[:, :], blk[:, :, 0])
                    elif step == 2:
                        ins = dve.tensor_copy(blk, rcol[:, :].unsqueeze(2).to_broadcast([P, 16, 32]))
                    else:
                        ins = dve.transpose(tmp[:, 1, :], tmp[:, 0, :])
                    ins.then_inc(s["rch"], 1)

                def out_high(g, c):
                    need(dve, "an", g * NC + c + 1)
                    dve.tensor_copy(h_hi[:, g, c * CH:(c + 1) * CH], od[:, 0, :]).then_inc(s["ah"], 1)

                for u in range(QK_FIRST):
                    qk_low(u)
                    pump(3 if u < 5 else 0)
                    if u == 5:
                        for _ in pieces:
                            pass
                    if u == 6:
                        need(dve, "vt", 1)
                        need(dve, "landed", 1)
                        dve.tensor_copy(keys[:, :], pD[:, 0, :]).then_inc(s["key"], 1)
                for i in range(NT):
                    for k in beside(i):
                        unit_max(0, k)
                    need(dve, "vp", i + 1)
                    dve.tensor_tensor(v_rows[:, i, :], pC[:, i % 2, :], bv_b[:, :], ALU.add).then_inc(s["vr"], 1)
                for u in range(QK_FIRST, 16):
                    ks = beside(NT + u - QK_FIRST)
                    for k in ks:
                        unit_max(0, k)
                        if k == ks[0] and u > QK_FIRST:
                            qk_low(u - 1)
                qk_low(15)
                rounds = extraction(link)
                group_max(0)
                need(dve, "key", 1)
                need(dve, "lo", 16)
                mid = sum(SHARE[:6])
                for g in range(NG):
                    if g + 1 < NG:
                        for u in range(NU):
                            unit_max(g + 1, u)
                            if g:
                                if u in (2, 4, 6, 8):
                                    sum_step(g - 1, 1, u // 2 - 1)
                                if u == 14:
                                    out_high(g - 1, 1)
                            if u - mid in (0, 2, 4, 6):
                                sum_step(g, 0, (u - mid) // 2)
                            if u - mid == 12:
                                out_high(g, 0)
                        group_max(g + 1)
                        for _ in range(ROUNDS // (NG - 1)):
                            next(rounds)
                        if g + 2 == NG:
                            dve.tensor_copy(run_a[:, CAP:2 * CAP], lb[0:E, :]).then_inc(s["lbd"], 1)
                    else:

                        def norm_chunk(gg, c):
                            for step in range(4):
                                sum_step(gg, c, step)
                            out_high(gg, c)

                        norm_chunk(g - 1, 1)
                        for i in range(NT):
                            if i % 4 == 0:
                                dve.wait_ge(s_x[i // 4], 16)
                            row_stats(link, s["var"], i)
                        need(dve, "rs", 1)
                        for i in range(NT):
                            row_norm(s["xn"], i)
                        norm_chunk(g, 0)
                        need(dve, "up", 16)
                        merge(link)
                        dve.tensor_copy(run_a[:, 0:CAP], first[:, :]).then_inc(s["lst"], 1)
                        norm_chunk(g, 1)

                def tile_sum(i):
                    need(dve, "op", i + 1)
                    if i == 0:
                        need(dve, "mod", 16 * 5)
                    dve.tensor_tensor(tmp[:, 0, :], AD[i // 2 % 2][:, i % 2, :], ga[:, :], ALU.mult).then_inc(s["of"], 1)
                    need(dve, "of", i + 1)
                    need(dve, "xg", i + 1)
                    dve.tensor_tensor(x2_rows[:, i, :], tmp[:, 0, :], od[:, (i + 1) % 2, :], ALU.add).then_inc(s["x2"], 1)
                    need(dve, "x2", i + 1)
                    link(dve.bn_stats(stat[:, i, :], x2_rows[:, i, :]))
                    link(dve.bn_aggr(mv[:, i, :], stat[:, i, :]))
                    dve.tensor_scalar(var[:, i:i + 1], mv[:, i, 1:2], EPS, None, ALU.add).then_inc(s["var"], 1)

                def tile_norm(i):
                    need(dve, "rs", i + 2)
                    if i:
                        need(dve, "h2", i)
                    link(dve.tensor_scalar(tmp[:, 1, :], x2_rows[:, i, :], mv[:, i, 0:1], rstd[:, i:i + 1],
                                           ALU.subtract, ALU.mult))
                    link(dve.tensor_tensor(tmp[:, 1, :], tmp[:, 1, :], cb1[:, :], ALU.mult))
                    if i >= 2:
                        dve.wait_ge(s_hw[i % 2], 16 * (i // 2))
                        need(dve, "tr", i - 1)
                    else:
                        dve.wait_ge(s_qkw[i % 2], 256)
                    dve.tensor_tensor(h2b[:, i % 2, :], tmp[:, 1, :], sbm[:, :], ALU.add).then_inc(s["h2"], 1)

                for i in range(NT + 1):
                    if i < NT:
                        tile_sum(i)
                    if i:
                        tile_norm(i - 1)
                pieces = router_sums(link)

                for w in range(4):
                    c, fh = w // 2, w % 2
                    need(dve, "tg", w + 1)
                    if w:
                        need(dve, "hs", w)
                    link(dve.scalar_tensor_tensor(out=tmp[0:FH, 0, :], in0=wk[0:FH, w % 2, :], scalar=1.0,
                                                  in1=pA[0:FH, w % 2, :], op0=ALU.add, op1=ALU.mult))
                    link(dve.scalar_tensor_tensor(out=tmp[0:FH, 1, :], in0=tmp[0:FH, 0, :], scalar=0.5,
                                                  in1=pD[0:FH, w % 2, :], op0=ALU.mult, op1=ALU.mult))
                    hi = hs[0][:, fh, c * CH:(c + 1) * CH]
                    link(dve.tensor_copy(hi, tmp[0:FH, 1, :]))
                    dve.tensor_tensor(hs[1][:, fh, c * CH:(c + 1) * CH], tmp[0:FH, 1, :], hi.bitcast(F32),
                                      ALU.subtract).then_inc(s["hs"], 1)
                    pump((3, 3, 1, 0)[w])
                need(dve, "hs", 4)
                for i in range(NT):
                    need(dve, "dn", i + 1)
                    if i >= 2:
                        need(dve, "pre", i - 1)
                    dve.tensor_tensor(tmp[:, i % 2, :], pC[:, i % 2, :], gb[:, :], ALU.mult).then_inc(s["sg"], 1)
                    if i >= PRE_POOL:
                        need(dve, "sg", i + 1)
                        dve.wait_ge(s_pw[i % 4], 16)
                        dve.tensor_tensor(pre_s[i % 4][:, :], tmp[:, i % 2, :], x2_rows[:, i, :], ALU.add).then_inc(s["prv"], 1)
                    pump(1)
                for _ in pieces:
                    pass

                end_of_batch(dve, "dve")

            batches(dve, body)

            for _ in router_choice(link, s["val_last"]):
                pass
            dve.wait_ge(s["vt_last"], 1)
            for n in (2, 3):
                dve.wait_ge(s_pw[n], 32)
            link(dve.tensor_copy(keys[:, :], pD[:, 0, :]))
            for _ in extraction(link):
                pass
            dve.tensor_copy(run_a[:, CAP:2 * CAP], lb[0:E, :]).then_inc(s["lb_last"], 1)
            dve.wait_ge(s["fgb"], 16)
            link(dve.tensor_copy(gbp[0][:, :], gbr[:, :]))
            link(dve.tensor_tensor(gbq[0][:, :], gbr[:, :], gbp[0][:, :], ALU.subtract))
            link(dve.tensor_copy(gbp[1][:, :], gbq[0][:, :]))
            link(dve.tensor_tensor(gbq[1][:, :], gbq[0][:, :], gbp[1][:, :], ALU.subtract))
            link(dve.tensor_copy(gbp[2][:, :], gbq[1][:, :]))
            dve.wait_ge(s["mrg"], 16)
            merge(link)
            link(dve.scalar_tensor_tensor(out=fz[:, :], in0=first[:, :], scalar=0.0, in1=slots_f[0:E, :], op0=ALU.is_equal,
                                          op1=ALU.mult))
            link(dve.tensor_scalar(idf[:, :], first[:, :], -1.0, float(T), ALU.mult, ALU.add))
            dve.tensor_tensor(idf[:, :], idf[:, :], fz[:, :], ALU.add).then_inc(s["idt"], 1)
            dve.wait_ge(s["vt_last"], 2)
            dve.tensor_copy(idu[:, :], pA[0:CAP, 0, 0:E]).then_inc(s["idt"], 1)
            for b in range(B):
                link(dve.tensor_scalar(oge[:, :], idf[:, :], float(b * S), None, ALU.is_ge))
                link(dve.scalar_tensor_tensor(out=ohb[b][:, :], in0=idf[:, :], scalar=float(b * S + S), in1=oge[:, :],
                                              op0=ALU.is_lt, op1=ALU.mult))
            dve.drain().then_inc(s["idx"], 1)
            dve.wait_ge(s["g12"], 16 * 15)

            def ohcopy(e, r, early):
                if not early:
                    dve.wait_ge(s["gbm"], e - 1)
                dve.tensor_copy(ohc[r % 2][:, :], oh[:, bass.ds(e * CAP, CAP)]).then_inc(s["oc"], 1)

            def gated(e, r, early):
                dve.wait_ge(s["the"], e + 1)
                if not early:
                    dve.wait_ge(s["hte"], e - 1)
                dve.scalar_tensor_tensor(out=hae[r % 2][:, :], in0=the[r % 2][:, :], scalar=1.0, in1=pA[0:CAP, r % 2, 0:F],
                                         op0=ALU.add, op1=ALU.mult).then_inc(s["ech"], 1)
                dve.wait_ge(s["ech"], e + 1)
                dve.scalar_tensor_tensor(out=hhe[r % 2][:, :], in0=hae[r % 2][:, :], scalar=0.5,
                                         in1=pA[0:CAP, r % 2, F:2 * F], op0=ALU.mult, op1=ALU.mult).then_inc(s["hhe"], 1)

            def weighted(e, r, early):
                dve.wait_ge(s["dne"], e + 1)
                dve.wait_ge(s["gbs"], e + 1)
                if not early:
                    dve.wait_ge(s["sc"], (e - 1) * 16)
                dve.scalar_tensor_tensor(out=ye[r % 2][:, :], in0=pC[0:CAP, r % 2, :], scalar=gath[r % 4][:, bass.ds(e + D, 1)],
                                         in1=gbs[r % 2][:, :], op0=ALU.mult, op1=ALU.mult).then_inc(s["ye"], 1)

            def rows_low(e, r):
                dve.wait_ge(s["gte"], e + 1)
                if r >= 2:
                    dve.wait_ge(s["gue"], e - 1)
                dve.tensor_tensor(gt[1][r % 2][:, :, :], pB[:, r % 2, 0:KT * CAP].rearrange("p (k q) -> p k q", k=KT),
                                  gt[0][r % 2][:, :, :].bitcast(F32), ALU.subtract).then_inc(s["gtl"], 1)

            def weights_low(e, r):
                dve.wait_ge(s["wgh"], e + 1)
                dve.tensor_tensor(wgs[1][r % 2][:, :, :], weg[r % 4][:, :, :], wgs[0][r % 2][:, :, :].bitcast(F32),
                                  ALU.subtract).then_inc(s["wgl"], 1)

            weights_low(0, 0)
            rows_low(0, 0)
            weights_low(1, 1)
            for e in range(3):
                ohcopy(e, e, e < 2)
                gated(e, e, e < 2)
                rows_low(e + 1, e + 1)
                weights_low(e + 2, e + 2)
                if e:
                    weighted(e - 1, e - 1, True)
            with dve.Fori(0, (E - NW) // NW - 1) as k:
                for r in range(NW):
                    e = k * NW + (r + 3)
                    ohcopy(e, r + 3, False)
                    gated(e, r + 3, False)
                    rows_low(k * NW + (r + 4), r + 4)
                    weighted(k * NW + (r + 2), r + 2, False)
                    weights_low(k * NW + (r + 5), r + 5)
            for e in range(E - NW - 1, E):
                ohcopy(e, e, False)
                gated(e, e, False)
                if e + 1 < E:
                    rows_low(e + 1, e + 1)
                weighted(e - 1, e - 1, False)
                if e + 2 < E:
                    weights_low(e + 2, e + 2)
            weighted(E - 1, E - 1, False)

        @block.tensor
        def _(pe):
            pe.wait_ge(s["csil"], 2)
            for n in range(6):
                if n >= 4:
                    pe.wait_ge(s["modc"], n - 3)
                for k in range(KT):
                    last = pe.matmul(AB[n // 2 % 2][0:B, n % 2, :], cts[:, k, :], wm[:, k, n * D:(n + 1) * D], start=k == 0,
                                     stop=k == KT - 1)
                last.then_inc(s["modm"], 1)
            pe.wait_ge(s["cst_v"], 14)
            pe.wait_ge(s["modc"], 6)

            def split_mm(dst, lhs, rhs, n, between=()):
                terms = [(k, a, b) for k in range(n) for a, b in ((0, 0), (1, 0), (0, 1))]
                for t, (k, a, b) in enumerate(terms):
                    if t % 2 and t // 2 < len(between):
                        between[t // 2]()
                    last = pe.matmul(dst, lhs(a, k), rhs(b, k), start=t == 0, stop=t == len(terms) - 1)
                return last

            hT = (h_hi, h_lo)
            pe.wait_ge(s["xn_1st"], NT)
            pe.wait_ge(s["wq_1st"], 32)

            def turn_keys(ready, turned):
                pe.wait_ge(ready, 1)
                for q in range(4):
                    last = pe.transpose(pD[:, 0, q * P:q * P + P], valt[:, q, :, :].rearrange("p h e -> p (h e)"), ident[:, :])
                last.then_inc(turned, 1)

            def body(it):
                for n in range(2 * KT):
                    h, k = n // KT, n % KT
                    if h:
                        need(pe, "hh", k + 1)
                    for i in range(4):
                        last = pe.transpose(AB[k // 2][:, k % 2, i * P:i * P + P], x_rows[:, 4 * h + i, k * P:k * P + P],
                                            ident[:, :])
                    last.then_inc(s["xt"], 1)
                def qk_unit(u, between=()):
                    m, t, c = qk_part(u)
                    w = (wq, wk_)[t]
                    if u in (0, 2):
                        need(pe, "hl", (u // 2 + 1) * KT)
                    if u == 4:
                        pe.wait_ge(s["wqk"], 32)
                    if u in (QK_FIRST, QK_FIRST + 1):
                        need(pe, "vr", NT - 1 + u - QK_FIRST)
                    elif u >= 2:
                        need(pe, "hi", u - 1)
                    split_mm(pC[:, u % 2, :], lambda a, k: w[a][:, k, m * P:m * P + P],
                             lambda b, k: hT[b][:, k, c * CH:(c + 1) * CH], KT, between).then_inc(s["qk"], 1)

                def unit(g, u):
                    i, kc, j, w = UNITS[u]
                    n = g * DPG + u
                    if u == 0:
                        pe.wait_ge(s_stk[g % 3], 128 * (g // 3 + 1))
                    if n >= 3:
                        need(pe, "df", n - 2)
                    elif n == 0:
                        need(pe, "key", 1)
                    pe.matmul(unit_bank[n % 3][:, 0:w], q_stk[g % 3][0:STK, j, i * P:i * P + P],
                              k_stk[g % 3][0:STK, j, kc * CH:kc * CH + w], start=True, stop=True).then_inc(s["dq"], 1)

                def turn_max(g):
                    n = g * DPG + NU
                    need(pe, "negm", g + 1)
                    pe.transpose(unit_bank[n % 3][0:GH * NT, 0:P], negm[:, :], ident[:, :]).then_inc(s["dq"], 1)

                def score(g, st, j):
                    c, kt, q0 = STEPS[st]
                    if st == 0 and j == 0:
                        pe.wait_ge(s["m"], 16 * (g + 1))
                    v = GH * (g * NS + st) + j
                    if v >= 3:
                        need(pe, "ex", v - 2)
                    last = pe.matmul(score_bank[v % 3][:, q0:CH], k_stk[g % 3][0:STK, j, kt * P:kt * P + P],
                                     q_stk[g % 3][0:STK, j, c * CH + q0:(c + 1) * CH], start=True, stop=True,
                                     skip_group_check=True)
                    if kt * P >= c * CH:
                        last = pe.matmul(score_bank[v % 3][:, q0:q0 + P], ident_b[:, :], mask_t[:, :], start=False,
                                         stop=True, skip_group_check=True)
                    last.then_inc(s["st"], 1)

                def weigh(g, st, bank):
                    c, kt, q0 = STEPS[st]
                    need(pe, "ex", GH * (g * NS + st) + GH)
                    if bank == 0 and kt == 0 and g * NC + c >= 1:
                        need(pe, "od", g * NC + c)
                    first, final = kt == 0, kt == (c + 1) * CH // P - 1
                    for j in range(GH):
                        h = GH * g + j
                        lhs = v_rows[:, kt, h * DH:(h + 1) * DH] if bank == 0 else ones[:, :]
                        last = pe.matmul(pC[j * DH:(j + 1) * DH, bank, q0:CH], lhs, p_buf[:, st % 2, j, q0:CH],
                                         start=first, stop=final, skip_group_check=True)
                    if bank:
                        last.then_inc(s["pv"], 1)

                def units_beside(n):
                    return [lambda k=k: unit(0, k) for k in beside(n)]

                for u in range(QK_FIRST):
                    qk_unit(u)
                    if u == 5:
                        turn_keys(s["val"], s["vt"])
                pe.wait_ge(s["wv"], 32)
                for i in range(NT):
                    if i < 2:
                        need(pe, "hi", QK_FIRST - 1 + i)
                    else:
                        need(pe, "vr", i - 1)
                    split_mm(pC[:, i % 2, :], lambda a, k: hT[a][:, k, i * P:i * P + P], lambda b, k: wv[b][:, k, :],
                             KT, units_beside(i)).then_inc(s["vp"], 1)
                for u in range(QK_FIRST, 16):
                    qk_unit(u, units_beside(NT + u - QK_FIRST))
                turn_max(0)
                need(pe, "vr", NT)
                need(pe, "hi", 16)
                for g in range(NG):
                    done = [0]
                    for st in range(NS):
                        n = SHARE[st] if g + 1 < NG else 0

                        def more_units(part, n=n, st=st, g=g, done=done):
                            upto = sum(SHARE[:st]) + (n + EARLY if g + st == 0 else round(n * part)) if n else 0
                            while done[0] < upto:
                                unit(g + 1, done[0])
                                done[0] += 1

                        if g + st == 0:
                            more_units(1)
                        score(g, st, 0)
                        more_units(PARTS[0])
                        score(g, st, 1)
                        score(g, st, 2)
                        more_units(PARTS[1])
                        if st:
                            weigh(g, st - 1, 0)
                        score(g, st, 3)
                        more_units(PARTS[2])
                        if st == TURN and g + 1 < NG:
                            more_units(1)
                            turn_max(g + 1)
                        if st:
                            weigh(g, st - 1, 1)
                        more_units(1)
                    weigh(g, NS - 1, 0)
                    weigh(g, NS - 1, 1)

                pe.wait_ge(s["wo"], 64)
                need(pe, "ex", GH * NG * NS)

                def project(i):
                    need(pe, "at", NG * NC - (1 if i < NT // NC else 0))
                    if i >= 4:
                        need(pe, "of", i - 3)
                    split_mm(AD[i // 2 % 2][:, i % 2, :], lambda a, k: hT[a][:, k, i * P:i * P + P], lambda b, k: wo[b][:, k, :],
                             KT).then_inc(s["op"], 1)

                def turn(i):
                    need(pe, "h2", i + 1)
                    if i >= 2:
                        need(pe, "h2h", i - 1)
                    for k in range(KT):
                        last = pe.transpose(pB[:, i % 2, k * P:k * P + P], h2b[:, i % 2, k * P:k * P + P], ident[:, :])
                    last.then_inc(s["tr"], 1)

                def logits(i):
                    need(pe, "wk", i + 1)
                    if i >= 2:
                        need(pe, "th", i - 1)
                    for k in range(KT):
                        last = pe.matmul(pC[:, i % 2, 0:E], wk[:, i % 2, k * P:k * P + P], gw[:, k, :], start=k == 0,
                                         stop=k == KT - 1)
                    last.then_inc(s["lg"], 1)

                def gate_up(w, part):
                    c, fh = w // 2, w % 2
                    if part == 0:
                        need(pe, "h2l", NT if c else NT // 2)
                        need(pe, "of", 7 + w if w < 2 else NT)
                    if part == 0 and w >= 2:
                        need(pe, "hs", w - 1)
                    last = split_mm(AD[part][0:FH, w % 2, :],
                                    lambda a, k: wsg[a][:, k, part * F + fh * FH:part * F + fh * FH + FH],
                                    lambda b, k: hT[b][:, k, c * CH:(c + 1) * CH], KT)
                    if part:
                        last.then_inc(s["gu"], 1)

                for i in range(4):
                    project(i)
                for i in range(NT):
                    turn(i)
                    if i + 4 < NT:
                        project(i + 4)
                    elif i + 3 >= NT:
                        gate_up((i + 3 - NT) // 2, (i + 3 - NT) % 2)
                    logits(i)
                gate_up(1, 1)
                for w in range(2, 4):
                    gate_up(w, 0)
                    gate_up(w, 1)
                need(pe, "th", NT)
                pe.wait_ge(s["wsd"], 32)
                for i in range(NT):
                    need(pe, "hs", 2 if i < 4 else 4)
                    if i >= 2:
                        need(pe, "sg", i - 1)
                    split_mm(pC[:, i % 2, :], lambda a, k: hs[a][:, k, i * P:i * P + P], lambda b, k: wsd[b][:, k, :],
                             2).then_inc(s["dn"], 1)
                end_of_batch(pe, "pe")

            batches(pe, body)

            turn_keys(s["val_last"], s["vt_last"])
            pe.wait_ge(s["idt"], 1)
            pe.transpose(pA[0:CAP, 0, 0:E], idf[:, :], ident[0:E, 0:E]).then_inc(s["vt_last"], 1)
            pe.wait_ge(s["idt"], 2)

            def turn_x(e, r, uses):
                pe.wait_ge(s_ga[r % 4], uses)
                for k in range(KT):
                    last = pe.transpose(pB[:, r % 2, k * CAP:(k + 1) * CAP], gath[r % 4][:, k * P:k * P + P],
                                        ident[0:CAP, 0:CAP])
                last.then_inc(s["xte"], 1)

            def gate_up(e, r):
                pe.wait_ge(s["gtl"], e + 1)
                pe.wait_ge(s["wgl"], e + 1)
                split_mm(pA[0:CAP, r % 2, 0:2 * F], lambda a, k: gt[a][r % 2][:, k, :], lambda b, k: wgs[b][r % 2][:, k, :],
                         KT).then_inc(s["gue"], 1)

            def down(e, r, early, uses):
                pe.wait_ge(s["htc"], e + 1)
                pe.wait_ge(s_wd[r % 4], uses)
                if not early:
                    pe.wait_ge(s["ye"], e - 1)
                for k in range(2):
                    last = pe.matmul(pC[0:CAP, r % 2, :], hte[r % 2][:, k, :], wed[r % 4][:, k, :], start=k == 0, stop=k == 1)
                last.then_inc(s["dne"], 1)
                pe.wait_ge(s["oc"], e + 1)
                if not (early and r == 0):
                    pe.wait_ge(s["gbs"], e)
                pe.matmul(pD[0:CAP, 0, :], ohc[r % 2][:, :], gb12[:, :], start=True, stop=True).then_inc(s["gbm"], 1)

            def turn_h(e, r, first):
                pe.wait_ge(s["hhe"], e + 1)
                if not first:
                    pe.wait_ge(s["htc"], e)
                for k in range(2):
                    last = pe.transpose(pD[0:FH, 1, k * CAP:(k + 1) * CAP], hhe[r % 2][:, k * FH:(k + 1) * FH],
                                        ident[0:CAP, 0:CAP])
                last.then_inc(s["hte"], 1)

            pe.wait_ge(s["ez"], NW + 2)
            turn_x(0, 0, 16)
            for e in range(3):
                gate_up(e, e)
                turn_x(e + 1, e + 1, 16)
                if e:
                    down(e - 1, e - 1, True, 16)
                turn_h(e, e, e == 0)
            with pe.Fori(0, (E - NW) // NW) as k:
                for r in range(NW):
                    e = k * NW + (r + 3)
                    gate_up(e, r + 3)
                    turn_x(k * NW + (r + 4), r + 4, k * 16 + 16 * ((r + 4) // 4 + 1))
                    down(k * NW + (r + 2), r + 2, False, k * 16 + 16 * ((r + 2) // 4 + 1))
                    turn_h(e, r + 3, False)
            gate_up(E - 1, E - 1)
            down(E - 2, E - 2, False, 16 * (E // 4))
            turn_h(E - 1, E - 1, False)
            down(E - 1, E - 1, False, 16 * (E // 4))


def _tiles(a):
    import numpy as np
    k = a.shape[-2] // P
    a = a.reshape(*a.shape[:-2], k, P, a.shape[-1])
    return np.ascontiguousarray(np.moveaxis(a, -3, -2))


def kernel(**inputs):
    import numpy as np
    import concourse.bacc as bacc
    from concourse.bass_utils import run_bass_kernel_spmd as run

    g = {k: np.asarray(v) for k, v in inputs.items()}
    w = {k[7:]: v for k, v in g.items() if k.startswith("L0_ffn_")}
    gate_up = np.concatenate([w["w_gate"], w["w_up"]], axis=-1)
    shared = np.concatenate([w["ws_gate"], w["ws_up"]], axis=-1)
    arrays = {
        "x": np.ascontiguousarray(g["L0_attn_X"].reshape(T, D)),
        "wqkvo": np.stack([_tiles(g["L0_attn_" + n].T).reshape(P, KT * D) for n in ("Wq", "Wk", "Wv", "Wo")]),
        "bq": g["L0_attn_bq"].reshape(KT, P).T, "bk": g["L0_attn_bk"].reshape(KT, P).T, "bv": g["L0_attn_bv"], "bo": g["L0_attn_bo"],
        "gate_w": _tiles(w["gate_w"]),
        "bias": w["bias"],
        "w_gu": _tiles(gate_up),
        "w_dn": np.ascontiguousarray(np.moveaxis(w["w_down"].reshape(E, 2, FH, D), 1, 2)),
        "ws_gu": _tiles(shared).reshape(P, KT * 2 * F),
        "ws_dn": np.ascontiguousarray(np.moveaxis(w["ws_down"].reshape(2, FH, D), 0, 1)).reshape(FH, 2 * D),
        "c_t": _tiles(g["L0_c"].T),
        "wmod": _tiles(g["L0_wmod"]),
    }
    nc = bacc.Bacc("TRN2", target_bir_lowering=False, num_devices=1)
    args = []
    feed = {}
    for name, a in arrays.items():
        a = np.ascontiguousarray(a)
        feed["in_" + name] = a
        args.append(nc.dram_tensor("in_" + name, a.shape, mybir.dt.from_np(a.dtype), kind="ExternalInput").ap())
    out = nc.dram_tensor("out_0", (T + CAP, D), F32, kind="ExternalOutput").ap()
    build(nc, *args, out)
    r = run(nc, [feed], core_ids=[0])
    return r.results[0]["out_0"][:T].reshape(B, S, D)
```
